# Optimizing a Trainium2 kernel written in Bass

```python
import numpy as np
import jax
import jax.numpy as jnp

def _softmax(x, axis=-1):
    return jax.nn.softmax(x, axis=axis)

def _gelu(x):
    return jax.nn.gelu(x, approximate=True)

def _silu(x):
    return jax.nn.silu(x)

def _sigmoid(x):
    return jax.nn.sigmoid(x)

def _layernorm(x, axis=-1, eps=1e-05):
    m = jnp.mean(x, axis=axis, keepdims=True)
    v = jnp.var(x, axis=axis, keepdims=True)
    return (x - m) / jnp.sqrt(v + eps)

def _scatter_add(tgt, idx, src, axis=0):
    return tgt.at[idx].add(src)

def _segment_sum(src, seg, n):
    return jax.ops.segment_sum(src, seg, n)
kernel_name = 'mk_decoder_preln_d1_seqx_r8_062bf8'

def setup_inputs(seed: int=0):
    np.random.seed(seed)
    _w = jnp.asarray

    def _rec_inputs():
        import jax
        import jax.numpy as jnp
        _rk = jax.random.key(seed)
        x = 2.818e-05 + 1 * jax.random.normal(jax.random.fold_in(_rk, 1), (32, 128, 128), jnp.float32)
        _lenS = 128 - jax.random.randint(jax.random.fold_in(_rk, 7), (32,), 0, max(1, 128 // 4) + 1, jnp.int32)
        _lenS2 = 128 - jax.random.randint(jax.random.fold_in(_rk, 8), (32,), 0, max(1, 128 // 4) + 1, jnp.int32)
        _ctx_2048P = jax.random.normal(jax.random.fold_in(_rk, 11), (32, 16, 256), jnp.float32)
        _ctx_2048c = jax.random.dirichlet(jax.random.fold_in(_rk, 511), 0.3 * jnp.ones((16,), jnp.float32), (32, 128))
        _ctx_2048t = jnp.einsum('bsk,bkd->bsd', _ctx_2048c, _ctx_2048P)
        _ctx_2048t = _ctx_2048t * jax.lax.rsqrt(jnp.mean(jnp.square(_ctx_2048t)) + 1e-12) * 0.953939
        ctx_2048 = -0.000125008 + 0.999885 * (_ctx_2048t + 0.3 * jax.random.normal(jax.random.fold_in(_rk, 611), (32, 128, 256), jnp.float32))
        _validS = jnp.arange(128)[None, :] < _lenS[:, None]
        _validS2 = jnp.arange(128)[None, :] < _lenS2[:, None]
        _causal = jnp.tril(jnp.ones((128, 128), dtype=bool))
        mask_BxS2_fk1 = jnp.where(jnp.broadcast_to(_validS2[:, :], (32, 128)), 1.0, 0.0).astype(jnp.float32)
        return (x, ctx_2048, mask_BxS2_fk1)
    x, ctx_2048, mask_BxS2_fk1 = _rec_inputs()

    def _L0_attn_setup():
        import math
        import jax, jax.numpy as jnp
        import numpy as np
        from jax.scipy.special import xlogy, gammaln

        def get_positional_embed(seq_len, feature_size):
            distances = jnp.arange(-seq_len + 1, seq_len, dtype=jnp.float32)
            n = feature_size // 6
            absd = jnp.abs(distances)[:, None]
            max_range = math.log(seq_len) / math.log(2.0)
            half_life = 2.0 ** jnp.linspace(3.0, max_range, n)
            feat_exp = jnp.exp(-math.log(2.0) / half_life[None, :] * absd)
            center_widths = 2.0 ** jnp.arange(1, n + 1, dtype=jnp.float32) - 1.0
            feat_cm = (center_widths[None, :] > absd).astype(jnp.float32)
            stddev = seq_len / (2.0 * n)
            start_mean = seq_len / n
            mean = jnp.linspace(start_mean, float(seq_len), n)[None, :]
            conc = (mean / stddev) ** 2
            rate = mean / stddev ** 2
            log_unnorm = xlogy(conc - 1.0, absd) - rate * absd
            log_norm = gammaln(conc) - conc * jnp.log(rate)
            probs = jnp.exp(log_unnorm - log_norm) + 1e-08
            feat_gamma = probs / jnp.max(probs, axis=-1, keepdims=True)
            emb = jnp.concatenate([feat_exp, feat_cm, feat_gamma], axis=-1)
            emb = jnp.concatenate([emb, jnp.sign(distances)[:, None] * emb], axis=-1)
            return emb

        def relative_shift(x):
            b, h, t1, t2m1 = x.shape
            x = jnp.pad(x, ((0, 0), (0, 0), (0, 0), (1, 0)))
            t2 = t2m1 + 1
            x = x.reshape(b, h, t2, t1)
            x = x[:, :, 1:, :]
            x = x.reshape(b, h, t1, t2 - 1)
            return x[..., :(t2 + 1) // 2]
        key = jax.random.key(seed)
        ks = jax.random.split(key, 9)
        B, L, D = (2, 128, 128)
        H, Dk, Dv = (8, 128, 128)
        R = 192
        sq = math.sqrt(2.0 / (D + Dk))
        sv = math.sqrt(2.0 / (D + Dv))
        return {'q': jax.random.normal(ks[0], (B, L, D), jnp.float32), 'w_qs': jax.random.normal(ks[1], (D, H * Dk), jnp.float32) * sq, 'w_ks': jax.random.normal(ks[2], (D, H * Dk), jnp.float32) * sq, 'w_vs': jax.random.normal(ks[3], (D, H * Dv), jnp.float32) * sv, 'w_rel_pos_k': jax.random.normal(ks[4], (R, H * Dk), jnp.float32) * 0.05, 'rel_embed_bias': jax.random.normal(ks[5], (1, H, 1, Dk), jnp.float32), 'rel_pos_bias': jax.random.normal(ks[6], (1, H, 1, Dk), jnp.float32), 'w_out': jax.random.normal(ks[7], (H * Dv, D), jnp.float32) * 0.02, 'b_out': jax.random.normal(ks[8], (D,), jnp.float32) * 0.02}
    _L0_attn_all = _L0_attn_setup()
    _L0_attn_in = {k: v for k, v in _L0_attn_all.items() if k in ('w_qs', 'w_ks', 'w_vs', 'w_rel_pos_k', 'rel_embed_bias', 'rel_pos_bias', 'w_out', 'b_out')}
    del _L0_attn_all

    def _L0_xattn_setup():
        import jax, jax.numpy as jnp
        import numpy as np
        B, S, T = (32, 64, 64)
        SRC_SIZE, TGT_SIZE, OUT_SIZE, NUM_HEAD = (256, 128, 128, 8)
        HEAD_DIM = OUT_SIZE // NUM_HEAD
        key = jax.random.key(seed)
        ks = jax.random.split(key, 12)
        src = jax.random.normal(ks[0], (B, S, SRC_SIZE), dtype=jnp.float32)
        tgt = jax.random.normal(ks[1], (B, T, TGT_SIZE), dtype=jnp.float32)
        src_mask = (jax.random.uniform(ks[2], (B, S)) > 0.3).astype(jnp.float32)
        src_mask = src_mask.at[:, 0].set(1.0)
        tgt_mask = (jax.random.uniform(ks[3], (B, T)) > 0.3).astype(jnp.float32)
        tgt_mask = tgt_mask.at[:, 0].set(1.0)

        def lin(k, out_f, in_f):
            return jax.random.normal(k, (out_f, in_f), dtype=jnp.float32) / np.sqrt(in_f)
        W_src = lin(ks[4], 2 * OUT_SIZE, SRC_SIZE)
        b_src = jnp.zeros((2 * OUT_SIZE,), jnp.float32)
        W_tgt = lin(ks[5], OUT_SIZE, TGT_SIZE)
        b_tgt = jnp.zeros((OUT_SIZE,), jnp.float32)
        W_out = lin(ks[6], OUT_SIZE, OUT_SIZE + TGT_SIZE)
        b_out = jnp.zeros((OUT_SIZE,), jnp.float32)
        return {'src': src, 'tgt': tgt, 'src_mask': src_mask, 'tgt_mask': tgt_mask, 'W_src': W_src, 'b_src': b_src, 'W_tgt': W_tgt, 'b_tgt': b_tgt, 'W_out': W_out, 'b_out': b_out}
    _L0_xattn_all = _L0_xattn_setup()
    _L0_xattn_in = {k: v for k, v in _L0_xattn_all.items() if k in ('W_src', 'b_src', 'W_tgt', 'b_tgt', 'W_out', 'b_out')}
    del _L0_xattn_all

    def _L0_ffn_setup():
        import jax, jax.numpy as jnp
        import numpy as np
        DIM = 128
        DEPTH = 6
        HEADS = 16
        DIM_HEAD = 64
        WINDOW = 32
        INNER = HEADS * DIM_HEAD
        DIM_INNER = int(DIM * 4 * 2 / 3)
        QK_SCALE = 8.0

        def shift_tokens(t):
            a, s = jnp.split(t, 2, -1)
            s = jnp.pad(s, ((0, 0), (1, 0), (0, 0)))[:, :-1]
            return jnp.concatenate([a, s], -1)

        def l2norm(t):
            return t / jnp.maximum(jnp.linalg.norm(t, axis=-1, keepdims=True), 1e-12)

        def rotate_half(x):
            x1, x2 = jnp.split(x, 2, -1)
            return jnp.concatenate([-x2, x1], -1)

        def rotary_tables(n):
            half = jnp.arange(0, DIM_HEAD, 2, dtype=jnp.float32)
            inv_freq = 1.0 / 10000.0 ** (half / DIM_HEAD)
            t = jnp.arange(n, dtype=jnp.float32)
            freqs = t[:, None] * inv_freq[None, :]
            freqs = jnp.concatenate([freqs, freqs], -1)
            base_scale = (half + 0.4 * DIM_HEAD) / (1.4 * DIM_HEAD)
            power = (t - n // 2) / (WINDOW // 2)
            scale = base_scale[None, :] ** power[:, None]
            scale = jnp.concatenate([scale, scale], -1)
            return (freqs, scale)

        def local_attention(q, k, v):
            b, h, n, d = q.shape
            w = WINDOW
            nw = n // w
            bq = q.reshape(b, h, nw, w, d)
            bk = k.reshape(b, h, nw, w, d)
            bv = v.reshape(b, h, nw, w, d)

            def look(t):
                p = jnp.pad(t, ((0, 0), (0, 0), (1, 0), (0, 0), (0, 0)))
                return jnp.concatenate([p[:, :, :nw], p[:, :, 1:]], axis=3)
            bk2, bv2 = (look(bk), look(bv))
            seq = jnp.arange(n).reshape(nw, w)
            seq_p = jnp.pad(seq, ((1, 0), (0, 0)), constant_values=-1)
            jt = jnp.concatenate([seq_p[:nw], seq_p[1:]], axis=1)
            it = seq[:, :, None]
            jb = jt[:, None, :]
            mask = (it < jb) | (it > jb + w) | (jb == -1)
            sim = jnp.einsum('bhwie,bhwje->bhwij', bq, bk2) * QK_SCALE
            sim = jnp.where(mask, -jnp.finfo(sim.dtype).max, sim)
            attn = jax.nn.softmax(sim, -1)
            out = jnp.einsum('bhwij,bhwje->bhwie', attn, bv2)
            return out.reshape(b, h, n, d)

        def attn_layer(x, Wqkv, qs, ksc, Wo):
            b, n, _ = x.shape
            qkv = x @ Wqkv
            q, k, v = jnp.split(qkv, 3, -1)
            sh = lambda t: t.reshape(b, n, HEADS, DIM_HEAD).transpose(0, 2, 1, 3)
            q, k, v = (sh(q), sh(k), sh(v))
            q = l2norm(q) * qs
            k = l2norm(k) * ksc
            freqs, scale = rotary_tables(n)
            cos, sin = (jnp.cos(freqs), jnp.sin(freqs))
            q = q * cos * scale + rotate_half(q) * sin * scale
            inv = 1.0 / scale
            k = k * cos * inv + rotate_half(k) * sin * inv
            out = local_attention(q, k, v)
            out = out.transpose(0, 2, 1, 3).reshape(b, n, INNER)
            return out @ Wo

        def ffn_layer(x, g, bln, W1, b1, W2, b2):
            mu = x.mean(-1, keepdims=True)
            var = ((x - mu) ** 2).mean(-1, keepdims=True)
            xn = (x - mu) / jnp.sqrt(var + 1e-05) * g + bln
            hg = xn @ W1 + b1
            a, gate = jnp.split(hg, 2, -1)
            return a * jax.nn.gelu(gate, approximate=False) @ W2 + b2
        key = jax.random.key(seed)
        ks = jax.random.split(key, 8)
        B, N = (2, 256)
        init = lambda k, shape: jax.random.normal(k, shape, jnp.float32) * 0.02
        return {'x': jax.random.normal(ks[0], (B, N, DIM), jnp.float32), 'Wqkv': init(ks[1], (DEPTH, DIM, 3 * INNER)), 'q_scale': jnp.ones((DEPTH, DIM_HEAD), jnp.float32), 'k_scale': jnp.ones((DEPTH, DIM_HEAD), jnp.float32), 'Wo': init(ks[2], (DEPTH, INNER, DIM)), 'ln_g': jnp.ones((DEPTH, DIM), jnp.float32), 'ln_b': jnp.zeros((DEPTH, DIM), jnp.float32), 'W1': init(ks[3], (DEPTH, DIM, 2 * DIM_INNER)), 'b1': jnp.zeros((DEPTH, 2 * DIM_INNER), jnp.float32), 'W2': init(ks[4], (DEPTH, DIM_INNER, DIM)), 'b2': jnp.zeros((DEPTH, DIM), jnp.float32)}
    _L0_ffn_all = _L0_ffn_setup()
    _L0_ffn_in = {k: v for k, v in _L0_ffn_all.items() if k in ('Wqkv', 'q_scale', 'k_scale', 'Wo', 'ln_g', 'ln_b', 'W1', 'b1', 'W2', 'b2')}
    del _L0_ffn_all
    return {'x': x, 'ctx_2048': ctx_2048, 'mask_BxS2_fk1': mask_BxS2_fk1, 'L0_attn_w_qs': _L0_attn_in['w_qs'], 'L0_attn_w_ks': _L0_attn_in['w_ks'], 'L0_attn_w_vs': _L0_attn_in['w_vs'], 'L0_attn_w_rel_pos_k': _L0_attn_in['w_rel_pos_k'], 'L0_attn_rel_embed_bias': _L0_attn_in['rel_embed_bias'], 'L0_attn_rel_pos_bias': _L0_attn_in['rel_pos_bias'], 'L0_attn_w_out': _L0_attn_in['w_out'], 'L0_attn_b_out': _L0_attn_in['b_out'], 'L0_xattn_W_src': _L0_xattn_in['W_src'], 'L0_xattn_b_src': _L0_xattn_in['b_src'], 'L0_xattn_W_tgt': _L0_xattn_in['W_tgt'], 'L0_xattn_b_tgt': _L0_xattn_in['b_tgt'], 'L0_xattn_W_out': _L0_xattn_in['W_out'], 'L0_xattn_b_out': _L0_xattn_in['b_out'], 'L0_ffn_Wqkv': _L0_ffn_in['Wqkv'], 'L0_ffn_q_scale': _L0_ffn_in['q_scale'], 'L0_ffn_k_scale': _L0_ffn_in['k_scale'], 'L0_ffn_Wo': _L0_ffn_in['Wo'], 'L0_ffn_ln_g': _L0_ffn_in['ln_g'], 'L0_ffn_ln_b': _L0_ffn_in['ln_b'], 'L0_ffn_W1': _L0_ffn_in['W1'], 'L0_ffn_b1': _L0_ffn_in['b1'], 'L0_ffn_W2': _L0_ffn_in['W2'], 'L0_ffn_b2': _L0_ffn_in['b2']}

def reference(x, ctx_2048, mask_BxS2_fk1, L0_attn_w_qs, L0_attn_w_ks, L0_attn_w_vs, L0_attn_w_rel_pos_k, L0_attn_rel_embed_bias, L0_attn_rel_pos_bias, L0_attn_w_out, L0_attn_b_out, L0_xattn_W_src, L0_xattn_b_src, L0_xattn_W_tgt, L0_xattn_b_tgt, L0_xattn_W_out, L0_xattn_b_out, L0_ffn_Wqkv, L0_ffn_q_scale, L0_ffn_k_scale, L0_ffn_Wo, L0_ffn_ln_g, L0_ffn_ln_b, L0_ffn_W1, L0_ffn_b1, L0_ffn_W2, L0_ffn_b2):
    import jax
    import jax.numpy as jnp

    def _L0_attn_ref(q, w_qs, w_ks, w_vs, w_rel_pos_k, rel_embed_bias, rel_pos_bias, w_out, b_out):
        import math
        import jax, jax.numpy as jnp
        import numpy as np
        from jax.scipy.special import xlogy, gammaln

        def get_positional_embed(seq_len, feature_size):
            distances = jnp.arange(-seq_len + 1, seq_len, dtype=jnp.float32)
            n = feature_size // 6
            absd = jnp.abs(distances)[:, None]
            max_range = math.log(seq_len) / math.log(2.0)
            half_life = 2.0 ** jnp.linspace(3.0, max_range, n)
            feat_exp = jnp.exp(-math.log(2.0) / half_life[None, :] * absd)
            center_widths = 2.0 ** jnp.arange(1, n + 1, dtype=jnp.float32) - 1.0
            feat_cm = (center_widths[None, :] > absd).astype(jnp.float32)
            stddev = seq_len / (2.0 * n)
            start_mean = seq_len / n
            mean = jnp.linspace(start_mean, float(seq_len), n)[None, :]
            conc = (mean / stddev) ** 2
            rate = mean / stddev ** 2
            log_unnorm = xlogy(conc - 1.0, absd) - rate * absd
            log_norm = gammaln(conc) - conc * jnp.log(rate)
            probs = jnp.exp(log_unnorm - log_norm) + 1e-08
            feat_gamma = probs / jnp.max(probs, axis=-1, keepdims=True)
            emb = jnp.concatenate([feat_exp, feat_cm, feat_gamma], axis=-1)
            emb = jnp.concatenate([emb, jnp.sign(distances)[:, None] * emb], axis=-1)
            return emb

        def relative_shift(x):
            b, h, t1, t2m1 = x.shape
            x = jnp.pad(x, ((0, 0), (0, 0), (0, 0), (1, 0)))
            t2 = t2m1 + 1
            x = x.reshape(b, h, t2, t1)
            x = x[:, :, 1:, :]
            x = x.reshape(b, h, t1, t2 - 1)
            return x[..., :(t2 + 1) // 2]
        B, L, _ = q.shape
        H, Dk = (rel_embed_bias.shape[1], rel_embed_bias.shape[3])
        Dv = w_vs.shape[1] // H
        scale = Dk ** (-0.5)
        Q = (q @ w_qs).reshape(B, L, H, Dk).transpose(0, 2, 1, 3) * scale
        K = (q @ w_ks).reshape(B, L, H, Dk).transpose(0, 2, 1, 3)
        V = (q @ w_vs).reshape(B, L, H, Dv).transpose(0, 2, 1, 3)
        attn = jnp.einsum('bnqd,bnkd->bnqk', Q + rel_embed_bias, K)
        positions = get_positional_embed(L, w_rel_pos_k.shape[0])
        rel_k = (positions @ w_rel_pos_k).reshape(-1, H, Dk).transpose(1, 0, 2)
        attn_pos = jnp.einsum('bnqd,nkd->bnqk', Q + rel_pos_bias, rel_k)
        attn_pos = relative_shift(attn_pos)
        a = jax.nn.softmax(attn + attn_pos, axis=-1)
        out = jnp.einsum('bnqk,bnkd->bnqd', a, V)
        out = out.transpose(0, 2, 1, 3).reshape(B, L, H * Dv)
        return out @ w_out + b_out

    def _L0_xattn_ref(src, tgt, src_mask, tgt_mask, W_src, b_src, W_tgt, b_tgt, W_out, b_out):
        import jax, jax.numpy as jnp
        import numpy as np
        B, S, T = (32, 64, 64)
        SRC_SIZE, TGT_SIZE, OUT_SIZE, NUM_HEAD = (256, 128, 128, 8)
        HEAD_DIM = OUT_SIZE // NUM_HEAD
        b, s, _ = src.shape
        t = tgt.shape[1]
        src_trans = jnp.einsum('bsf,of->bso', src, W_src) + b_src
        tgt_trans = jnp.einsum('btf,of->bto', tgt, W_tgt) + b_tgt
        src_trans = src_trans * src_mask[:, :, None]
        tgt_trans = tgt_trans * tgt_mask[:, :, None]
        src_key, src_val = jnp.split(src_trans, 2, axis=2)
        k = src_key.reshape(b, s, NUM_HEAD, HEAD_DIM)
        v = src_val.reshape(b, s, NUM_HEAD, HEAD_DIM)
        q = tgt_trans.reshape(b, t, NUM_HEAD, HEAD_DIM)
        scores = jnp.einsum('bthd,bshd->bhts', q, k) / np.sqrt(HEAD_DIM)
        scores = jnp.where(src_mask[:, None, None, :] == 0, -jnp.inf, scores)
        attn = jax.nn.softmax(scores, axis=-1)
        tgt_update = jnp.einsum('bhts,bshd->bthd', attn, v).reshape(b, t, OUT_SIZE)
        cat_tgt = jnp.concatenate([tgt, tgt_update], axis=2)
        return jnp.einsum('btf,of->bto', cat_tgt, W_out) + b_out

    def _L0_ffn_ref(x, Wqkv, q_scale, k_scale, Wo, ln_g, ln_b, W1, b1, W2, b2):
        import jax, jax.numpy as jnp
        import numpy as np
        DIM = 128
        DEPTH = 6
        HEADS = 16
        DIM_HEAD = 64
        WINDOW = 32
        INNER = HEADS * DIM_HEAD
        DIM_INNER = int(DIM * 4 * 2 / 3)
        QK_SCALE = 8.0

        def shift_tokens(t):
            a, s = jnp.split(t, 2, -1)
            s = jnp.pad(s, ((0, 0), (1, 0), (0, 0)))[:, :-1]
            return jnp.concatenate([a, s], -1)

        def l2norm(t):
            return t / jnp.maximum(jnp.linalg.norm(t, axis=-1, keepdims=True), 1e-12)

        def rotate_half(x):
            x1, x2 = jnp.split(x, 2, -1)
            return jnp.concatenate([-x2, x1], -1)

        def rotary_tables(n):
            half = jnp.arange(0, DIM_HEAD, 2, dtype=jnp.float32)
            inv_freq = 1.0 / 10000.0 ** (half / DIM_HEAD)
            t = jnp.arange(n, dtype=jnp.float32)
            freqs = t[:, None] * inv_freq[None, :]
            freqs = jnp.concatenate([freqs, freqs], -1)
            base_scale = (half + 0.4 * DIM_HEAD) / (1.4 * DIM_HEAD)
            power = (t - n // 2) / (WINDOW // 2)
            scale = base_scale[None, :] ** power[:, None]
            scale = jnp.concatenate([scale, scale], -1)
            return (freqs, scale)

        def local_attention(q, k, v):
            b, h, n, d = q.shape
            w = WINDOW
            nw = n // w
            bq = q.reshape(b, h, nw, w, d)
            bk = k.reshape(b, h, nw, w, d)
            bv = v.reshape(b, h, nw, w, d)

            def look(t):
                p = jnp.pad(t, ((0, 0), (0, 0), (1, 0), (0, 0), (0, 0)))
                return jnp.concatenate([p[:, :, :nw], p[:, :, 1:]], axis=3)
            bk2, bv2 = (look(bk), look(bv))
            seq = jnp.arange(n).reshape(nw, w)
            seq_p = jnp.pad(seq, ((1, 0), (0, 0)), constant_values=-1)
            jt = jnp.concatenate([seq_p[:nw], seq_p[1:]], axis=1)
            it = seq[:, :, None]
            jb = jt[:, None, :]
            mask = (it < jb) | (it > jb + w) | (jb == -1)
            sim = jnp.einsum('bhwie,bhwje->bhwij', bq, bk2) * QK_SCALE
            sim = jnp.where(mask, -jnp.finfo(sim.dtype).max, sim)
            attn = jax.nn.softmax(sim, -1)
            out = jnp.einsum('bhwij,bhwje->bhwie', attn, bv2)
            return out.reshape(b, h, n, d)

        def attn_layer(x, Wqkv, qs, ksc, Wo):
            b, n, _ = x.shape
            qkv = x @ Wqkv
            q, k, v = jnp.split(qkv, 3, -1)
            sh = lambda t: t.reshape(b, n, HEADS, DIM_HEAD).transpose(0, 2, 1, 3)
            q, k, v = (sh(q), sh(k), sh(v))
            q = l2norm(q) * qs
            k = l2norm(k) * ksc
            freqs, scale = rotary_tables(n)
            cos, sin = (jnp.cos(freqs), jnp.sin(freqs))
            q = q * cos * scale + rotate_half(q) * sin * scale
            inv = 1.0 / scale
            k = k * cos * inv + rotate_half(k) * sin * inv
            out = local_attention(q, k, v)
            out = out.transpose(0, 2, 1, 3).reshape(b, n, INNER)
            return out @ Wo

        def ffn_layer(x, g, bln, W1, b1, W2, b2):
            mu = x.mean(-1, keepdims=True)
            var = ((x - mu) ** 2).mean(-1, keepdims=True)
            xn = (x - mu) / jnp.sqrt(var + 1e-05) * g + bln
            hg = xn @ W1 + b1
            a, gate = jnp.split(hg, 2, -1)
            return a * jax.nn.gelu(gate, approximate=False) @ W2 + b2
        for i in range(DEPTH):
            x = attn_layer(shift_tokens(x), Wqkv[i], q_scale[i], k_scale[i], Wo[i]) + x
            x = ffn_layer(shift_tokens(x), ln_g[i], ln_b[i], W1[i], b1[i], W2[i], b2[i]) + x
        return x
    x = x + _L0_attn_ref(_layernorm(x, axis=-1), L0_attn_w_qs, L0_attn_w_ks, L0_attn_w_vs, L0_attn_w_rel_pos_k, L0_attn_rel_embed_bias, L0_attn_rel_pos_bias, L0_attn_w_out, L0_attn_b_out)
    x = x + _L0_xattn_ref(ctx_2048, _layernorm(x, axis=-1), mask_BxS2_fk1, mask_BxS2_fk1, L0_xattn_W_src, L0_xattn_b_src, L0_xattn_W_tgt, L0_xattn_b_tgt, L0_xattn_W_out, L0_xattn_b_out)
    x = x + _L0_ffn_ref(_layernorm(x, axis=-1), L0_ffn_Wqkv, L0_ffn_q_scale, L0_ffn_k_scale, L0_ffn_Wo, L0_ffn_ln_g, L0_ffn_ln_b, L0_ffn_W1, L0_ffn_b1, L0_ffn_W2, L0_ffn_b2)
    return x

_drawn_inputs = setup_inputs


def setup_inputs(seed=0):
    import zlib

    import numpy as np

    out = dict(_drawn_inputs(seed))
    spreads = {'L0_xattn_b_src': (0.0, 0.1),
     'L0_xattn_b_tgt': (0.0, 0.735),
     'L0_xattn_b_out': (0.0, 0.1),
     'L0_ffn_q_scale': (1.0, 0.6),
     'L0_ffn_k_scale': (1.0, 0.6),
     'L0_ffn_ln_g': (1.0, 0.6),
     'L0_ffn_ln_b': (0.0, 0.8),
     'L0_ffn_b1': (0.0, 0.8),
     'L0_ffn_b2': (0.0, 0.1)}
    factors = {'L0_attn_b_out': 3.304, 'L0_ffn_W1': 4.338, 'L0_ffn_W2': 4.253}
    for name, (base, spread) in spreads.items():
        noise = np.random.default_rng([zlib.crc32(name.encode()), seed]).standard_normal(out[name].shape)
        drawn = base * np.exp(spread * noise) if base else spread * noise
        out[name] = jnp.asarray(drawn.astype(out[name].dtype))
    for name, factor in factors.items():
        out[name] = (out[name] * factor).astype(out[name].dtype)
    return out
```

```python
import math

import numpy as np

import concourse.bass as bass
import concourse.mybir as mybir
from concourse.alu_op_type import AluOpType as ALU
from contextlib import ExitStack

F32 = mybir.dt.float32
BF16 = mybir.dt.bfloat16
ACT = mybir.ActivationFunctionType
X_AXIS = mybir.AxisListType.X

B, T, D = 32, 128, 128
H0, DK = 8, 128
NF = 192
NR = 2 * T - 1
CTX = 256
HX, DX = 8, 16
LAYERS, HL, DL = 6, 16, 64
WINDOW = 32
INNER = HL * DL
FF = int(D * 4 * 2 / 3)
G = 4
UNITS = B * HL // G
QUAD = 4
QUADS = B // QUAD
NQ = QUAD * T
FF_CHUNKS = [(0, 128), (128, 128), (256, FF - 256)]
OUT_CHUNKS = INNER // 128
EPS = 1e-5
MASKED = -1e30
SCORE_SCALE0 = DK ** -0.5
SCORE_SCALEX = DX ** -0.5
QK_SCALE = 8.0


def positional_features():
    f = np.float32
    dist = np.arange(-T + 1, T, dtype=f)
    n = NF // 6
    absd = np.abs(dist)[:, None]
    half_life = f(2.0) ** np.linspace(3.0, math.log(T) / math.log(2.0), n, dtype=f)
    feat_exp = np.exp(f(-math.log(2.0)) / half_life[None, :] * absd)
    widths = f(2.0) ** np.arange(1, n + 1, dtype=f) - f(1.0)
    feat_cm = (widths[None, :] > absd).astype(f)
    stddev = T / (2.0 * n)
    mean = np.linspace(T / n, float(T), n, dtype=f)[None, :]
    conc = (mean / f(stddev)) ** 2
    rate = mean / f(stddev ** 2)
    logs = np.log(np.where(absd > 0, absd, f(1.0))).astype(f)
    log_unnorm = np.where(absd > 0, (conc - f(1.0)) * logs, f(-np.inf)) - rate * absd
    lgam = np.array([[math.lgamma(float(c)) for c in conc[0]]], dtype=f)
    log_norm = lgam - conc * np.log(rate)
    probs = np.exp((log_unnorm - log_norm).astype(f)) + f(1e-8)
    feat_gamma = probs / probs.max(axis=-1, keepdims=True)
    emb = np.concatenate([feat_exp, feat_cm, feat_gamma], axis=-1)
    emb = np.concatenate([emb, np.sign(dist)[:, None] * emb], axis=-1)
    return np.ascontiguousarray(emb.T.astype(f))


def rotary_tables():
    f = np.float32
    half = np.arange(0, DL, 2, dtype=f)
    inv_freq = f(1.0) / f(10000.0) ** (half / f(DL))
    t = np.arange(T, dtype=f)
    freqs = t[:, None] * inv_freq[None, :]
    freqs = np.concatenate([freqs, freqs], -1)
    base = (half + f(0.4 * DL)) / f(1.4 * DL)
    power = (t - f(T // 2)) / f(WINDOW // 2)
    scale = base[None, :] ** power[:, None]
    scale = np.concatenate([scale, scale], -1)
    cos, sin = np.cos(freqs), np.sin(freqs)
    sign = np.concatenate([np.ones(DL // 2, f), -np.ones(DL // 2, f)])[None, :]
    q = f(QK_SCALE) * scale
    k = f(1.0) / scale
    return np.ascontiguousarray(np.stack([cos * q, cos * k, sin * q * sign, sin * k * sign], 1).astype(f))


def band_mask():
    i, j = np.arange(T)[:, None], np.arange(T)[None, :]
    return np.where((j <= i) & (j >= i - WINDOW), 0.0, MASKED).astype(np.float32)


def head_rows():
    return (np.arange(D)[:, None] // DX == np.arange(HX)[None, :]).astype(np.float32)


CONSTANTS = {
    "pos_feats": positional_features, "rotary": rotary_tables, "band": band_mask, "head_rows": head_rows,
    "eye": lambda: np.eye(128, dtype=np.float32),
}


def pipeline(eng, units, period, max_skew, emit, peeled=1):
    for i in range(peeled):
        for k in range(period):
            emit(k, i, lambda d, i=i, k=k: i * period + k - d >= 0)
    with eng.Fori(peeled, units // period) as i:
        for k in range(period):
            emit(k, i, lambda d: True)
    for k in range(max_skew):
        emit(k, units // period, lambda d, k=k: k - d < 0)


def reused(first, k, d, depth):
    return not (isinstance(first, int) and first + k - d < depth)


def build(nc, x, ctx_in, mask, w_qs, w_ks, w_vs, w_rel, emb_bias, pos_bias, w_out0, b_out0,
          W_src, b_src, W_tgt, b_tgt, W_outx, b_outx,
          Wqkv, q_scale, k_scale, Wo, ln_g, ln_b, W1, b1, W2, b2,
          pos_feats, rotary, band, head_rows_in, eye, out):
    ctx = ExitStack()
    with ctx:
        def sb(name, shape, dt=F32):
            return ctx.enter_context(nc.sbuf_tensor(name, shape, dt))

        def pb(name):
            return ctx.enter_context(nc.psum_tensor(name, [128, 512], F32))

        def sem(name):
            return ctx.enter_context(nc.semaphore(name))

        ident = sb("ident", [128, 128])
        ident_bf = sb("ident_bf", [128, 128], BF16)
        band_f = sb("band_f", [128, T])
        band_bf = sb("band_bf", [128, 2, T], BF16)
        mean_w = sb("mean_w", [128, 128])
        neg_half = sb("neg_half", [128, 2 * G])
        x_all = sb("x_all", [128, B, D])
        zT = sb("zT", [128, B, T])

        banks = [pb(f"bank{i}") for i in range(6)]
        bank_pair = ctx.enter_context(nc.psum_tensor("bank_pair", [128, 2, 512], F32))
        banks += [bank_pair[:, 0, :], bank_pair[:, 1, :]]
        pos_scratch = nc.dram_tensor("pos_scratch", [2, T * H0 * NR + NR], F32, kind="Internal").ap()

        loaded_w0 = sem("loaded_w0")
        loaded_x = sem("loaded_x")
        const_set = sem("const_set")
        half_set = sem("half_set")
        const_cast = sem("const_cast")
        setup_pe = sem("setup_pe")
        setup_ev = sem("setup_ev")
        setup_cp = sem("setup_cp")

        passed = {id(e): sem(f"passed_{n}") for n, e in (("dve", nc.vector), ("pool", nc.gpsimd), ("sp", nc.sync))}

        def wait_apart(eng, semaphore, value):
            eng.wait_ge(semaphore, value)
            eng.sem_inc(passed[id(eng)], 1)

        part1 = ExitStack()

        def sb1(name, shape, dt=F32):
            return part1.enter_context(nc.sbuf_tensor(name, shape, dt))

        A_w = sb1("A_w", [128, H0, 128])
        C_w = sb1("C_w", [128, H0, NR])
        M_w = sb1("M_w", [128, H0, 128])
        u_b = sb1("u_b", [128, H0])
        pos_c = sb1("pos_c", [128, H0, NR])
        srcT = sb1("srcT", [128, 2, 2 * D])
        tgtT = sb1("tgtT", [128, D])
        outxT = sb1("outxT", [128, 2, D])
        btgt = sb1("btgt", [128, 1])
        bk = sb1("bk", [128, 1])
        bv_row = sb1("bv_row", [128, D])
        bo0_row = sb1("bo0_row", [128, D])
        box_row = sb1("box_row", [128, D])
        heads = sb1("heads", [128, HX])
        mrow = sb1("mrow", [128, B, T])
        mcol = sb1("mcol", [128, B])

        setup = ExitStack()

        def sbs(name, shape, dt=F32):
            return setup.enter_context(nc.sbuf_tensor(name, shape, dt))

        wq_raw = sbs("wq_raw", [128, H0 * DK])
        wk_raw = sbs("wk_raw", [128, H0 * DK])
        wv_raw = sbs("wv_raw", [128, H0 * DK])
        wo_raw = sbs("wo_raw", [128, H0, D])
        rel_a = sbs("rel_a", [128, H0 * DK])
        rel_b = sbs("rel_b", [NF - 128, H0 * DK])
        feat_a = sbs("feat_a", [128, NR])
        feat_b = sbs("feat_b", [NF - 128, NR])
        eb = sbs("eb", [128, H0])
        pbias = sbs("pbias", [128, H0])
        src_raw = sbs("src_raw", [128, 2, CTX])
        tgt_raw = sbs("tgt_raw", [128, D])
        outx_raw = sbs("outx_raw", [128, 2 * D])
        mask_raw = sbs("mask_raw", [B, T])
        wT = sbs("wT", [128, 3, 128])
        relT = sbs("relT", [128, NR])
        pb_rep = sbs("pb_rep", [128, 128])

        W0_LOADS = [
            (wq_raw[:, :], w_qs), (wk_raw[:, :], w_ks), (wv_raw[:, :], w_vs),
            (wo_raw[:, :, :], w_out0.rearrange("(h e) d -> e h d", h=H0)),
            (rel_a[:, :], w_rel[0:128, :]), (rel_b[:, :], w_rel[128:NF, :]),
            (feat_a[:, :], pos_feats[0:128, :]), (feat_b[:, :], pos_feats[128:NF, :]),
            (eb[:, :], emb_bias.rearrange("a h b d -> d (a h b)")),
            (pbias[:, :], pos_bias.rearrange("a h b d -> d (a h b)")),
            (src_raw[:, :, :], W_src.rearrange("(c p) n -> p c n", p=128)),
            (tgt_raw[:, :], W_tgt), (outx_raw[:, :], W_outx), (mask_raw[:, :], mask),
            (btgt[:, :], b_tgt.rearrange("(p a) -> p a", a=1)),
            (bk[:, :], b_src[0:D].rearrange("(p a) -> p a", a=1)),
            (bv_row[:, :], b_src[D:2 * D].partition_broadcast(128)),
            (bo0_row[:, :], b_out0.partition_broadcast(128)),
            (box_row[:, :], b_outx.partition_broadcast(128)),
            (heads[:, :], head_rows_in),
            (mrow[:, :, :], mask.partition_broadcast(128)),
            (ident[:, :], eye), (band_f[:, :], band),
        ]

        def setup_tensor(pe):
            n = [0]

            def group(*mms):
                if n[0] >= 2:
                    pe.wait_ge(setup_ev, n[0] - 1)
                for out_ap, lhsT, rhs, start, stop, tr in mms:
                    last = nc.tensor.matmul(out_ap, lhsT, rhs, start=start, stop=stop, is_transpose=tr)
                last.then_inc(setup_pe, 1)
                n[0] += 1

            pe.wait_ge(loaded_w0, 16 * len(W0_LOADS))
            pe.wait_ge(const_set, 1)
            for h in range(H0):
                bank = banks[n[0] % 2]
                group(*[(bank[:, 128 * j:128 * j + 128], w[:, h * DK:(h + 1) * DK], ident[:, :], True, True, True)
                        for j, w in enumerate((wq_raw, wk_raw, wv_raw))])
                bank = banks[n[0] % 2]
                group((bank[:, 0:NR], rel_a[:, h * DK:(h + 1) * DK], feat_a[:, :], True, False, None),
                      (bank[:, 0:NR], rel_b[:, h * DK:(h + 1) * DK], feat_b[:, :], False, True, None))
                pe.wait_ge(setup_ev, n[0])
                pe.wait_ge(setup_cp, h + 1)
                bank = banks[n[0] % 2]
                group((bank[:, 0:128], wT[:, 0, :], wT[:, 1, :], True, True, None),
                      (bank[:, 128:256], wT[:, 2, :], wo_raw[:, h, :], True, True, None),
                      (bank[:, 256:257], wT[:, 1, :], eb[:, h:h + 1], True, True, None))
                bank = banks[n[0] % 2]
                group((bank[:, 0:NR], wT[:, 0, :], relT[:, :], True, True, None),
                      (bank[:, 256:256 + NR], pb_rep[:, :], relT[:, :], True, True, None))
            bank = banks[n[0] % 2]
            group(*[(bank[:, (2 * c + o) * 128:(2 * c + o) * 128 + 128], src_raw[:, o, c * 128:(c + 1) * 128],
                     ident[:, :], True, True, True) for c in range(2) for o in range(2)])
            bank = banks[n[0] % 2]
            group((bank[:, 0:128], tgt_raw[:, :], ident[:, :], True, True, True),
                  (bank[:, 128:256], outx_raw[:, 0:128], ident[:, :], True, True, True),
                  (bank[:, 256:384], outx_raw[:, 128:256], ident[:, :], True, True, True),
                  (bank[:, 384:384 + B], mask_raw[:, :], ident[0:B, 0:B], True, True, True))

        def setup_vector(dve):
            n = [0]

            def take(*copies):
                dve.wait_ge(setup_pe, n[0] + 1)
                for f in copies:
                    last = f()
                last.then_inc(setup_ev, 1)
                n[0] += 1

            dve.wait_ge(loaded_w0, 16 * len(W0_LOADS))
            nc.vector.tensor_copy(ident_bf[:, :], ident[:, :]).then_inc(const_cast, 1)
            nc.vector.tensor_copy(band_bf[:, :, :], band_f[:, :].unsqueeze(1).to_broadcast([128, 2, T])).then_inc(const_cast, 1)
            for h in range(H0):
                bank = banks[n[0] % 2]
                take(lambda: nc.vector.tensor_copy(wT[:, :, :], bank[:, 0:384].rearrange("p (j n) -> p j n", j=3)))
                bank = banks[n[0] % 2]
                take(lambda: nc.vector.tensor_copy(relT[:, :], bank[:, 0:NR]))
                if h:
                    dve.wait_ge(setup_pe, 4 * h)
                nc.vector.tensor_copy(pb_rep[:, :], pbias[:, h:h + 1].to_broadcast([128, 128])).then_inc(setup_cp, 1)
                bank = banks[n[0] % 2]
                take(lambda: nc.vector.tensor_scalar(A_w[:, h, :], bank[:, 0:128], SCORE_SCALE0, None, ALU.mult),
                     lambda: nc.vector.tensor_copy(M_w[:, h, :], bank[:, 128:256]),
                     lambda: nc.vector.tensor_copy(u_b[:, h:h + 1], bank[:, 256:257]))
                bank = banks[n[0] % 2]
                take(lambda: nc.vector.tensor_scalar(C_w[:, h, :], bank[:, 0:NR], SCORE_SCALE0, None, ALU.mult),
                     lambda: nc.vector.tensor_copy(pos_c[:, h, :], bank[:, 256:256 + NR]))
            bank = banks[n[0] % 2]
            take(lambda: nc.vector.tensor_copy(srcT[:, :, :], bank[:, :].rearrange("p (c n) -> p c n", c=2)))
            bank = banks[n[0] % 2]
            take(lambda: nc.vector.tensor_copy(tgtT[:, :], bank[:, 0:128]),
                 lambda: nc.vector.tensor_copy(outxT[:, :, :], bank[:, 128:384].rearrange("p (c n) -> p c n", c=2)),
                 lambda: nc.vector.tensor_copy(mcol[:, :], bank[:, 384:384 + B]))

        SETUP_RESULTS = 4 * H0 + 2
        setup.close()

        st1 = sb1("st1", [128, 2, 6])
        mv1 = sb1("mv1", [128, 2, 2])
        rs1 = sb1("rs1", [128, 2, 1])
        st2 = sb1("st2", [128, 2, 6])
        mv2 = sb1("mv2", [128, 2, 2])
        rs2 = sb1("rs2", [128, 2, 1])
        st3 = sb1("st3", [128, 2, 6])
        mv3 = sb1("mv3", [128, 2, 2])
        rs3 = sb1("rs3", [128, 2, 1])
        xh = sb1("xh", [128, 2, D])
        xhT = sb1("xhT", [128, 2, T])
        GT = sb1("GT", [128, 2, H0, T])
        pos_sb = sb1("pos_sb", [128, H0, NR])
        sc = sb1("sc", [128, 2, H0, T])
        Y = sb1("Y", [128, 2, H0, D])
        pT = sb1("pT", [128, H0, T])
        nmax = sb1("nmax", [128, 2, H0])
        rsum = sb1("rsum", [128, 2, H0])
        rinv = sb1("rinv", [128, 2, H0])
        xb = sb1("xb", [128, 2, D])
        x1 = sb1("x1", [128, 2, D])
        x1b = sb1("x1b", [128, 2, D])
        xh2 = sb1("xh2", [128, 2, D])
        xh2T = sb1("xh2T", [128, 2, T])
        ctx_sb = sb1("ctx_sb", [128, 2, CTX])
        ctxT = sb1("ctxT", [128, 2, T])
        kT = sb1("kT", [128, T])
        kexp = sb1("kexp", [128, HX, T])
        v2 = sb1("v2", [128, 2, HX, DX + 1])
        q2T = sb1("q2T", [128, T])
        madd = sb1("madd", [128, T])
        p2 = sb1("p2", [128, 2, HX, T])
        p2T = sb1("p2T", [128, HX, T])
        nmax2 = sb1("nmax2", [128, 2, HX])
        r2 = sb1("r2", [128, HX])
        upd = sb1("upd", [128, D])
        updT = sb1("updT", [128, T])
        zh = sb1("zh", [128, D])

        S1 = {n: sem("a_" + n) for n in (
            "stats1 mean1 shift1 rstd1 xh xhT_mm xhT G_mm G pos_mm pos pos_stored shifted_in S_mm summed nmax exp psum rinv pn "
            "pT_mm pT Y_mm Y o_mm xb x1 x1b stats2 mean2 shift2 rstd2 xh2 xh2T_mm xh2T ctx_in ctxT_mm ctxT K_mm KV_mm kv kT v2b v2 kexp q2_mm q2T0 q2T "
            "madd S2_mm summed2 nmax2 exp2 p2T_mm p2T o2_mm r2 upd updT_mm updT out2_mm x2 stats3 mean3 shift3 rstd3 zh zT_mm zT").split()}

        W0 = [banks[2], banks[3]]
        W1b = [banks[4], banks[5]]
        SMALL_T = banks[6][:, 0:128]
        CTX_T = banks[6][:, 128:384]
        KQ_PS = banks[6][:, 384:512]
        V_PS = banks[7][:, 0:128]
        O_PS = banks[7][:, 128:256]
        O2_PS = banks[7][:, 256:256 + HX * (DX + 1)]
        HALF = H0 // 2

        def part1_sync(sp):
            def emit(k, i, on):
                first = 2 * i
                u0 = first + k
                if on(0):
                    if reused(first, k, 0, 2):
                        wait_apart(sp, S1["ctxT_mm"], u0 - 1)
                    sp.dma_start(ctx_sb[:, k % 2, :], ctx_in[bass.ds(u0, 1)].rearrange("a t c -> t (a c)")).then_inc(S1["ctx_in"], 16)
                    wait_apart(sp, S1["pos"], 4 * u0 + 4)
                    if reused(first, k, 0, 2):
                        wait_apart(sp, S1["shifted_in"], 16 * (u0 - 1))
                    sp.dma_start(pos_scratch[k % 2, 0:T * H0 * NR].rearrange("(t n) -> t n", t=T),
                                 pos_sb[:, :, :].rearrange("p h n -> p (h n)")).then_inc(S1["pos_stored"], 16)
                    wait_apart(sp, S1["pos_stored"], 16 * (u0 + 1))
                    if reused(first, k, 0, 2):
                        sp.wait_ge(S1["pT_mm"], u0 - 1)
                    sp.dma_start(sc[:, k % 2, :, :], shifted_view(k % 2)).then_inc(S1["shifted_in"], 16)
            pipeline(sp, B, 2, 0, emit, peeled=2)

        def shifted_view(slot):
            v = pos_scratch[slot, T - 1:T]
            return bass.AP(v.tensor, v.offset, [[H0 * NR - 1, T], [NR, H0], [1, T]])

        def part1_tensor(pe):
            def emit(k, i, on):
                first = 2 * i
                u0, u1, u2 = first + k, first + k - 1, first + k - 2
                i0, i1, i2 = k % 2, (k - 1) % 2, k % 2
                if on(0):
                    pe.wait_ge(S1["xh"], u0 + 1)
                    if reused(first, k, 0, 2):
                        pe.wait_ge(S1["q2T"], u0 - 1)
                    elif reused(first, k, 0, 1):
                        pe.wait_ge(S1["xhT"], u0)
                    nc.tensor.transpose(SMALL_T, xh[:, i0, :], ident[:, :]).then_inc(S1["xhT_mm"], 1)
                if on(2):
                    pe.wait_ge(S1["exp2"], u2 + 1)
                    if on(1):
                        pe.wait_ge(S1["summed"], u2 + 2)
                    for h in range(HX):
                        last = nc.tensor.transpose(W0[h // HALF][:, h % HALF * 128:h % HALF * 128 + 128], p2[:, i2, h, :], ident[:, :])
                    last.then_inc(S1["p2T_mm"], 1)
                if on(0):
                    pe.wait_ge(S1["xhT"], u0 + 1)
                    if reused(first, k, 1, 1):
                        pe.wait_ge(S1["summed2"], u0 - 1)
                    for h in range(H0):
                        last = nc.tensor.matmul(W1b[h // HALF][:, h % HALF * 128:h % HALF * 128 + 128], A_w[:, h, :], xhT[:, i0, :], start=True, stop=True)
                    last.then_inc(S1["G_mm"], 1)
                    for pr in range(4):
                        if pr >= 2:
                            pe.wait_ge(S1["pos"], 4 * u0 + pr - 1)
                        elif reused(first, k, 0, 1):
                            pe.wait_ge(S1["pos"], 4 * u0 + pr - 1)
                        nc.tensor.matmul(banks[pr % 2][:, 0:2 * NR], xhT[:, i0, :], C_w[:, 2 * pr:2 * pr + 2, :].rearrange("p h n -> p (h n)"),
                                         start=True, stop=True).then_inc(S1["pos_mm"], 1)
                if on(2):
                    pe.wait_ge(S1["p2T"], u2 + 1)
                    pe.wait_ge(S1["v2b"], u2 + 1)
                    for h in range(HX):
                        last = nc.tensor.matmul(O2_PS[:, h * (DX + 1):(h + 1) * (DX + 1)], p2T[:, h, :], v2[:, i2, h, :], start=True, stop=True)
                    last.then_inc(S1["o2_mm"], 1)
                if on(0):
                    pe.wait_ge(S1["G"], u0 + 1)
                    if on(2):
                        pe.wait_ge(S1["p2T"], u2 + 1)
                    for h in range(H0):
                        last = nc.tensor.matmul(W0[h // HALF][:, h % HALF * 128:h % HALF * 128 + 128], GT[:, i0, h, :], xhT[:, i0, :], start=True, stop=True)
                    last.then_inc(S1["S_mm"], 1)
                if on(2):
                    pe.wait_ge(S1["upd"], u2 + 1)
                    if on(0):
                        pe.wait_ge(S1["xhT"], u0 + 1)
                    else:
                        pe.wait_ge(S1["q2T"], u2 + 1)
                    nc.tensor.transpose(SMALL_T, upd[:, :], ident[:, :]).then_inc(S1["updT_mm"], 1)
                if on(0):
                    pe.wait_ge(S1["G"], u0 + 1)
                    for j in range(2):
                        last = nc.tensor.matmul(W1b[j][:, :], xhT[:, i0, :], M_w[:, HALF * j:HALF * (j + 1), :].rearrange("p h n -> p (h n)"), start=True, stop=True)
                    last.then_inc(S1["Y_mm"], 1)
                if on(1):
                    pe.wait_ge(S1["pn"], u1 + 1)
                    if on(0):
                        pe.wait_ge(S1["Y"], u0 + 1)
                    for h in range(H0):
                        last = nc.tensor.transpose(W1b[h // HALF][:, h % HALF * 128:h % HALF * 128 + 128], sc[:, i1, h, :], ident[:, :])
                    last.then_inc(S1["pT_mm"], 1)
                if on(2):
                    pe.wait_ge(S1["updT"], u2 + 1)
                    nc.tensor.matmul(O_PS, xh2T[:, i2, :], outxT[:, 0, :], start=True, stop=False)
                    nc.tensor.matmul(O_PS, updT[:, :], outxT[:, 1, :], start=False, stop=True).then_inc(S1["out2_mm"], 1)
                if on(1):
                    pe.wait_ge(S1["ctx_in"], 16 * (u1 + 1))
                    if on(2):
                        pe.wait_ge(S1["updT"], u2 + 1)
                    elif on(0):
                        pe.wait_ge(S1["xhT"], u0 + 1)
                    for c in range(2):
                        last = nc.tensor.transpose(CTX_T[:, c * 128:c * 128 + 128], ctx_sb[:, i1, c * 128:c * 128 + 128], ident[:, :])
                    last.then_inc(S1["ctxT_mm"], 1)
                if on(1):
                    pe.wait_ge(S1["pT"], u1 + 1)
                    pe.wait_ge(S1["Y"], u1 + 1)
                    if on(2):
                        pe.wait_ge(S1["x2"], u2 + 1)
                    elif reused(first, k, 1, 1):
                        pe.wait_ge(S1["v2b"], u1)
                    for h in range(H0):
                        last = nc.tensor.matmul(O_PS, pT[:, h, :], Y[:, i1, h, :], start=(h == 0), stop=(h == H0 - 1))
                    last.then_inc(S1["o_mm"], 1)
                if on(1):
                    pe.wait_ge(S1["ctxT"], u1 + 1)
                    for c in range(2):
                        last = nc.tensor.matmul(KQ_PS, srcT[:, c, 0:D], ctxT[:, c, :], start=(c == 0), stop=(c == 1))
                    last.then_inc(S1["K_mm"], 1)
                    pe.wait_ge(S1["x1"], u1 + 1)
                    for c in range(2):
                        last = nc.tensor.matmul(V_PS, ctxT[:, c, :], srcT[:, c, D:2 * D], start=(c == 0), stop=(c == 1))
                    last.then_inc(S1["KV_mm"], 1)
                if on(2):
                    pe.wait_ge(S1["zh"], u2 + 1)
                    if on(1):
                        pe.wait_ge(S1["kv"], u1 + 1)
                    nc.tensor.transpose(SMALL_T, zh[:, :], ident[:, :]).then_inc(S1["zT_mm"], 1)
                if on(1):
                    pe.wait_ge(S1["xh2"], u1 + 1)
                    if on(2):
                        pe.wait_ge(S1["zT"], u2 + 1)
                    else:
                        pe.wait_ge(S1["kv"], u1 + 1)
                    nc.tensor.transpose(SMALL_T, xh2[:, i1, :], ident[:, :]).then_inc(S1["xh2T_mm"], 1)
                    pe.wait_ge(S1["xh2T"], u1 + 1)
                    nc.tensor.matmul(KQ_PS, tgtT[:, :], xh2T[:, i1, :], start=True, stop=True).then_inc(S1["q2_mm"], 1)
                    pe.wait_ge(S1["q2T"], u1 + 1)
                    pe.wait_ge(S1["kexp"], u1 + 1)
                    pe.wait_ge(S1["pT"], u1 + 1)
                    for j in range(2):
                        last = nc.tensor.matmul(W1b[j][:, :], q2T[:, :], kexp[:, HALF * j:HALF * (j + 1), :].rearrange("p h n -> p (h n)"), start=True, stop=True)
                    last.then_inc(S1["S2_mm"], 1)
            pipeline(pe, B, 2, 2, emit, peeled=2)

        def part1_scalar(act):
            def emit(k, i, on):
                first = 2 * i
                u0, u1, u2 = first + k, first + k - 1, first + k - 2
                i0, i1, i2 = k % 2, (k - 1) % 2, k % 2
                if on(0):
                    act.wait_ge(S1["xhT_mm"], u0 + 1)
                    if reused(first, k, 0, 2):
                        act.wait_ge(S1["Y_mm"], u0 - 1)
                    nc.scalar.activation(xhT[:, i0, :], SMALL_T, ACT.Copy).then_inc(S1["xhT"], 1)
                if on(2):
                    act.wait_ge(S1["p2T_mm"], u2 + 1)
                    if reused(first, k, 2, 1):
                        act.wait_ge(S1["o2_mm"], u2)
                    for j in range(2):
                        last = nc.scalar.activation(p2T[:, HALF * j:HALF * (j + 1), :].rearrange("p h n -> p (h n)"), W0[j][:, :], ACT.Copy)
                    last.then_inc(S1["p2T"], 1)
                if on(1):
                    act.wait_ge(S1["nmax"], u1 + 1)
                    if reused(first, k, 1, 2):
                        act.wait_ge(S1["rinv"], u1 - 1)
                    for h in range(H0):
                        last = nc.scalar.activation(sc[:, i1, h, :], sc[:, i1, h, :], ACT.Exp, bias=nmax[:, i1, h:h + 1], scale=1.0,
                                                    accum_out=rsum[:, i1, h:h + 1])
                    last.then_inc(S1["exp"], 1)
                if on(2):
                    act.wait_ge(S1["updT_mm"], u2 + 1)
                    if reused(first, k, 2, 1):
                        act.wait_ge(S1["out2_mm"], u2)
                    nc.scalar.activation(updT[:, :], SMALL_T, ACT.Copy).then_inc(S1["updT"], 1)
                if on(0):
                    act.wait_ge(S1["Y_mm"], u0 + 1)
                    if reused(first, k, 0, 2):
                        act.wait_ge(S1["o_mm"], u0 - 1)
                    for j in range(2):
                        last = nc.scalar.activation(Y[:, i0, HALF * j:HALF * (j + 1), :].rearrange("p h n -> p (h n)"), W1b[j][:, :], ACT.Copy)
                    last.then_inc(S1["Y"], 1)
                if on(1):
                    act.wait_ge(S1["pT_mm"], u1 + 1)
                    if reused(first, k, 1, 1):
                        act.wait_ge(S1["o_mm"], u1)
                    for j in range(2):
                        last = nc.scalar.activation(pT[:, HALF * j:HALF * (j + 1), :].rearrange("p h n -> p (h n)"), W1b[j][:, :], ACT.Copy)
                    last.then_inc(S1["pT"], 1)
                    act.wait_ge(S1["ctxT_mm"], u1 + 1)
                    if reused(first, k, 1, 1):
                        act.wait_ge(S1["KV_mm"], u1)
                    nc.scalar.activation(ctxT[:, :, :].rearrange("p c n -> p (c n)"), CTX_T, ACT.Copy).then_inc(S1["ctxT"], 1)
                if on(2):
                    act.wait_ge(S1["zT_mm"], u2 + 1)
                    nc.scalar.activation(zT[:, bass.ds(u2, 1), :].rearrange("p a n -> p (a n)"), SMALL_T, ACT.Copy).then_inc(S1["zT"], 1)
                if on(1):
                    act.wait_ge(S1["xh2T_mm"], u1 + 1)
                    if reused(first, k, 1, 2):
                        act.wait_ge(S1["out2_mm"], u1 - 1)
                    nc.scalar.activation(xh2T[:, i1, :], SMALL_T, ACT.Copy).then_inc(S1["xh2T"], 1)
                    act.wait_ge(S1["nmax2"], u1 + 1)
                    for h in range(HX):
                        last = nc.scalar.activation(p2[:, i1, h, :], p2[:, i1, h, :], ACT.Exp, bias=nmax2[:, i1, h:h + 1], scale=SCORE_SCALEX)
                    last.then_inc(S1["exp2"], 1)
            pipeline(act, B, 2, 2, emit, peeled=2)

        def part1_vector(dve):
            def batch(u):
                return bass.ds(u, 1)

            def norm_stats(src, st, mv, which, u):
                nc.vector.bn_stats(st, src).then_inc(S1["stats" + which], 1)
                wait_apart(dve, S1["stats" + which], u + 1)
                nc.vector.bn_aggr(mv, st).then_inc(S1["mean" + which], 1)

            def emit(k, i, on):
                first = 2 * i
                u0, u1, u2 = first + k, first + k - 1, first + k - 2
                i0, i1, i2 = k % 2, (k - 1) % 2, k % 2
                if on(0):
                    xin = x_all[:, batch(u0), :].rearrange("p a n -> p (a n)")
                    norm_stats(xin, st1[:, i0, :], mv1[:, i0, :], "1", u0)
                    dve.wait_ge(S1["rstd1"], u0 + 1)
                    if reused(first, k, 0, 2):
                        dve.wait_ge(S1["xhT_mm"], u0 - 1)
                    nc.vector.tensor_scalar(xh[:, i0, :], xin, mv1[:, i0, 0:1], rs1[:, i0, :], ALU.subtract, ALU.mult).then_inc(S1["xh"], 1)
                    dve.wait_ge(S1["G_mm"], u0 + 1)
                    if reused(first, k, 0, 2):
                        dve.wait_ge(S1["S_mm"], u0 - 1)
                    for j in range(2):
                        last = nc.vector.tensor_tensor(GT[:, i0, HALF * j:HALF * (j + 1), :], W1b[j][:, :].rearrange("p (h n) -> p h n", h=HALF),
                                                       u_b[:, HALF * j:HALF * (j + 1)].unsqueeze(2).to_broadcast([128, HALF, T]), ALU.add)
                    last.then_inc(S1["G"], 1)
                    if reused(first, k, 0, 1):
                        dve.wait_ge(S1["pos_stored"], 16 * u0)
                    for pr in range(4):
                        dve.wait_ge(S1["pos_mm"], 4 * u0 + pr + 1)
                        nc.vector.tensor_tensor(pos_sb[:, 2 * pr:2 * pr + 2, :].rearrange("p h n -> p (h n)"), banks[pr % 2][:, 0:2 * NR],
                                                pos_c[:, 2 * pr:2 * pr + 2, :].rearrange("p h n -> p (h n)"), ALU.add).then_inc(S1["pos"], 1)
                if on(1):
                    dve.wait_ge(S1["exp"], u1 + 1)
                    if reused(first, k, 1, 2):
                        dve.wait_ge(S1["pn"], u1 - 1)
                    nc.vector.reciprocal(rinv[:, i1, :], rsum[:, i1, :]).then_inc(S1["rinv"], 1)
                if on(2):
                    o2 = O2_PS.rearrange("p (h n) -> p h n", h=HX)
                    dve.wait_ge(S1["o2_mm"], u2 + 1)
                    nc.vector.reciprocal(r2[:, :], o2[:, :, DX]).then_inc(S1["r2"], 1)
                    dve.wait_ge(S1["r2"], u2 + 1)
                    if reused(first, k, 2, 1):
                        dve.wait_ge(S1["updT_mm"], u2)
                    nc.vector.tensor_tensor(upd[:, :].rearrange("p (h n) -> p h n", h=HX), o2[:, :, 0:DX],
                                            r2[:, :].unsqueeze(2).to_broadcast([128, HX, DX]), ALU.mult).then_inc(S1["upd"], 1)
                    dve.wait_ge(S1["out2_mm"], u2 + 1)
                    dve.wait_ge(S1["x1b"], u2 + 1)
                    xout = x_all[:, batch(u2), :].rearrange("p a n -> p (a n)")
                    nc.vector.tensor_tensor(xout, O_PS, x1b[:, i2, :], ALU.add).then_inc(S1["x2"], 1)
                    wait_apart(dve, S1["x2"], u2 + 1)
                    norm_stats(xout, st3[:, i2, :], mv3[:, i2, :], "3", u2)
                    dve.wait_ge(S1["rstd3"], u2 + 1)
                    if reused(first, k, 2, 1):
                        dve.wait_ge(S1["zT_mm"], u2)
                    nc.vector.tensor_scalar(zh[:, :], xout, mv3[:, i2, 0:1], rs3[:, i2, :], ALU.subtract, ALU.mult).then_inc(S1["zh"], 1)
                if on(1):
                    dve.wait_ge(S1["o_mm"], u1 + 1)
                    dve.wait_ge(S1["xb"], u1 + 1)
                    if reused(first, k, 1, 2):
                        dve.wait_ge(S1["x1b"], u1 - 1)
                    nc.vector.tensor_tensor(x1[:, i1, :], O_PS, xb[:, i1, :], ALU.add).then_inc(S1["x1"], 1)
                    wait_apart(dve, S1["x1"], u1 + 1)
                    norm_stats(x1[:, i1, :], st2[:, i1, :], mv2[:, i1, :], "2", u1)
                    dve.wait_ge(S1["K_mm"], u1 + 1)
                    if reused(first, k, 1, 1):
                        dve.wait_ge(S1["kexp"], u1)
                    mr = mrow[:, batch(u1), :].rearrange("p a n -> p (a n)")
                    nc.vector.scalar_tensor_tensor(kT[:, :], KQ_PS, bk[:, :], mr, ALU.add, ALU.mult).then_inc(S1["kv"], 1)
                    if reused(first, k, 1, 2):
                        dve.wait_ge(S1["o2_mm"], u1 - 1)
                    vdst = v2[:, i1, :, 0:DX]
                    dve.wait_ge(S1["KV_mm"], u1 + 1)
                    nc.vector.tensor_tensor(vdst, V_PS.rearrange("p (h n) -> p h n", h=HX), bv_row[:, :].rearrange("p (h n) -> p h n", h=HX), ALU.add).then_inc(S1["v2b"], 1)
                    nc.vector.tensor_scalar(madd[:, :], mr, 0.0, MASKED, ALU.is_equal, ALU.mult).then_inc(S1["madd"], 1)
                    dve.wait_ge(S1["v2b"], u1 + 1)
                    nc.vector.tensor_scalar(vdst, vdst, mcol[:, batch(u1)], None, ALU.mult).then_inc(S1["v2"], 1)
                    dve.wait_ge(S1["rstd2"], u1 + 1)
                    if reused(first, k, 1, 2):
                        dve.wait_ge(S1["xh2T_mm"], u1 - 1)
                    nc.vector.tensor_scalar(xh2[:, i1, :], x1[:, i1, :], mv2[:, i1, 0:1], rs2[:, i1, :], ALU.subtract, ALU.mult).then_inc(S1["xh2"], 1)
                    dve.wait_ge(S1["q2_mm"], u1 + 1)
                    if reused(first, k, 1, 1):
                        dve.wait_ge(S1["S2_mm"], u1)
                    nc.vector.scalar_tensor_tensor(q2T[:, :], KQ_PS, btgt[:, :], mr, ALU.add, ALU.mult).then_inc(S1["q2T"], 1)
                if on(0):
                    dve.wait_ge(S1["S_mm"], u0 + 1)
                    dve.wait_ge(S1["shifted_in"], 16 * (u0 + 1))
                    for j in range(2):
                        part = sc[:, i0, HALF * j:HALF * (j + 1), :].rearrange("p h n -> p (h n)")
                        last = nc.vector.tensor_tensor(part, W0[j][:, :], part, ALU.add)
                    last.then_inc(S1["summed"], 1)
                if on(1):
                    dve.wait_ge(S1["S2_mm"], u1 + 1)
                    dve.wait_ge(S1["madd"], u1 + 1)
                    if reused(first, k, 1, 2):
                        dve.wait_ge(S1["p2T_mm"], u1 - 1)
                    for j in range(2):
                        last = nc.vector.tensor_tensor(p2[:, i1, HALF * j:HALF * (j + 1), :], W1b[j][:, :].rearrange("p (h n) -> p h n", h=HALF),
                                                       madd[:, :].unsqueeze(1).to_broadcast([128, HALF, T]), ALU.add)
                    last.then_inc(S1["summed2"], 1)
                if on(0):
                    dve.wait_ge(S1["summed"], u0 + 1)
                    nc.vector.tensor_reduce(nmax[:, i0, :], sc[:, i0, :, :], X_AXIS, ALU.max, negate=True).then_inc(S1["nmax"], 1)
                if on(1):
                    dve.wait_ge(S1["summed2"], u1 + 1)
                    nc.vector.tensor_reduce(r2max[:, :], p2[:, i1, :, :], X_AXIS, ALU.max, negate=True).then_inc(S1["q2T0"], 1)
                    dve.wait_ge(S1["q2T0"], u1 + 1)
                    nc.vector.tensor_scalar(nmax2[:, i1, :], r2max[:, :], SCORE_SCALEX, None, ALU.mult).then_inc(S1["nmax2"], 1)
            pipeline(dve, B, 2, 2, emit, peeled=2)

        r2max = sb1("r2max", [128, HX])

        def part1_pool(pool):
            def rstd(mv, rs, which, u):
                wait_apart(pool, S1["mean" + which], u + 1)
                nc.gpsimd.tensor_scalar(rs, mv[:, 1:2], EPS, 0.0, ALU.add, ALU.add).then_inc(S1["shift" + which], 1)
                pool.wait_ge(S1["shift" + which], u + 1)
                nc.gpsimd.tensor_tensor(rs, rs, neg_half[:, 0:1], ALU.pow).then_inc(S1["rstd" + which], 1)

            def emit(k, i, on):
                first = 2 * i
                u0, u1, u2 = first + k, first + k - 1, first + k - 2
                i0, i1, i2 = k % 2, (k - 1) % 2, k % 2
                if on(0):
                    rstd(mv1[:, i0, :], rs1[:, i0, :], "1", u0)
                    nc.gpsimd.tensor_tensor(xb[:, i0, :], x_all[:, bass.ds(u0, 1), :].rearrange("p a n -> p (a n)"), bo0_row[:, :], ALU.add).then_inc(S1["xb"], 1)
                if on(1):
                    pool.wait_ge(S1["rinv"], u1 + 1)
                    nc.gpsimd.tensor_tensor(sc[:, i1, :, :], sc[:, i1, :, :], rinv[:, i1, :].unsqueeze(2).to_broadcast([128, H0, T]), ALU.mult).then_inc(S1["pn"], 1)
                if on(2):
                    rstd(mv3[:, i2, :], rs3[:, i2, :], "3", u2)
                if on(1):
                    pool.wait_ge(S1["x1"], u1 + 1)
                    nc.gpsimd.tensor_tensor(x1b[:, i1, :], x1[:, i1, :], box_row[:, :], ALU.add).then_inc(S1["x1b"], 1)
                    rstd(mv2[:, i1, :], rs2[:, i1, :], "2", u1)
                    pool.wait_ge(S1["kv"], u1 + 1)
                    if reused(first, k, 1, 1):
                        pool.wait_ge(S1["S2_mm"], u1)
                    nc.gpsimd.tensor_tensor(kexp[:, :, :], kT[:, :].unsqueeze(1).to_broadcast([128, HX, T]),
                                            heads[:, :].unsqueeze(2).to_broadcast([128, HX, T]), ALU.mult).then_inc(S1["kexp"], 1)
            pipeline(pool, B, 2, 2, emit, peeled=2)

        part1.close()

        wqkv = sb("wqkv", [128, 3, INNER])
        wo = sb("wo", [128, OUT_CHUNKS, D])
        w1 = sb("w1", [128, 2 * FF])
        w2 = sb("w2", [128, 3, D])
        vecs = sb("vecs", [128, 3])
        b1c = sb("b1c", [128, 2, 3])
        rot_base = sb("rot_base", [128, 4, DL])
        qk_scl = sb("qk_scl", [128, 2, DL])
        rot_tab = sb("rot_tab", [128, 4, DL])
        xs = sb("xs", [128, 2, T])
        sq = sb("sq", [128, 2, 2 * G, DL])
        ss = sb("ss", [128, 2, 2 * G])
        ssc = sb("ssc", [128, 2, 2 * G])
        rn = sb("rn", [128, 8, 2 * G])
        own = sb("own", [128, 4, 2 * G, DL])
        crossed = sb("crossed", [128, 4, 2 * G, DL])
        rot = sb("rot", [128, 4, 2 * G, DL])
        qkT = sb("qkT", [128, 2, 4, T])
        v_sb = sb("v_sb", [128, 8, G, DL + 1])
        nm = sb("nm", [128, 2, G // 2, 2])
        mx = sb("mx", [128, 2, 2, G // 2])
        p = sb("p", [128, 2, G, T])
        pTl = sb("pTl", [128, 2, G, T])
        ri = sb("ri", [128, 2, G])
        o_sb = sb("o_sb", [128, 2, G, DL])
        oT = sb("oT", [128, 8, 2 * T])
        xs4 = sb("xs4", [128, 2, QUAD, T])
        xc = sb("xc", [128, 2, NQ])
        xsq = sb("xsq", [128, NQ])
        var_sb = sb("var_sb", [128, QUAD])
        rstd_rep = sb("rstd_rep", [128, QUAD, T])
        xn0 = sb("xn0", [128, NQ])
        xn = sb("xn", [128, 2, NQ])
        gel = sb("gel", [128, 2, NQ])
        uf = sb("uf", [128, 2, 3, NQ])
        zq = sb("zq", [128, 2, NQ])
        res = sb("res", [128, 2, QUAD, D])

        L = {n: sem("l_" + n) for n in (
            "w_attn w_ffn tab xs proj_qk proj square ssum clamp rn own_crossed rot0 rot v T1 qkT S mx nm exp T2 pT PV ri o OT oT WO res").split()}
        Fm = {n: sem("f_" + n) for n in (
            "xs4 mean_mm xc sq var_mm var rstd rstd_rep rstd_mm xn0 xn ga gelu u y_mm res").split()}
        O = {n: sem("o_" + n) for n in "copied T_mm added stored_even stored_odd".split()}
        O_stored = [O["stored_even"], O["stored_odd"]]
        zeroed = sem("zeroed")

        ATTN_LOADS, FFN_LOADS = 4, 10
        v_ps, pv_ps = banks[2][:, 0:G * DL], banks[2][:, 0:G * (DL + 1)]
        oT_ps, y_ps = banks[3][:, 0:2 * T], banks[3][:, 256:384]
        qkT_ps, pT_ps = banks[4], banks[5]
        s_ps = bank_pair[:, :, 0:2 * T]
        UB = HL // G

        def layers_sync(sp):
            def load(l):
                if not isinstance(l, int):
                    wait_apart(sp, L["proj"], l * UNITS)
                    wait_apart(sp, L["tab"], l)
                    wait_apart(sp, L["WO"], l * B)
                lay = bass.ds(l, 1)
                sp.dma_start(wqkv[:, :, :].rearrange("p a n -> p (a n)"), Wqkv[lay].rearrange("a p n -> p (a n)")).then_inc(L["w_attn"], 16)
                sp.dma_start(wo[:, :, :], Wo[lay].rearrange("a (c p) n -> p (a c) n", p=128)).then_inc(L["w_attn"], 16)
                sp.dma_start(qk_scl[:, 0, :], q_scale[lay].rearrange("a n -> (a n)").partition_broadcast(128)).then_inc(L["w_attn"], 16)
                sp.dma_start(qk_scl[:, 1, :], k_scale[lay].rearrange("a n -> (a n)").partition_broadcast(128)).then_inc(L["w_attn"], 16)
                if not isinstance(l, int):
                    wait_apart(sp, Fm["res"], l * QUADS)
                sp.dma_start(w1[:, :], W1[lay].rearrange("a p n -> p (a n)")).then_inc(L["w_ffn"], 16)
                sp.dma_start(w2[:, 0:2, :], W2[lay, 0:256].rearrange("a (c p) n -> p (a c) n", p=128)).then_inc(L["w_ffn"], 16)
                sp.dma_start(w2[0:FF - 256, 2, :], W2[lay, 256:FF].rearrange("a p n -> p (a n)")).then_inc(L["w_ffn"], 16)
                for j, v in enumerate((ln_g, ln_b, b2)):
                    sp.dma_start(vecs[:, j:j + 1], v[lay].rearrange("a p -> p a")).then_inc(L["w_ffn"], 16)
                for half in range(2):
                    sp.dma_start(b1c[:, half, 0:2], b1[lay, half * FF:half * FF + 256].rearrange("a (c p) -> p (a c)", p=128)).then_inc(L["w_ffn"], 16)
                    sp.dma_start(b1c[0:FF - 256, half, 2:3], b1[lay, half * FF + 256:(half + 1) * FF].rearrange("a p -> p a")).then_inc(L["w_ffn"], 16)

            load(0)
            with sp.Fori(1, LAYERS) as l:
                load(l)

        def attention_tensor(pe, l):
            U, NB = l * UNITS, l * B

            def emit(k, i, on):
                first = 8 * i

                def n(d):
                    return U + first + (k - d)
                if on(0):
                    bt = k // UB % 2
                    if k % UB == 0:
                        pe.wait_ge(L["xs"], NB + batch_of(i, k, 0) + 1)
                    if reused(first, k, 0, 2):
                        pe.wait_ge(L["own_crossed"], n(0) - 1)
                    g = k % UB
                    nc.tensor.matmul(banks[k % 2][:, :].rearrange("p (a n) -> p a n", a=2), xs[:, bt, :], wqkv[:, 0:2, g * G * DL:(g + 1) * G * DL],
                                     start=True, stop=True).then_inc(L["proj_qk"], 1)
                    if on(7):
                        pe.wait_ge(L["o"], n(7) + 1)
                    elif reused(first, k, 0, 1):
                        pe.wait_ge(L["v"], n(0))
                    nc.tensor.matmul(v_ps, xs[:, bt, :], wqkv[:, 2, g * G * DL:(g + 1) * G * DL], start=True, stop=True).then_inc(L["proj"], 1)
                if on(7):
                    pe.wait_ge(L["o"], n(7) + 1)
                    if reused(first, k, 7, 1):
                        pe.wait_ge(L["oT"], n(7))
                    if on(9) and (k - 9) % UB == UB - 1:
                        pe.wait_ge(L["res"], NB + batch_of(i, k, 9) + 1)
                    for c in range(2):
                        last = nc.tensor.transpose(oT_ps[:, c * T:(c + 1) * T], o_sb[:, (k - 7) % 2, 2 * c:2 * c + 2, :].rearrange("p h n -> p (h n)"), ident[:, :])
                    last.then_inc(L["OT"], 1)
                if on(3):
                    pe.wait_ge(L["rot"], n(3) + 1)
                    if reused(first, k, 3, 1):
                        pe.wait_ge(L["qkT"], n(3))
                    for c in range(4):
                        last = nc.tensor.transpose(qkT_ps[:, c * T:(c + 1) * T], rot[:, (k - 3) % 4, 2 * c:2 * c + 2, :].rearrange("p h n -> p (h n)"), ident[:, :])
                    last.then_inc(L["T1"], 1)
                if on(4):
                    j = (k - 4) % 2
                    pe.wait_ge(L["qkT"], n(4) + 1)
                    if reused(first, k, 4, 1):
                        pe.wait_ge(L["exp"], n(4))
                    for odd in range(2):
                        nc.tensor.matmul(s_ps[:, odd, :], ident_bf[:, :], band_bf[:, :, :].rearrange("p h n -> p (h n)"), start=True, stop=False, skip_group_check=True)
                    for h in range(G):
                        r = slice(h % 2 * DL, h % 2 * DL + DL)
                        last = nc.tensor.matmul(s_ps[:, h % 2, h // 2 * T:(h // 2 + 1) * T], qkT[r, j, h // 2, :], qkT[r, j, 2 + h // 2, :], start=False, stop=(h // 2 == 1), skip_group_check=True)
                    last.then_inc(L["S"], 1)
                if on(5):
                    pe.wait_ge(L["exp"], n(5) + 1)
                    if reused(first, k, 5, 1):
                        pe.wait_ge(L["pT"], n(5))
                    for h in range(G):
                        last = nc.tensor.transpose(pT_ps[:, h * T:(h + 1) * T], p[:, (k - 5) % 2, h, :], ident[:, :])
                    last.then_inc(L["T2"], 1)
                if on(6):
                    pe.wait_ge(L["pT"], n(6) + 1)
                    if on(0):
                        pe.wait_ge(L["v"], n(0) + 1)
                    else:
                        pe.wait_ge(L["o"], n(6))
                    for h in range(G):
                        last = nc.tensor.matmul(pv_ps[:, h * (DL + 1):(h + 1) * (DL + 1)], pTl[:, (k - 6) % 2, h, :], v_sb[:, (k - 6) % 8, h, :], start=True, stop=True)
                    last.then_inc(L["PV"], 1)
                if on(8) and (k - 8) % UB == UB - 1:
                    pe.wait_ge(L["oT"], n(8) + 1)
                    if on(7):
                        pe.wait_ge(L["oT"], n(7) + 1)
                    for c in range(OUT_CHUNKS):
                        slot = (k - 8 - (UB - 1) + c // 2) % 8
                        last = nc.tensor.matmul(y_ps, wo[:, c, :], oT[:, slot, c % 2 * T:(c % 2 + 1) * T], start=(c == 0), stop=(c == OUT_CHUNKS - 1))
                    last.then_inc(L["WO"], 1)
            pe.wait_ge(L["w_attn"], 16 * ATTN_LOADS * (l + 1))
            pipeline(pe, UNITS, 8, 8, emit, peeled=2)

        def batch_of(i, k, d):
            return 2 * i + (k - d) // UB

        def attention_scalar(act, l):
            U = l * UNITS

            def emit(k, i, on):
                first = 8 * i

                def n(d):
                    return U + first + (k - d)
                if on(0):
                    act.wait_ge(L["proj_qk"], n(0) + 1)
                    if reused(first, k, 0, 2):
                        act.wait_ge(L["ssum"], n(0) - 1)
                    nc.scalar.activation(sq[:, k % 2, :, :].rearrange("p h n -> p (h n)"), banks[k % 2][:, :], ACT.Square).then_inc(L["square"], 1)
                    act.wait_ge(L["proj"], n(0) + 1)
                    if reused(first, k, 0, 8):
                        act.wait_ge(L["PV"], n(0) - 7)
                    nc.scalar.activation(v_sb[:, k % 8, :, 0:DL], v_ps.rearrange("p (h n) -> p h n", h=G), ACT.Copy).then_inc(L["v"], 1)
                if on(7):
                    act.wait_ge(L["OT"], n(7) + 1)
                    nc.scalar.activation(oT[:, (k - 7) % 8, :], oT_ps, ACT.Copy).then_inc(L["oT"], 1)
                if on(3):
                    act.wait_ge(L["T1"], n(3) + 1)
                    if reused(first, k, 3, 2):
                        act.wait_ge(L["S"], n(3) - 1)
                    nc.scalar.activation(qkT[:, (k - 3) % 2, :, :].rearrange("p c n -> p (c n)"), qkT_ps[:, :], ACT.Copy).then_inc(L["qkT"], 1)
                if on(4):
                    act.wait_ge(L["nm"], n(4) + 1)
                    if reused(first, k, 4, 2):
                        act.wait_ge(L["T2"], n(4) - 1)
                    for h in range(G):
                        last = nc.scalar.activation(p[:, (k - 4) % 2, h, :], s_ps[:, h % 2, h // 2 * T:(h // 2 + 1) * T], ACT.Exp,
                                                    bias=nm[:, (k - 4) % 2, h // 2, h % 2:h % 2 + 1], scale=rn[:, (k - 4) % 8, h:h + 1])
                    last.then_inc(L["exp"], 1)
            pipeline(act, UNITS, 8, 8, emit)

        def shift_copy(dst, src, width):
            nc.vector.tensor_copy(dst[0:64], src[0:64])
            return nc.vector.tensor_copy(dst[64:128, :, 1:T], src[64:128, :, 0:T - 1])

        def attention_vector(dve, l):
            U, NB = l * UNITS, l * B

            def emit(k, i, on):
                first = 8 * i

                def n(d):
                    return U + first + (k - d)
                if on(0) and k % UB == 0:
                    b = batch_of(i, k, 0)
                    if reused(first, k, 0, 2 * UB):
                        dve.wait_ge(L["proj"], n(0) - UB)
                    shift_copy(xs[:, k // UB % 2, :].unsqueeze(1), zT[:, bass.ds(b, 1), :], T).then_inc(L["xs"], 1)
                if on(0):
                    j = k % 2
                    dve.wait_ge(L["square"], n(0) + 1)
                    if reused(first, k, 0, 4):
                        dve.wait_ge(L["rot"], n(0) - 3)
                    qk = banks[j][:, :].rearrange("p (a h n) -> p a h n", a=2, h=G)
                    nc.vector.tensor_tensor(own[:, k % 4, :, :].rearrange("p (a h) n -> p a h n", a=2), qk,
                                            rot_tab[:, 0:2, :].unsqueeze(2).to_broadcast([128, 2, G, DL]), ALU.mult)
                    nc.vector.tensor_tensor(crossed[:, k % 4, :, :].rearrange("p (a h) n -> p a h n", a=2), qk,
                                            rot_tab[:, 2:4, :].unsqueeze(2).to_broadcast([128, 2, G, DL]), ALU.mult).then_inc(L["own_crossed"], 1)
                    if reused(first, k, 0, 2):
                        dve.wait_ge(L["clamp"], n(0) - 1)
                    nc.vector.tensor_reduce(ss[:, j, :], sq[:, j, :, :], X_AXIS, ALU.add).then_inc(L["ssum"], 1)
                if on(4):
                    j = (k - 4) % 2
                    dve.wait_ge(L["S"], n(4) + 1)
                    nc.vector.tensor_reduce(mx[:, j, :, :], s_ps.rearrange("p o (h n) -> p o h n", h=2), X_AXIS, ALU.max, negate=True).then_inc(L["mx"], 1)
                    dve.wait_ge(L["mx"], n(4) + 1)
                    if reused(first, k, 4, 2):
                        dve.wait_ge(L["exp"], n(4) - 1)
                    nc.vector.tensor_tensor(nm[:, j, :, :], mx[:, j, :, :].rearrange("p o h -> p h o"),
                                            rn[:, (k - 4) % 8, 0:G].rearrange("p (h o) -> p h o", o=2), ALU.mult).then_inc(L["nm"], 1)
                if on(5):
                    dve.wait_ge(L["T2"], n(5) + 1)
                    if reused(first, k, 5, 2):
                        dve.wait_ge(L["PV"], n(5) - 1)
                    nc.vector.tensor_copy(pTl[:, (k - 5) % 2, :, :].rearrange("p h n -> p (h n)"), pT_ps[:, :]).then_inc(L["pT"], 1)
                if on(6):
                    j = (k - 6) % 2
                    pv = pv_ps.rearrange("p (h n) -> p h n", h=G)
                    dve.wait_ge(L["PV"], n(6) + 1)
                    nc.vector.reciprocal(ri[:, j, :], pv[:, :, DL]).then_inc(L["ri"], 1)
                    dve.wait_ge(L["ri"], n(6) + 1)
                    if reused(first, k, 6, 2):
                        dve.wait_ge(L["OT"], n(6) - 1)
                    nc.vector.tensor_tensor(o_sb[:, j, :, :], pv[:, :, 0:DL], ri[:, j, :].unsqueeze(2).to_broadcast([128, G, DL]), ALU.mult).then_inc(L["o"], 1)
                if on(8) and (k - 8) % UB == UB - 1:
                    b = batch_of(i, k, 8)
                    dve.wait_ge(L["WO"], NB + b + 1)
                    zb = zT[:, bass.ds(b, 1), :].rearrange("p a n -> p (a n)")
                    nc.vector.tensor_tensor(zb, y_ps, zb, ALU.add).then_inc(L["res"], 1)
            dve.wait_ge(L["w_attn"], 16 * ATTN_LOADS * (l + 1))
            for a in range(2):
                last = nc.vector.tensor_tensor(rot_tab[:, 2 * a:2 * a + 2, :], rot_base[:, 2 * a:2 * a + 2, :], qk_scl[:, :, :], ALU.mult)
            last.then_inc(L["tab"], 1)
            dve.wait_ge(L["tab"], l + 1)
            pipeline(dve, UNITS, 8, 8, emit)

        def attention_pool(pool, l):
            U = l * UNITS

            def emit(k, i, on):
                first = 8 * i
                def n(d):
                    return U + first + (k - d)
                j, j4 = k % 2, k % 4
                wait_apart(pool, L["ssum"], n(0) + 1)
                nc.gpsimd.tensor_scalar(ssc[:, j, :], ss[:, j, :], 1e-24, 0.0, ALU.max, ALU.add).then_inc(L["clamp"], 1)
                pool.wait_ge(L["clamp"], n(0) + 1)
                if reused(first, k, 0, 8):
                    pool.wait_ge(L["exp"], n(0) - 7)
                nc.gpsimd.tensor_tensor(rn[:, k % 8, :], ssc[:, j, :], neg_half[:, 0:2 * G], ALU.pow).then_inc(L["rn"], 1)
                pool.wait_ge(L["own_crossed"], n(0) + 1)
                if reused(first, k, 0, 4):
                    pool.wait_ge(L["T1"], n(0) - 3)
                hl = DL // 2
                nc.gpsimd.tensor_tensor(rot[:, j4, :, 0:hl], own[:, j4, :, 0:hl], crossed[:, j4, :, hl:DL], ALU.add)
                nc.gpsimd.tensor_tensor(rot[:, j4, :, hl:DL], own[:, j4, :, hl:DL], crossed[:, j4, :, 0:hl], ALU.add).then_inc(L["rot0"], 1)
                pool.wait_ge(L["rn"], n(0) + 1)
                pool.wait_ge(L["rot0"], n(0) + 1)
                nc.gpsimd.tensor_tensor(rot[:, j4, G:2 * G, :], rot[:, j4, G:2 * G, :],
                                        rn[:, k % 8, G:2 * G].unsqueeze(2).to_broadcast([128, G, DL]), ALU.mult).then_inc(L["rot"], 1)
            pipeline(pool, UNITS, 8, 0, emit)

        mean_ps, var_ps, yf_ps = banks[0], banks[1], banks[7]

        def ffn_tensor(pe, l):
            Q = l * QUADS

            def emit(k, i, on):
                first = 2 * i
                def n(d):
                    return Q + first + (k - d)

                def gate_value(c):
                    turn = 3 * n(1) + c
                    g_ps, a_ps = gate_banks(c, k)
                    c0, m = FF_CHUNKS[c]
                    if not (isinstance(first, int) and 3 * (first + k - 1) + c < 2):
                        pe.wait_ge(Fm["u"], turn - 1)
                    nc.tensor.matmul(g_ps[0:m, :], w1[:, FF + c0:FF + c0 + m], xn[:, (k - 1) % 2, :], start=True, stop=True)
                    nc.tensor.matmul(a_ps[0:m, :], w1[:, c0:c0 + m], xn[:, (k - 1) % 2, :], start=True, stop=True).then_inc(Fm["ga"], 1)

                if on(0):
                    pe.wait_ge(Fm["xs4"], n(0) + 1)
                    if reused(first, k, 0, 1):
                        pe.wait_ge(Fm["xc"], n(0))
                    nc.tensor.matmul(mean_ps[:, :], mean_w[:, :], xs4[:, k % 2, :, :].rearrange("p a n -> p (a n)"), start=True, stop=True).then_inc(Fm["mean_mm"], 1)
                if on(2):
                    if reused(first, k, 2, 1):
                        pe.wait_ge(Fm["res"], n(2))
                    pe.wait_ge(Fm["u"], 3 * n(2) + 3)
                    for c, (c0, m) in enumerate(FF_CHUNKS):
                        last = nc.tensor.matmul(yf_ps[:, :], w2[0:m, c, :], uf[0:m, k % 2, c, :], start=(c == 0), stop=(c == 2))
                    last.then_inc(Fm["y_mm"], 1)
                if on(1):
                    pe.wait_ge(Fm["xn"], n(1) + 1)
                    gate_value(0)
                if on(0):
                    pe.wait_ge(Fm["sq"], n(0) + 1)
                    if reused(first, k, 0, 1):
                        pe.wait_ge(Fm["xn0"], n(0))
                    for a in range(QUAD):
                        last = nc.tensor.matmul(var_ps[:, a:a + 1], xsq[:, a * T:(a + 1) * T], mean_w[:, 0:1], start=True, stop=True)
                    last.then_inc(Fm["var_mm"], 1)
                if on(1):
                    gate_value(1)
                if on(0):
                    pe.wait_ge(Fm["rstd_rep"], n(0) + 1)
                    for a in range(QUAD):
                        last = nc.tensor.matmul(var_ps[:, a * T:(a + 1) * T], rstd_rep[:, a, :], ident[:, :], start=True, stop=True)
                    last.then_inc(Fm["rstd_mm"], 1)
                if on(1):
                    gate_value(2)
            pe.wait_ge(L["w_ffn"], 16 * FFN_LOADS * (l + 1))
            pipeline(pe, QUADS, 2, 2, emit, peeled=2)

        def gate_banks(c, k):
            t = (3 * ((k - 1) % 2) + c) % 2
            return banks[2 + 2 * t], banks[3 + 2 * t]

        def ffn_scalar(act, l):
            Q = l * QUADS

            def emit(k, i, on):
                first = 2 * i
                def n(d):
                    return Q + first + (k - d)
                if on(0):
                    act.wait_ge(Fm["xc"], n(0) + 1)
                    if reused(first, k, 0, 1):
                        act.wait_ge(Fm["var_mm"], n(0))
                    nc.scalar.activation(xsq[:, :], xc[:, k % 2, :], ACT.Square).then_inc(Fm["sq"], 1)
                if on(1):
                    for c, (c0, m) in enumerate(FF_CHUNKS):
                        turn = 3 * n(1) + c
                        act.wait_ge(Fm["ga"], turn + 1)
                        g_ps, _ = gate_banks(c, k)
                        t = (3 * ((k - 1) % 2) + c) % 2
                        if not (isinstance(first, int) and 3 * (first + k - 1) + c < 2):
                            act.wait_ge(Fm["u"], turn - 1)
                        nc.scalar.activation(gel[0:m, t, :], g_ps[0:m, :], ACT.Gelu, bias=b1c[0:m, 1, c:c + 1], scale=1.0).then_inc(Fm["gelu"], 1)
            act.wait_ge(L["w_ffn"], 16 * FFN_LOADS * (l + 1))
            pipeline(act, QUADS, 2, 2, emit, peeled=2)

        def ffn_vector(dve, l):
            Q = l * QUADS

            def emit(k, i, on):
                first = 2 * i
                def n(d):
                    return Q + first + (k - d)
                if on(0):
                    if reused(first, k, 0, 2):
                        dve.wait_ge(Fm["xc"], n(0) - 1)
                    shift_copy(xs4[:, k % 2, :, :], zT[:, bass.ds((first + k) * QUAD, QUAD), :], NQ).then_inc(Fm["xs4"], 1)
                    dve.wait_ge(Fm["mean_mm"], n(0) + 1)
                    dve.wait_ge(Fm["xs4"], n(0) + 1)
                    nc.vector.tensor_tensor(xc[:, k % 2, :], xs4[:, k % 2, :, :].rearrange("p a n -> p (a n)"), mean_ps[:, :], ALU.subtract).then_inc(Fm["xc"], 1)
                if on(2):
                    dve.wait_ge(Fm["y_mm"], n(2) + 1)
                    zb = zT[:, bass.ds((first + (k - 2)) * QUAD, QUAD), :].rearrange("p a n -> p (a n)")
                    nc.vector.scalar_tensor_tensor(zb, yf_ps[:, :], vecs[:, 2:3], zb, ALU.add, ALU.add).then_inc(Fm["res"], 1)
                if on(1):
                    value_chunk(k, first, n, 0)
                if on(0):
                    dve.wait_ge(Fm["var_mm"], n(0) + 1)
                    nc.vector.tensor_scalar(var_sb[:, :], var_ps[:, 0:QUAD], EPS, None, ALU.add).then_inc(Fm["var"], 1)
                if on(1):
                    value_chunk(k, first, n, 1)
                if on(0):
                    dve.wait_ge(Fm["rstd"], n(0) + 1)
                    nc.vector.tensor_copy(rstd_rep[:, :, :], var_sb[:, :].unsqueeze(2).to_broadcast([128, QUAD, T])).then_inc(Fm["rstd_rep"], 1)
                if on(1):
                    value_chunk(k, first, n, 2)
                if on(0):
                    dve.wait_ge(Fm["rstd_mm"], n(0) + 1)
                    nc.vector.tensor_tensor(xn0[:, :], xc[:, k % 2, :], var_ps[:, :], ALU.mult).then_inc(Fm["xn0"], 1)
                    dve.wait_ge(Fm["xn0"], n(0) + 1)
                    nc.vector.tensor_scalar(xn[:, k % 2, :], xn0[:, :], vecs[:, 0:1], vecs[:, 1:2], ALU.mult, ALU.add).then_inc(Fm["xn"], 1)

            def value_chunk(k, first, n, c):
                c0, m = FF_CHUNKS[c]
                t = (3 * ((k - 1) % 2) + c) % 2
                _, a_ps = gate_banks(c, k)
                dve.wait_ge(Fm["gelu"], 3 * n(1) + c + 1)
                nc.vector.scalar_tensor_tensor(uf[0:m, (k - 1) % 2, c, :], a_ps[0:m, :], b1c[0:m, 0, c:c + 1], gel[0:m, t, :],
                                               ALU.add, ALU.mult).then_inc(Fm["u"], 1)

            dve.wait_ge(L["w_ffn"], 16 * FFN_LOADS * (l + 1))
            dve.wait_ge(L["res"], (l + 1) * B)
            pipeline(dve, QUADS, 2, 2, emit, peeled=2)
            dve.wait_ge(Fm["res"], (l + 1) * QUADS)

        def ffn_pool(pool, l):
            Q = l * QUADS

            def emit(k, i, on):
                first = 2 * i
                pool.wait_ge(Fm["var"], Q + first + k + 1)
                nc.gpsimd.tensor_tensor(var_sb[:, :], var_sb[:, :], neg_half[:, 0:QUAD], ALU.pow).then_inc(Fm["rstd"], 1)
            pipeline(pool, QUADS, 2, 0, emit, peeled=2)

        def final_scalar(act):
            def emit(k, i, on):
                first = 2 * i
                if reused(first, k, 0, 2):
                    act.wait_ge(O["T_mm"], first + k - 1)
                nc.scalar.activation(zq[:, k % 2, :], zT[:, bass.ds((first + k) * QUAD, QUAD), :].rearrange("p a n -> p (a n)"), ACT.Copy).then_inc(O["copied"], 1)
            act.wait_ge(Fm["res"], LAYERS * QUADS)
            pipeline(act, QUADS, 2, 0, emit, peeled=2)

        def final_tensor(pe):
            def emit(k, i, on):
                first = 2 * i
                pe.wait_ge(O["copied"], first + k + 1)
                if reused(first, k, 0, 2):
                    pe.wait_ge(O["added"], first + k - 1)
                for a in range(QUAD):
                    last = nc.tensor.transpose(banks[k % 2][:, a * 128:(a + 1) * 128], zq[:, k % 2, a * 128:(a + 1) * 128], ident[:, :])
                last.then_inc(O["T_mm"], 1)
            pipeline(pe, QUADS, 2, 0, emit, peeled=2)

        def final_vector(dve):
            def emit(k, i, on):
                first = 2 * i
                dve.wait_ge(O["T_mm"], first + k + 1)
                if reused(first, k, 0, 2):
                    dve.wait_ge(O_stored[k % 2], 16 * i)
                nc.vector.tensor_tensor(res[:, k % 2, :, :].rearrange("p a n -> p (a n)"), banks[k % 2][:, :],
                                        x_all[:, bass.ds((first + k) * QUAD, QUAD), :].rearrange("p a n -> p (a n)"), ALU.add).then_inc(O["added"], 1)
            pipeline(dve, QUADS, 2, 0, emit, peeled=2)

        def final_sync(sp):
            def emit(k, i, on):
                first = 2 * i
                wait_apart(sp, O["added"], first + k + 1)
                sp.dma_start(out[bass.ds((first + k) * QUAD, QUAD)].rearrange("b t d -> t b d"), res[:, k % 2, :, :]).then_inc(O_stored[k % 2], 16)
            pipeline(sp, QUADS, 2, 0, emit, peeled=2)
            for stored in O_stored:
                sp.wait_ge(stored, 16 * QUADS // 2)

        part1_done = sem("part1_done")
        ones_set = sem("ones_set")
        rot_in = sem("rot_in")

        ctx.enter_context(nc.allow_non_contiguous_dma(reason="small vectors laid out over partitions"))
        block = ctx.enter_context(nc.Block())

        @block.sync
        def _(sp):
            for dst, src in W0_LOADS:
                sp.dma_start(dst, src).then_inc(loaded_w0, 16)
            for c in range(4):
                sp.dma_start(x_all[:, c * 8:(c + 1) * 8, :], x[c * 8:(c + 1) * 8].rearrange("b t d -> t b d")).then_inc(loaded_x, 16)
            part1_sync(sp)
            sp.wait_ge(part1_done, 4)
            sp.dma_start(rot_base[:, :, :], rotary).then_inc(rot_in, 16)
            layers_sync(sp)
            final_sync(sp)

        @block.tensor
        def _(pe):
            setup_tensor(pe)
            pe.wait_ge(setup_ev, SETUP_RESULTS)
            part1_tensor(pe)
            pe.wait_ge(S1["zT"], B)
            nc.tensor.nop().then_inc(part1_done, 1)
            pe.wait_ge(const_cast, 2)
            with pe.Fori(0, LAYERS) as l:
                attention_tensor(pe, l)
                ffn_tensor(pe, l)
            final_tensor(pe)

        @block.vector
        def _(dve):
            nc.vector.memset(mean_w[:, :], 1.0 / D).then_inc(const_set, 1)
            setup_vector(dve)
            dve.wait_ge(setup_ev, SETUP_RESULTS)
            nc.vector.memset(v2[:, :, :, :], 1.0).then_inc(ones_set, 1)
            dve.wait_ge(ones_set, 1)
            dve.wait_ge(loaded_x, 64)
            part1_vector(dve)
            dve.wait_ge(S1["zT"], B)
            nc.vector.nop().then_inc(part1_done, 1)
            dve.wait_ge(part1_done, 4)
            nc.vector.memset(v_sb[:, :, :, :], 1.0).then_inc(ones_set, 1)
            nc.vector.memset(xs[64:128, :, 0:1], 0.0).then_inc(zeroed, 1)
            nc.vector.memset(xs4[64:128, :, :, 0:1], 0.0).then_inc(zeroed, 1)
            dve.wait_ge(ones_set, 2)
            dve.wait_ge(zeroed, 2)
            dve.wait_ge(rot_in, 16)
            with dve.Fori(0, LAYERS) as l:
                attention_vector(dve, l)
                ffn_vector(dve, l)
            final_vector(dve)

        @block.scalar
        def _(act):
            act.wait_ge(setup_ev, SETUP_RESULTS)
            part1_scalar(act)
            act.wait_ge(S1["zT"], B)
            nc.scalar.nop().then_inc(part1_done, 1)
            act.wait_ge(part1_done, 4)
            with act.Fori(0, LAYERS) as l:
                attention_scalar(act, l)
                ffn_scalar(act, l)
            final_scalar(act)

        @block.gpsimd
        def _(pool):
            nc.gpsimd.memset(neg_half[:, :], -0.5).then_inc(half_set, 1)
            pool.wait_ge(half_set, 1)
            pool.wait_ge(setup_ev, SETUP_RESULTS)
            pool.wait_ge(loaded_x, 64)
            part1_pool(pool)
            pool.wait_ge(S1["zT"], B)
            nc.gpsimd.nop().then_inc(part1_done, 1)
            pool.wait_ge(part1_done, 4)
            with pool.Fori(0, LAYERS) as l:
                attention_pool(pool, l)
                ffn_pool(pool, l)


_INS = ["x", "ctx_2048", "mask_BxS2_fk1", "L0_attn_w_qs", "L0_attn_w_ks", "L0_attn_w_vs", "L0_attn_w_rel_pos_k",
        "L0_attn_rel_embed_bias", "L0_attn_rel_pos_bias", "L0_attn_w_out", "L0_attn_b_out",
        "L0_xattn_W_src", "L0_xattn_b_src", "L0_xattn_W_tgt", "L0_xattn_b_tgt", "L0_xattn_W_out", "L0_xattn_b_out",
        "L0_ffn_Wqkv", "L0_ffn_q_scale", "L0_ffn_k_scale", "L0_ffn_Wo", "L0_ffn_ln_g", "L0_ffn_ln_b",
        "L0_ffn_W1", "L0_ffn_b1", "L0_ffn_W2", "L0_ffn_b2"]


def kernel(**inputs):
    import concourse.bacc as bacc
    from concourse.bass_utils import run_bass_kernel_spmd

    nc = bacc.Bacc("TRN2", target_bir_lowering=False, num_devices=1)
    arrays, args = {}, []
    given = [(n, np.ascontiguousarray(inputs[n])) for n in _INS] + [(n, make()) for n, make in CONSTANTS.items()]
    for name, a in given:
        arrays[f"in_{name}"] = a
        args.append(nc.dram_tensor(f"in_{name}", a.shape, mybir.dt.from_np(a.dtype), kind="ExternalInput").ap())
    args.append(nc.dram_tensor("out_0", (B, T, D), F32, kind="ExternalOutput").ap())
    build(nc, *args)
    r = run_bass_kernel_spmd(nc, [arrays], core_ids=[0])
    return r.results[0]["out_0"]
```

```python
import math

import numpy as np

import concourse.bass as bass
import concourse.mybir as mybir
from concourse.alu_op_type import AluOpType as ALU
from contextlib import ExitStack

F32 = mybir.dt.float32
BF16 = mybir.dt.bfloat16
ACT = mybir.ActivationFunctionType
X_AXIS = mybir.AxisListType.X

B, T, D = 32, 128, 128
H0, DK = 8, 128
NF = 192
NR = 2 * T - 1
CTX = 256
HX, DX = 8, 16
LAYERS, HL, DL = 6, 16, 64
WINDOW = 32
INNER = HL * DL
FF = int(D * 4 * 2 / 3)
G = 4
UNITS = B * HL // G
QUAD = 4
QUADS = B // QUAD
NQ = QUAD * T
FF_CHUNKS = [(0, 128), (128, 128), (256, FF - 256)]
OUT_CHUNKS = INNER // 128
EPS = 1e-5
MASKED = -1e30
SCORE_SCALE0 = DK ** -0.5
SCORE_SCALEX = DX ** -0.5
QK_SCALE = 8.0


def positional_features():
    f = np.float32
    dist = np.arange(-T + 1, T, dtype=f)
    n = NF // 6
    absd = np.abs(dist)[:, None]
    half_life = f(2.0) ** np.linspace(3.0, math.log(T) / math.log(2.0), n, dtype=f)
    feat_exp = np.exp(f(-math.log(2.0)) / half_life[None, :] * absd)
    widths = f(2.0) ** np.arange(1, n + 1, dtype=f) - f(1.0)
    feat_cm = (widths[None, :] > absd).astype(f)
    stddev = T / (2.0 * n)
    mean = np.linspace(T / n, float(T), n, dtype=f)[None, :]
    conc = (mean / f(stddev)) ** 2
    rate = mean / f(stddev ** 2)
    logs = np.log(np.where(absd > 0, absd, f(1.0))).astype(f)
    log_unnorm = np.where(absd > 0, (conc - f(1.0)) * logs, f(-np.inf)) - rate * absd
    lgam = np.array([[math.lgamma(float(c)) for c in conc[0]]], dtype=f)
    log_norm = lgam - conc * np.log(rate)
    probs = np.exp((log_unnorm - log_norm).astype(f)) + f(1e-8)
    feat_gamma = probs / probs.max(axis=-1, keepdims=True)
    emb = np.concatenate([feat_exp, feat_cm, feat_gamma], axis=-1)
    emb = np.concatenate([emb, np.sign(dist)[:, None] * emb], axis=-1)
    return np.ascontiguousarray(emb.T.astype(f))


def rotary_tables():
    f = np.float32
    half = np.arange(0, DL, 2, dtype=f)
    inv_freq = f(1.0) / f(10000.0) ** (half / f(DL))
    t = np.arange(T, dtype=f)
    freqs = t[:, None] * inv_freq[None, :]
    freqs = np.concatenate([freqs, freqs], -1)
    base = (half + f(0.4 * DL)) / f(1.4 * DL)
    power = (t - f(T // 2)) / f(WINDOW // 2)
    scale = base[None, :] ** power[:, None]
    scale = np.concatenate([scale, scale], -1)
    cos, sin = np.cos(freqs), np.sin(freqs)
    sign = np.concatenate([np.ones(DL // 2, f), -np.ones(DL // 2, f)])[None, :]
    q = f(QK_SCALE) * scale
    k = f(1.0) / scale
    return np.ascontiguousarray(np.stack([cos * q, cos * k, sin * q * sign, sin * k * sign], 1).astype(f))


def band_mask():
    i, j = np.arange(T)[:, None], np.arange(T)[None, :]
    return np.where((j <= i) & (j >= i - WINDOW), 0.0, MASKED).astype(np.float32)


def head_rows():
    return (np.arange(D)[:, None] // DX == np.arange(HX)[None, :]).astype(np.float32)


CONSTANTS = {
    "pos_feats": positional_features, "rotary": rotary_tables, "band": band_mask, "head_rows": head_rows,
    "eye": lambda: np.eye(128, dtype=np.float32),
}


def pipeline(eng, units, period, max_skew, emit, peeled=1, peeled_last=0):
    bodies = units // period
    for i in range(peeled):
        for k in range(period):
            emit(k, i, lambda d, i=i, k=k: 0 <= i * period + k - d < units)
    with eng.Fori(peeled, bodies - peeled_last) as i:
        for k in range(period):
            emit(k, i, lambda d: True)
    for i in range(bodies - peeled_last, bodies):
        for k in range(period):
            emit(k, i, lambda d, i=i, k=k: i * period + k - d < units)
    for k in range(max_skew):
        emit(k, bodies, lambda d, k=k: k - d < 0)


def reused(first, k, d, depth):
    return not (isinstance(first, int) and first + k - d < depth)


def build(nc, x, ctx_in, mask, w_qs, w_ks, w_vs, w_rel, emb_bias, pos_bias, w_out0, b_out0,
          W_src, b_src, W_tgt, b_tgt, W_outx, b_outx,
          Wqkv, q_scale, k_scale, Wo, ln_g, ln_b, W1, b1, W2, b2,
          pos_feats, rotary, band, head_rows_in, eye, out):
    ctx = ExitStack()
    with ctx:
        def sb(name, shape, dt=F32):
            return ctx.enter_context(nc.sbuf_tensor(name, shape, dt))

        def pb(name):
            return ctx.enter_context(nc.psum_tensor(name, [128, 512], F32))

        def sem(name):
            return ctx.enter_context(nc.semaphore(name))

        ident = sb("ident", [128, 128])
        ident_bf = sb("ident_bf", [128, 128], BF16)
        band_f = sb("band_f", [128, T])
        band_bf = sb("band_bf", [128, 2, T], BF16)
        mean_w = sb("mean_w", [128, 128])
        neg_half = sb("neg_half", [128, 2 * G])
        x_all = sb("x_all", [128, B, D])
        zT = sb("zT", [128, B, T])

        banks = [pb(f"bank{i}") for i in range(6)]
        bank_pair = ctx.enter_context(nc.psum_tensor("bank_pair", [128, 2, 512], F32))
        banks += [bank_pair[:, 0, :], bank_pair[:, 1, :]]
        pos_scratch = nc.dram_tensor("pos_scratch", [2, T * H0 * NR + NR], F32, kind="Internal").ap()

        loaded_w0 = sem("loaded_w0")
        loaded_x = sem("loaded_x")
        const_set = sem("const_set")
        half_set = sem("half_set")
        const_cast = sem("const_cast")
        setup_pe = sem("setup_pe")
        setup_ev = sem("setup_ev")
        setup_cp = sem("setup_cp")

        passed = {id(e): sem(f"passed_{n}") for n, e in (("dve", nc.vector), ("pool", nc.gpsimd), ("sp", nc.sync))}

        def wait_apart(eng, semaphore, value):
            eng.wait_ge(semaphore, value)
            eng.sem_inc(passed[id(eng)], 1)

        part1 = ExitStack()

        def sb1(name, shape, dt=F32):
            return part1.enter_context(nc.sbuf_tensor(name, shape, dt))

        A_w = sb1("A_w", [128, H0, 128])
        C_w = sb1("C_w", [128, H0, NR])
        M_w = sb1("M_w", [128, H0, 128])
        u_b = sb1("u_b", [128, H0])
        pos_c = sb1("pos_c", [128, H0, NR])
        srcT = sb1("srcT", [128, 2, 2 * D])
        tgtT = sb1("tgtT", [128, D])
        outxT = sb1("outxT", [128, 2, D])
        btgt = sb1("btgt", [128, 1])
        bk = sb1("bk", [128, 1])
        bv_row = sb1("bv_row", [128, D])
        bo0_row = sb1("bo0_row", [128, D])
        box_row = sb1("box_row", [128, D])
        heads = sb1("heads", [128, HX])
        mrow = sb1("mrow", [128, B, T])
        mcol = sb1("mcol", [128, B])

        setup = ExitStack()

        def sbs(name, shape, dt=F32):
            return setup.enter_context(nc.sbuf_tensor(name, shape, dt))

        wq_raw = sbs("wq_raw", [128, H0 * DK])
        wk_raw = sbs("wk_raw", [128, H0 * DK])
        wv_raw = sbs("wv_raw", [128, H0 * DK])
        wo_raw = sbs("wo_raw", [128, H0, D])
        rel_a = sbs("rel_a", [128, H0 * DK])
        rel_b = sbs("rel_b", [NF - 128, H0 * DK])
        feat_a = sbs("feat_a", [128, NR])
        feat_b = sbs("feat_b", [NF - 128, NR])
        eb = sbs("eb", [128, H0])
        pbias = sbs("pbias", [128, H0])
        src_raw = sbs("src_raw", [128, 2, CTX])
        tgt_raw = sbs("tgt_raw", [128, D])
        outx_raw = sbs("outx_raw", [128, 2 * D])
        mask_raw = sbs("mask_raw", [B, T])
        wT = sbs("wT", [128, 3, 128])
        relT = sbs("relT", [128, NR])
        pb_rep = sbs("pb_rep", [128, 128])

        W0_LOADS = [
            (wq_raw[:, :], w_qs), (wk_raw[:, :], w_ks), (wv_raw[:, :], w_vs),
            (wo_raw[:, :, :], w_out0.rearrange("(h e) d -> e h d", h=H0)),
            (rel_a[:, :], w_rel[0:128, :]), (rel_b[:, :], w_rel[128:NF, :]),
            (feat_a[:, :], pos_feats[0:128, :]), (feat_b[:, :], pos_feats[128:NF, :]),
            (eb[:, :], emb_bias.rearrange("a h b d -> d (a h b)")),
            (pbias[:, :], pos_bias.rearrange("a h b d -> d (a h b)")),
            (src_raw[:, :, :], W_src.rearrange("(c p) n -> p c n", p=128)),
            (tgt_raw[:, :], W_tgt), (outx_raw[:, :], W_outx), (mask_raw[:, :], mask),
            (btgt[:, :], b_tgt.rearrange("(p a) -> p a", a=1)),
            (bk[:, :], b_src[0:D].rearrange("(p a) -> p a", a=1)),
            (bv_row[:, :], b_src[D:2 * D].partition_broadcast(128)),
            (bo0_row[:, :], b_out0.partition_broadcast(128)),
            (box_row[:, :], b_outx.partition_broadcast(128)),
            (heads[:, :], head_rows_in),
            (mrow[:, :, :], mask.partition_broadcast(128)),
            (ident[:, :], eye), (band_f[:, :], band),
        ]

        def setup_tensor(pe):
            n = [0]

            def group(*mms):
                if n[0] >= 2:
                    pe.wait_ge(setup_ev, n[0] - 1)
                for out_ap, lhsT, rhs, start, stop, tr in mms:
                    last = nc.tensor.matmul(out_ap, lhsT, rhs, start=start, stop=stop, is_transpose=tr)
                last.then_inc(setup_pe, 1)
                n[0] += 1

            pe.wait_ge(loaded_w0, 16 * len(W0_LOADS))
            pe.wait_ge(const_set, 1)
            for h in range(H0):
                bank = banks[n[0] % 2]
                group(*[(bank[:, 128 * j:128 * j + 128], w[:, h * DK:(h + 1) * DK], ident[:, :], True, True, True)
                        for j, w in enumerate((wq_raw, wk_raw, wv_raw))])
                bank = banks[n[0] % 2]
                group((bank[:, 0:NR], rel_a[:, h * DK:(h + 1) * DK], feat_a[:, :], True, False, None),
                      (bank[:, 0:NR], rel_b[:, h * DK:(h + 1) * DK], feat_b[:, :], False, True, None))
                pe.wait_ge(setup_ev, n[0])
                pe.wait_ge(setup_cp, h + 1)
                bank = banks[n[0] % 2]
                group((bank[:, 0:128], wT[:, 0, :], wT[:, 1, :], True, True, None),
                      (bank[:, 128:256], wT[:, 2, :], wo_raw[:, h, :], True, True, None),
                      (bank[:, 256:257], wT[:, 1, :], eb[:, h:h + 1], True, True, None))
                bank = banks[n[0] % 2]
                group((bank[:, 0:NR], wT[:, 0, :], relT[:, :], True, True, None),
                      (bank[:, 256:256 + NR], pb_rep[:, :], relT[:, :], True, True, None))
            bank = banks[n[0] % 2]
            group(*[(bank[:, (2 * c + o) * 128:(2 * c + o) * 128 + 128], src_raw[:, o, c * 128:(c + 1) * 128],
                     ident[:, :], True, True, True) for c in range(2) for o in range(2)])
            bank = banks[n[0] % 2]
            group((bank[:, 0:128], tgt_raw[:, :], ident[:, :], True, True, True),
                  (bank[:, 128:256], outx_raw[:, 0:128], ident[:, :], True, True, True),
                  (bank[:, 256:384], outx_raw[:, 128:256], ident[:, :], True, True, True),
                  (bank[:, 384:384 + B], mask_raw[:, :], ident[0:B, 0:B], True, True, True))

        def setup_vector(dve):
            n = [0]

            def take(*copies):
                dve.wait_ge(setup_pe, n[0] + 1)
                for f in copies:
                    last = f()
                last.then_inc(setup_ev, 1)
                n[0] += 1

            dve.wait_ge(loaded_w0, 16 * len(W0_LOADS))
            nc.vector.tensor_copy(ident_bf[:, :], ident[:, :]).then_inc(const_cast, 1)
            nc.vector.tensor_copy(band_bf[:, :, :], band_f[:, :].unsqueeze(1).to_broadcast([128, 2, T])).then_inc(const_cast, 1)
            for h in range(H0):
                bank = banks[n[0] % 2]
                take(lambda: nc.vector.tensor_copy(wT[:, :, :], bank[:, 0:384].rearrange("p (j n) -> p j n", j=3)))
                bank = banks[n[0] % 2]
                take(lambda: nc.vector.tensor_copy(relT[:, :], bank[:, 0:NR]))
                if h:
                    dve.wait_ge(setup_pe, 4 * h)
                nc.vector.tensor_copy(pb_rep[:, :], pbias[:, h:h + 1].to_broadcast([128, 128])).then_inc(setup_cp, 1)
                bank = banks[n[0] % 2]
                take(lambda: nc.vector.tensor_scalar(A_w[:, h, :], bank[:, 0:128], SCORE_SCALE0, None, ALU.mult),
                     lambda: nc.vector.tensor_copy(M_w[:, h, :], bank[:, 128:256]),
                     lambda: nc.vector.tensor_copy(u_b[:, h:h + 1], bank[:, 256:257]))
                bank = banks[n[0] % 2]
                take(lambda: nc.vector.tensor_scalar(C_w[:, h, :], bank[:, 0:NR], SCORE_SCALE0, None, ALU.mult),
                     lambda: nc.vector.tensor_copy(pos_c[:, h, :], bank[:, 256:256 + NR]))
            bank = banks[n[0] % 2]
            take(lambda: nc.vector.tensor_copy(srcT[:, :, :], bank[:, :].rearrange("p (c n) -> p c n", c=2)))
            bank = banks[n[0] % 2]
            take(lambda: nc.vector.tensor_copy(tgtT[:, :], bank[:, 0:128]),
                 lambda: nc.vector.tensor_copy(outxT[:, :, :], bank[:, 128:384].rearrange("p (c n) -> p c n", c=2)),
                 lambda: nc.vector.tensor_copy(mcol[:, :], bank[:, 384:384 + B]))

        SETUP_RESULTS = 4 * H0 + 2
        setup.close()

        st1 = sb1("st1", [128, 2, 6])
        mv1 = sb1("mv1", [128, 2, 2])
        rs1 = sb1("rs1", [128, 2, 1])
        st2 = sb1("st2", [128, 2, 6])
        mv2 = sb1("mv2", [128, 2, 2])
        rs2 = sb1("rs2", [128, 2, 1])
        st3 = sb1("st3", [128, 2, 6])
        mv3 = sb1("mv3", [128, 2, 2])
        rs3 = sb1("rs3", [128, 2, 1])
        xh = sb1("xh", [128, 2, D])
        xhT = sb1("xhT", [128, 2, T])
        GT = sb1("GT", [128, 2, H0, T])
        pos_sb = sb1("pos_sb", [128, H0, NR])
        sc = sb1("sc", [128, 2, H0, T])
        Y = sb1("Y", [128, 2, H0, D])
        pT = sb1("pT", [128, H0, T])
        nmax = sb1("nmax", [128, 2, H0])
        rsum = sb1("rsum", [128, 2, H0])
        rinv = sb1("rinv", [128, 2, H0])
        xb = sb1("xb", [128, 2, D])
        x1 = sb1("x1", [128, 2, D])
        x1b = sb1("x1b", [128, 2, D])
        xh2 = sb1("xh2", [128, 2, D])
        xh2T = sb1("xh2T", [128, 2, T])
        ctx_sb = sb1("ctx_sb", [128, 2, CTX])
        ctxT = sb1("ctxT", [128, 2, T])
        kT = sb1("kT", [128, T])
        kexp = sb1("kexp", [128, HX, T])
        v2 = sb1("v2", [128, 2, HX, DX + 1])
        q2T = sb1("q2T", [128, T])
        madd = sb1("madd", [128, T])
        p2 = sb1("p2", [128, 2, HX, T])
        p2T = sb1("p2T", [128, HX, T])
        nmax2 = sb1("nmax2", [128, 2, HX])
        r2 = sb1("r2", [128, HX])
        upd = sb1("upd", [128, D])
        updT = sb1("updT", [128, T])
        zh = sb1("zh", [128, D])

        S1 = {n: sem("a_" + n) for n in (
            "stats1 mean1 shift1 rstd1 xh xhT_mm xhT G_mm G pos_mm pos pos_stored shifted_in S_mm summed nmax exp psum rinv pn "
            "pT_mm pT Y_mm Y o_mm xb x1 x1b stats2 mean2 shift2 rstd2 xh2 xh2T_mm xh2T ctx_in ctxT_mm ctxT K_mm KV_mm kv kT v2b v2 kexp q2_mm max2 q2T "
            "madd S2_mm summed2 nmax2 exp2 p2T_mm p2T o2_mm r2 upd updT_mm updT out2_mm x2 stats3 mean3 shift3 rstd3 zh zT_mm zT").split()}

        YB = [banks[0], banks[1]]
        W0 = [banks[2], banks[3]]
        POS_PS = YB + W0
        W1b = [banks[4], banks[5]]
        SMALL_T = banks[6][:, 0:128]
        CTX_T = banks[6][:, 128:384]
        KQ_PS = banks[6][:, 384:512]
        V_PS = banks[7][:, 0:128]
        O_PS = banks[7][:, 128:256]
        O2_PS = banks[0][:, 0:HX * (DX + 1)]
        HALF = H0 // 2

        def part1_sync(sp):
            def emit(k, i, on):
                first = 2 * i
                u0 = first + k
                if on(0):
                    if reused(first, k, 0, 2):
                        wait_apart(sp, S1["ctxT_mm"], u0 - 1)
                    sp.dma_start(ctx_sb[:, k % 2, :], ctx_in[bass.ds(u0, 1)].rearrange("a t c -> t (a c)")).then_inc(S1["ctx_in"], 16)
                    wait_apart(sp, S1["pos"], 4 * u0 + 4)
                    if reused(first, k, 0, 2):
                        wait_apart(sp, S1["shifted_in"], 16 * (u0 - 1))
                    sp.dma_start(pos_scratch[k % 2, 0:T * H0 * NR].rearrange("(t n) -> t n", t=T),
                                 pos_sb[:, :, :].rearrange("p h n -> p (h n)")).then_inc(S1["pos_stored"], 16)
                    wait_apart(sp, S1["pos_stored"], 16 * (u0 + 1))
                    if reused(first, k, 0, 2):
                        sp.wait_ge(S1["pT_mm"], u0 - 1)
                    sp.dma_start(sc[:, k % 2, :, :], shifted_view(k % 2)).then_inc(S1["shifted_in"], 16)
            pipeline(sp, B, 2, 0, emit, peeled=2)

        def shifted_view(slot):
            v = pos_scratch[slot, T - 1:T]
            return bass.AP(v.tensor, v.offset, [[H0 * NR - 1, T], [NR, H0], [1, T]])

        def part1_tensor(pe):
            def emit(k, i, on):
                first = 2 * i
                u0, u1, u2, u3 = first + k, first + k - 1, first + k - 2, first + k - 3
                i0, i1, i2 = k % 2, (k - 1) % 2, k % 2
                if on(0):
                    pe.wait_ge(S1["xh"], u0 + 1)
                    if reused(first, k, 0, 2):
                        pe.wait_ge(S1["q2T"], u0 - 1)
                    elif reused(first, k, 0, 1):
                        pe.wait_ge(S1["xhT"], u0)
                    nc.tensor.transpose(SMALL_T, xh[:, i0, :], ident[:, :]).then_inc(S1["xhT_mm"], 1)
                if on(1):
                    pe.wait_ge(S1["ctx_in"], 16 * (u1 + 1))
                    if on(0):
                        pe.wait_ge(S1["xhT"], u0 + 1)
                    else:
                        pe.wait_ge(S1["q2T"], u1)
                    for c in range(2):
                        last = nc.tensor.transpose(CTX_T[:, c * 128:c * 128 + 128], ctx_sb[:, i1, c * 128:c * 128 + 128], ident[:, :])
                    last.then_inc(S1["ctxT_mm"], 1)
                if on(0):
                    pe.wait_ge(S1["xhT"], u0 + 1)
                    if reused(first, k, 0, 1):
                        pe.wait_ge(S1["Y"], u0)
                    for pr in range(4):
                        if pr == 2 and reused(first, k, 0, 1):
                            pe.wait_ge(S1["summed"], u0)
                        nc.tensor.matmul(POS_PS[pr][:, 0:2 * NR], xhT[:, i0, :], C_w[:, 2 * pr:2 * pr + 2, :].rearrange("p h n -> p (h n)"),
                                         start=True, stop=True).then_inc(S1["pos_mm"], 1)
                if on(3):
                    pe.wait_ge(S1["zh"], u3 + 1)
                    if on(1):
                        pe.wait_ge(S1["ctxT"], u1 + 1)
                    elif on(2):
                        pe.wait_ge(S1["q2T"], u1)
                    else:
                        pe.wait_ge(S1["updT"], u2)
                    nc.tensor.transpose(SMALL_T, zh[:, :], ident[:, :]).then_inc(S1["zT_mm"], 1)
                if on(0):
                    for h in range(H0):
                        if h % HALF == 0:
                            pe.wait_ge(S1["pos"], 4 * u0 + 3 + h // HALF)
                        last = nc.tensor.matmul(W0[h // HALF][:, h % HALF * 128:h % HALF * 128 + 128], A_w[:, h, :], xhT[:, i0, :], start=True, stop=True)
                    last.then_inc(S1["G_mm"], 1)
                if on(1):
                    pe.wait_ge(S1["ctxT"], u1 + 1)
                    if on(3):
                        pe.wait_ge(S1["zT"], u3 + 1)
                    for c in range(2):
                        last = nc.tensor.matmul(KQ_PS, srcT[:, c, 0:D], ctxT[:, c, :], start=(c == 0), stop=(c == 1))
                    last.then_inc(S1["K_mm"], 1)
                    if on(3):
                        pe.wait_ge(S1["x2"], u1 - 1)
                    elif on(2):
                        pe.wait_ge(S1["x1"], u1)
                    for c in range(2):
                        last = nc.tensor.matmul(V_PS, ctxT[:, c, :], srcT[:, c, D:2 * D], start=(c == 0), stop=(c == 1))
                    last.then_inc(S1["KV_mm"], 1)
                if on(2):
                    pe.wait_ge(S1["exp2"], u2 + 1)
                    pe.wait_ge(S1["summed2"], u2 + 1)
                    for h in range(HX):
                        last = nc.tensor.transpose(W1b[h // HALF][:, h % HALF * 128:h % HALF * 128 + 128], p2[:, i2, h, :], ident[:, :])
                    last.then_inc(S1["p2T_mm"], 1)
                if on(0):
                    pe.wait_ge(S1["G"], u0 + 1)
                    for h in range(H0):
                        last = nc.tensor.matmul(W0[h // HALF][:, h % HALF * 128:h % HALF * 128 + 128], GT[:, i0, h, :], xhT[:, i0, :], start=True, stop=True)
                    last.then_inc(S1["S_mm"], 1)
                if on(1):
                    pe.wait_ge(S1["pn"], u1 + 1)
                    if on(2):
                        pe.wait_ge(S1["p2T"], u2 + 1)
                    for h in range(H0):
                        last = nc.tensor.transpose(W1b[h // HALF][:, h % HALF * 128:h % HALF * 128 + 128], sc[:, i1, h, :], ident[:, :])
                    last.then_inc(S1["pT_mm"], 1)
                if on(2):
                    pe.wait_ge(S1["p2T"], u2 + 1)
                    if on(0):
                        pe.wait_ge(S1["pos"], 4 * u0 + 4)
                    elif on(1):
                        pe.wait_ge(S1["Y"], u1 + 1)
                    else:
                        pe.wait_ge(S1["upd"], u2)
                    for h in range(HX):
                        last = nc.tensor.matmul(O2_PS[:, h * (DX + 1):(h + 1) * (DX + 1)], p2T[:, h, :], v2[:, i2, h, :], start=True, stop=True)
                    last.then_inc(S1["o2_mm"], 1)
                if on(1):
                    pe.wait_ge(S1["pT"], u1 + 1)
                    pe.wait_ge(S1["v2b"], u1 + 1)
                    for h in range(H0):
                        last = nc.tensor.matmul(O_PS, pT[:, h, :], Y[:, i1, h, :], start=(h == 0), stop=(h == H0 - 1))
                    last.then_inc(S1["o_mm"], 1)
                if on(2):
                    pe.wait_ge(S1["upd"], u2 + 1)
                    if on(1):
                        pe.wait_ge(S1["kv"], u1 + 1)
                    else:
                        pe.wait_ge(S1["zT"], u3 + 1)
                    nc.tensor.transpose(SMALL_T, upd[:, :], ident[:, :]).then_inc(S1["updT_mm"], 1)
                if on(0):
                    if on(2):
                        pe.wait_ge(S1["upd"], u2 + 1)
                    pe.wait_ge(S1["pos"], 4 * u0 + 4)
                    for j in range(2):
                        last = nc.tensor.matmul(YB[j][:, :], xhT[:, i0, :], M_w[:, HALF * j:HALF * (j + 1), :].rearrange("p h n -> p (h n)"), start=True, stop=True)
                    last.then_inc(S1["Y_mm"], 1)
                if on(1):
                    pe.wait_ge(S1["xh2"], u1 + 1)
                    pe.wait_ge(S1["kv"], u1 + 1)
                    if on(2):
                        pe.wait_ge(S1["updT"], u2 + 1)
                    nc.tensor.transpose(SMALL_T, xh2[:, i1, :], ident[:, :]).then_inc(S1["xh2T_mm"], 1)
                if on(2):
                    pe.wait_ge(S1["updT"], u2 + 1)
                    if on(1):
                        pe.wait_ge(S1["x1"], u1 + 1)
                    else:
                        pe.wait_ge(S1["x2"], u2)
                    nc.tensor.matmul(O_PS, xh2T[:, i2, :], outxT[:, 0, :], start=True, stop=False)
                    nc.tensor.matmul(O_PS, updT[:, :], outxT[:, 1, :], start=False, stop=True).then_inc(S1["out2_mm"], 1)
                if on(1):
                    pe.wait_ge(S1["xh2T"], u1 + 1)
                    nc.tensor.matmul(KQ_PS, tgtT[:, :], xh2T[:, i1, :], start=True, stop=True).then_inc(S1["q2_mm"], 1)
                    pe.wait_ge(S1["q2T"], u1 + 1)
                    pe.wait_ge(S1["kexp"], u1 + 1)
                    pe.wait_ge(S1["pT"], u1 + 1)
                    for j in range(2):
                        last = nc.tensor.matmul(W1b[j][:, :], q2T[:, :], kexp[:, HALF * j:HALF * (j + 1), :].rearrange("p h n -> p (h n)"), start=True, stop=True)
                    last.then_inc(S1["S2_mm"], 1)
            pipeline(pe, B, 2, 3, emit, peeled=2)

        def part1_scalar(act):
            def emit(k, i, on):
                first = 2 * i
                u0, u1, u2, u3 = first + k, first + k - 1, first + k - 2, first + k - 3
                i0, i1, i2 = k % 2, (k - 1) % 2, k % 2
                if on(0):
                    act.wait_ge(S1["xhT_mm"], u0 + 1)
                    if reused(first, k, 0, 2):
                        act.wait_ge(S1["Y_mm"], u0 - 1)
                    nc.scalar.activation(xhT[:, i0, :], SMALL_T, ACT.Copy).then_inc(S1["xhT"], 1)
                if on(1):
                    act.wait_ge(S1["ctxT_mm"], u1 + 1)
                    if reused(first, k, 1, 1):
                        act.wait_ge(S1["KV_mm"], u1)
                    nc.scalar.activation(ctxT[:, :, :].rearrange("p c n -> p (c n)"), CTX_T, ACT.Copy).then_inc(S1["ctxT"], 1)
                    act.wait_ge(S1["nmax"], u1 + 1)
                    if reused(first, k, 1, 2):
                        act.wait_ge(S1["rinv"], u1 - 1)
                    for h in range(H0):
                        last = nc.scalar.activation(sc[:, i1, h, :], sc[:, i1, h, :], ACT.Exp, bias=nmax[:, i1, h:h + 1], scale=1.0,
                                                    accum_out=rsum[:, i1, h:h + 1])
                    last.then_inc(S1["exp"], 1)
                if on(3):
                    act.wait_ge(S1["zT_mm"], u3 + 1)
                    nc.scalar.activation(zT[:, bass.ds(u3, 1), :].rearrange("p a n -> p (a n)"), SMALL_T, ACT.Copy).then_inc(S1["zT"], 1)
                if on(2):
                    act.wait_ge(S1["nmax2"], u2 + 1)
                    for h in range(HX):
                        last = nc.scalar.activation(p2[:, i2, h, :], p2[:, i2, h, :], ACT.Exp, bias=nmax2[:, i2, h:h + 1], scale=SCORE_SCALEX)
                    last.then_inc(S1["exp2"], 1)
                    act.wait_ge(S1["p2T_mm"], u2 + 1)
                    if reused(first, k, 2, 1):
                        act.wait_ge(S1["o2_mm"], u2)
                    for j in range(2):
                        last = nc.scalar.activation(p2T[:, HALF * j:HALF * (j + 1), :].rearrange("p h n -> p (h n)"), W1b[j][:, :], ACT.Copy)
                    last.then_inc(S1["p2T"], 1)
                if on(1):
                    act.wait_ge(S1["pT_mm"], u1 + 1)
                    if reused(first, k, 1, 1):
                        act.wait_ge(S1["o_mm"], u1)
                    for j in range(2):
                        last = nc.scalar.activation(pT[:, HALF * j:HALF * (j + 1), :].rearrange("p h n -> p (h n)"), W1b[j][:, :], ACT.Copy)
                    last.then_inc(S1["pT"], 1)
                if on(2):
                    act.wait_ge(S1["updT_mm"], u2 + 1)
                    if reused(first, k, 2, 1):
                        act.wait_ge(S1["out2_mm"], u2)
                    nc.scalar.activation(updT[:, :], SMALL_T, ACT.Copy).then_inc(S1["updT"], 1)
                if on(1):
                    act.wait_ge(S1["xh2T_mm"], u1 + 1)
                    if reused(first, k, 1, 2):
                        act.wait_ge(S1["out2_mm"], u1 - 1)
                    nc.scalar.activation(xh2T[:, i1, :], SMALL_T, ACT.Copy).then_inc(S1["xh2T"], 1)
                if on(0):
                    act.wait_ge(S1["Y_mm"], u0 + 1)
                    if reused(first, k, 0, 2):
                        act.wait_ge(S1["o_mm"], u0 - 1)
                    for j in range(2):
                        last = nc.scalar.activation(Y[:, i0, HALF * j:HALF * (j + 1), :].rearrange("p h n -> p (h n)"), YB[j][:, :], ACT.Copy)
                    last.then_inc(S1["Y"], 1)
            pipeline(act, B, 2, 3, emit, peeled=2)

        def part1_vector(dve):
            def batch(u):
                return bass.ds(u, 1)

            def norm_stats(src, st, mv, which, u):
                nc.vector.bn_stats(st, src).then_inc(S1["stats" + which], 1)
                wait_apart(dve, S1["stats" + which], u + 1)
                nc.vector.bn_aggr(mv, st).then_inc(S1["mean" + which], 1)

            def first_norm(u, j, again):
                xin = x_all[:, batch(u), :].rearrange("p a n -> p (a n)")
                norm_stats(xin, st1[:, j, :], mv1[:, j, :], "1", u)
                dve.wait_ge(S1["rstd1"], u + 1)
                if again:
                    dve.wait_ge(S1["xhT_mm"], u - 1)
                nc.vector.tensor_scalar(xh[:, j, :], xin, mv1[:, j, 0:1], rs1[:, j, :], ALU.subtract, ALU.mult).then_inc(S1["xh"], 1)

            def emit(k, i, on):
                first = 2 * i
                u0, u1, u2 = first + k, first + k - 1, first + k - 2
                i0, i1, i2 = k % 2, (k - 1) % 2, k % 2

                def pos_pair(pr):
                    dve.wait_ge(S1["pos_mm"], 4 * u0 + pr + 1)
                    nc.vector.tensor_tensor(pos_sb[:, 2 * pr:2 * pr + 2, :].rearrange("p h n -> p (h n)"), POS_PS[pr][:, 0:2 * NR],
                                            pos_c[:, 2 * pr:2 * pr + 2, :].rearrange("p h n -> p (h n)"), ALU.add).then_inc(S1["pos"], 1)

                def sum_scores(j):
                    part = sc[:, i0, HALF * j:HALF * (j + 1), :].rearrange("p h n -> p (h n)")
                    return nc.vector.tensor_tensor(part, W0[j][:, :], part, ALU.add)

                if on(2):
                    dve.wait_ge(S1["S2_mm"], u2 + 1)
                    dve.wait_ge(S1["madd"], u2 + 1)
                    if reused(first, k, 2, 2):
                        dve.wait_ge(S1["p2T_mm"], u2 - 1)
                    for j in range(2):
                        last = nc.vector.tensor_tensor(p2[:, i2, HALF * j:HALF * (j + 1), :], W1b[j][:, :].rearrange("p (h n) -> p h n", h=HALF),
                                                       madd[:, :].unsqueeze(1).to_broadcast([128, HALF, T]), ALU.add)
                    last.then_inc(S1["summed2"], 1)
                    dve.wait_ge(S1["summed2"], u2 + 1)
                    nc.vector.tensor_reduce(r2max[:, :], p2[:, i2, :, :], X_AXIS, ALU.max, negate=True).then_inc(S1["max2"], 1)
                    dve.wait_ge(S1["max2"], u2 + 1)
                    if reused(first, k, 2, 2):
                        dve.wait_ge(S1["exp2"], u2 - 1)
                    nc.vector.tensor_scalar(nmax2[:, i2, :], r2max[:, :], SCORE_SCALEX, None, ALU.mult).then_inc(S1["nmax2"], 1)
                if on(0):
                    if reused(first, k, 0, 1):
                        dve.wait_ge(S1["pos_stored"], 16 * u0)
                    for pr in range(3):
                        pos_pair(pr)
                if on(1):
                    dve.wait_ge(S1["exp"], u1 + 1)
                    if reused(first, k, 1, 2):
                        dve.wait_ge(S1["pn"], u1 - 1)
                    nc.vector.reciprocal(rinv[:, i1, :], rsum[:, i1, :]).then_inc(S1["rinv"], 1)
                if on(0):
                    pos_pair(3)
                    dve.wait_ge(S1["G_mm"], u0 + 1)
                    if reused(first, k, 0, 2):
                        dve.wait_ge(S1["S_mm"], u0 - 1)
                    for j in range(2):
                        last = nc.vector.tensor_tensor(GT[:, i0, HALF * j:HALF * (j + 1), :], W0[j][:, :].rearrange("p (h n) -> p h n", h=HALF),
                                                       u_b[:, HALF * j:HALF * (j + 1)].unsqueeze(2).to_broadcast([128, HALF, T]), ALU.add)
                    last.then_inc(S1["G"], 1)
                if on(1):
                    mr = mrow[:, batch(u1), :].rearrange("p a n -> p (a n)")
                    dve.wait_ge(S1["K_mm"], u1 + 1)
                    if reused(first, k, 1, 1):
                        dve.wait_ge(S1["kexp"], u1)
                    nc.vector.scalar_tensor_tensor(kT[:, :], KQ_PS, bk[:, :], mr, ALU.add, ALU.mult).then_inc(S1["kv"], 1)
                    if reused(first, k, 1, 2):
                        dve.wait_ge(S1["o2_mm"], u1 - 1)
                    vdst = v2[:, i1, :, 0:DX]
                    dve.wait_ge(S1["KV_mm"], u1 + 1)
                    nc.vector.tensor_tensor(vdst, V_PS.rearrange("p (h n) -> p h n", h=HX), bv_row[:, :].rearrange("p (h n) -> p h n", h=HX), ALU.add).then_inc(S1["v2b"], 1)
                    nc.vector.tensor_scalar(madd[:, :], mr, 0.0, MASKED, ALU.is_equal, ALU.mult).then_inc(S1["madd"], 1)
                    dve.wait_ge(S1["v2b"], u1 + 1)
                    nc.vector.tensor_scalar(vdst, vdst, mcol[:, batch(u1)], None, ALU.mult).then_inc(S1["v2"], 1)
                if on(-1):
                    first_norm(u0 + 1, (k + 1) % 2, reused(first, k, -1, 2))
                if on(2):
                    o2 = O2_PS.rearrange("p (h n) -> p h n", h=HX)
                    dve.wait_ge(S1["o2_mm"], u2 + 1)
                    nc.vector.reciprocal(r2[:, :], o2[:, :, DX]).then_inc(S1["r2"], 1)
                    dve.wait_ge(S1["r2"], u2 + 1)
                    if reused(first, k, 2, 1):
                        dve.wait_ge(S1["updT_mm"], u2)
                    nc.vector.tensor_tensor(upd[:, :].rearrange("p (h n) -> p h n", h=HX), o2[:, :, 0:DX],
                                            r2[:, :].unsqueeze(2).to_broadcast([128, HX, DX]), ALU.mult).then_inc(S1["upd"], 1)
                if on(1):
                    dve.wait_ge(S1["o_mm"], u1 + 1)
                    dve.wait_ge(S1["xb"], u1 + 1)
                    if reused(first, k, 1, 2):
                        dve.wait_ge(S1["x1b"], u1 - 1)
                    nc.vector.tensor_tensor(x1[:, i1, :], O_PS, xb[:, i1, :], ALU.add).then_inc(S1["x1"], 1)
                    wait_apart(dve, S1["x1"], u1 + 1)
                    norm_stats(x1[:, i1, :], st2[:, i1, :], mv2[:, i1, :], "2", u1)
                if on(0):
                    dve.wait_ge(S1["S_mm"], u0 + 1)
                    dve.wait_ge(S1["shifted_in"], 16 * (u0 + 1))
                    sum_scores(0)
                if on(1):
                    dve.wait_ge(S1["rstd2"], u1 + 1)
                    if reused(first, k, 1, 2):
                        dve.wait_ge(S1["xh2T_mm"], u1 - 1)
                    nc.vector.tensor_scalar(xh2[:, i1, :], x1[:, i1, :], mv2[:, i1, 0:1], rs2[:, i1, :], ALU.subtract, ALU.mult).then_inc(S1["xh2"], 1)
                if on(0):
                    sum_scores(1).then_inc(S1["summed"], 1)
                if on(1):
                    dve.wait_ge(S1["q2_mm"], u1 + 1)
                    if reused(first, k, 1, 1):
                        dve.wait_ge(S1["S2_mm"], u1)
                    nc.vector.scalar_tensor_tensor(q2T[:, :], KQ_PS, btgt[:, :], mr, ALU.add, ALU.mult).then_inc(S1["q2T"], 1)
                if on(2):
                    dve.wait_ge(S1["out2_mm"], u2 + 1)
                    dve.wait_ge(S1["x1b"], u2 + 1)
                    xout = x_all[:, batch(u2), :].rearrange("p a n -> p (a n)")
                    nc.vector.tensor_tensor(xout, O_PS, x1b[:, i2, :], ALU.add).then_inc(S1["x2"], 1)
                    wait_apart(dve, S1["x2"], u2 + 1)
                    norm_stats(xout, st3[:, i2, :], mv3[:, i2, :], "3", u2)
                if on(0):
                    dve.wait_ge(S1["summed"], u0 + 1)
                    nc.vector.tensor_reduce(nmax[:, i0, :], sc[:, i0, :, :], X_AXIS, ALU.max, negate=True).then_inc(S1["nmax"], 1)
                if on(2):
                    dve.wait_ge(S1["rstd3"], u2 + 1)
                    if reused(first, k, 2, 1):
                        dve.wait_ge(S1["zT_mm"], u2)
                    nc.vector.tensor_scalar(zh[:, :], xout, mv3[:, i2, 0:1], rs3[:, i2, :], ALU.subtract, ALU.mult).then_inc(S1["zh"], 1)
            first_norm(0, 0, False)
            pipeline(dve, B, 2, 2, emit, peeled=2, peeled_last=1)

        r2max = sb1("r2max", [128, HX])

        def part1_pool(pool):
            def rstd(mv, rs, which, u):
                wait_apart(pool, S1["mean" + which], u + 1)
                nc.gpsimd.tensor_scalar(rs, mv[:, 1:2], EPS, 0.0, ALU.add, ALU.add).then_inc(S1["shift" + which], 1)
                pool.wait_ge(S1["shift" + which], u + 1)
                nc.gpsimd.tensor_tensor(rs, rs, neg_half[:, 0:1], ALU.pow).then_inc(S1["rstd" + which], 1)

            def first_norm(u, j):
                rstd(mv1[:, j, :], rs1[:, j, :], "1", u)

            def emit(k, i, on):
                first = 2 * i
                u0, u1, u2 = first + k, first + k - 1, first + k - 2
                i1, i2 = (k - 1) % 2, k % 2
                if on(1):
                    pool.wait_ge(S1["rinv"], u1 + 1)
                    nc.gpsimd.tensor_tensor(sc[:, i1, :, :], sc[:, i1, :, :], rinv[:, i1, :].unsqueeze(2).to_broadcast([128, H0, T]), ALU.mult).then_inc(S1["pn"], 1)
                    nc.gpsimd.tensor_tensor(xb[:, i1, :], x_all[:, bass.ds(u1, 1), :].rearrange("p a n -> p (a n)"), bo0_row[:, :], ALU.add).then_inc(S1["xb"], 1)
                    pool.wait_ge(S1["kv"], u1 + 1)
                    if reused(first, k, 1, 1):
                        pool.wait_ge(S1["S2_mm"], u1)
                    nc.gpsimd.tensor_tensor(kexp[:, :, :], kT[:, :].unsqueeze(1).to_broadcast([128, HX, T]),
                                            heads[:, :].unsqueeze(2).to_broadcast([128, HX, T]), ALU.mult).then_inc(S1["kexp"], 1)
                if on(-1):
                    first_norm(u0 + 1, (k + 1) % 2)
                if on(1):
                    rstd(mv2[:, i1, :], rs2[:, i1, :], "2", u1)
                    nc.gpsimd.tensor_tensor(x1b[:, i1, :], x1[:, i1, :], box_row[:, :], ALU.add).then_inc(S1["x1b"], 1)
                if on(2):
                    rstd(mv3[:, i2, :], rs3[:, i2, :], "3", u2)
            first_norm(0, 0)
            pipeline(pool, B, 2, 2, emit, peeled=2, peeled_last=1)

        part1.close()

        wqkv = sb("wqkv", [128, 3, INNER])
        wo = sb("wo", [128, OUT_CHUNKS, D])
        w1 = sb("w1", [128, 2 * FF])
        w2 = sb("w2", [128, 3, D])
        vecs = sb("vecs", [128, 3])
        b1c = sb("b1c", [128, 2, 3])
        rot_base = sb("rot_base", [128, 4, DL])
        qk_scl = sb("qk_scl", [128, 2, DL])
        rot_tab = sb("rot_tab", [128, 4, DL])
        xs = sb("xs", [128, 2, T])
        sq = sb("sq", [128, 2, 2 * G, DL])
        ss = sb("ss", [128, 2, 2 * G])
        ssc = sb("ssc", [128, 2, 2 * G])
        rn = sb("rn", [128, 8, 2 * G])
        own = sb("own", [128, 4, 2 * G, DL])
        crossed = sb("crossed", [128, 4, 2 * G, DL])
        rot = sb("rot", [128, 4, 2 * G, DL])
        qkT = sb("qkT", [128, 2, 4, T])
        v_sb = sb("v_sb", [128, 8, G, DL + 1])
        nm = sb("nm", [128, 2, G // 2, 2])
        mx = sb("mx", [128, 2, 2, G // 2])
        p = sb("p", [128, 2, G, T])
        pTl = sb("pTl", [128, 2, G, T])
        ri = sb("ri", [128, 2, G])
        o_sb = sb("o_sb", [128, 2, G, DL])
        oT = sb("oT", [128, 8, 2 * T])
        xs4 = sb("xs4", [128, 2, QUAD, T])
        xc = sb("xc", [128, 2, NQ])
        xsq = sb("xsq", [128, 2, NQ])
        var_sb = sb("var_sb", [128, QUAD])
        rstd_rep = sb("rstd_rep", [128, QUAD, T])
        xn0 = sb("xn0", [128, NQ])
        xn = sb("xn", [128, 2, NQ])
        gel = sb("gel", [128, 2, NQ])
        uf = sb("uf", [128, 2, 3, NQ])
        zq = sb("zq", [128, 2, NQ])
        res = sb("res", [128, 2, QUAD, D])

        L = {n: sem("l_" + n) for n in (
            "w_attn w_ffn tab xs proj_qk proj square ssum clamp rn own_crossed rot0 rot v T1 qkT S mx nm exp T2 pT PV ri o OT oT WO res").split()}
        Fm = {n: sem("f_" + n) for n in (
            "xs4 mean_mm xc sq var_mm var rstd rstd_rep rstd_mm xn0 xn ga gelu u y_mm res").split()}
        O = {n: sem("o_" + n) for n in "copied T_mm added stored_even stored_odd".split()}
        O_stored = [O["stored_even"], O["stored_odd"]]
        zeroed = sem("zeroed")

        ATTN_LOADS, FFN_LOADS = 4, 10
        v_ps, pv_ps = banks[2][:, 0:G * DL], banks[2][:, 0:G * (DL + 1)]
        oT_ps, y_ps = banks[3][:, 0:2 * T], banks[3][:, 256:384]
        qkT_ps, pT_ps = banks[4], banks[5]
        s_ps = bank_pair[:, :, 0:2 * T]
        UB = HL // G

        def layers_sync(sp):
            def load(l):
                if not isinstance(l, int):
                    wait_apart(sp, L["proj"], l * UNITS)
                    wait_apart(sp, L["tab"], l)
                    wait_apart(sp, L["WO"], l * B)
                lay = bass.ds(l, 1)
                sp.dma_start(wqkv[:, :, :].rearrange("p a n -> p (a n)"), Wqkv[lay].rearrange("a p n -> p (a n)")).then_inc(L["w_attn"], 16)
                sp.dma_start(wo[:, :, :], Wo[lay].rearrange("a (c p) n -> p (a c) n", p=128)).then_inc(L["w_attn"], 16)
                sp.dma_start(qk_scl[:, 0, :], q_scale[lay].rearrange("a n -> (a n)").partition_broadcast(128)).then_inc(L["w_attn"], 16)
                sp.dma_start(qk_scl[:, 1, :], k_scale[lay].rearrange("a n -> (a n)").partition_broadcast(128)).then_inc(L["w_attn"], 16)
                if not isinstance(l, int):
                    wait_apart(sp, Fm["res"], l * QUADS)
                sp.dma_start(w1[:, :], W1[lay].rearrange("a p n -> p (a n)")).then_inc(L["w_ffn"], 16)
                sp.dma_start(w2[:, 0:2, :], W2[lay, 0:256].rearrange("a (c p) n -> p (a c) n", p=128)).then_inc(L["w_ffn"], 16)
                sp.dma_start(w2[0:FF - 256, 2, :], W2[lay, 256:FF].rearrange("a p n -> p (a n)")).then_inc(L["w_ffn"], 16)
                for j, v in enumerate((ln_g, ln_b, b2)):
                    sp.dma_start(vecs[:, j:j + 1], v[lay].rearrange("a p -> p a")).then_inc(L["w_ffn"], 16)
                for half in range(2):
                    sp.dma_start(b1c[:, half, 0:2], b1[lay, half * FF:half * FF + 256].rearrange("a (c p) -> p (a c)", p=128)).then_inc(L["w_ffn"], 16)
                    sp.dma_start(b1c[0:FF - 256, half, 2:3], b1[lay, half * FF + 256:(half + 1) * FF].rearrange("a p -> p a")).then_inc(L["w_ffn"], 16)

            load(0)
            with sp.Fori(1, LAYERS) as l:
                load(l)

        def attention_tensor(pe, l):
            U, NB = l * UNITS, l * B

            def emit(k, i, on):
                first = 8 * i

                def n(d):
                    return U + first + (k - d)
                if on(0):
                    bt = k // UB % 2
                    if k % UB == 0:
                        pe.wait_ge(L["xs"], NB + batch_of(i, k, 0) + 1)
                    if reused(first, k, 0, 2):
                        pe.wait_ge(L["own_crossed"], n(0) - 1)
                    g = k % UB
                    nc.tensor.matmul(banks[k % 2][:, :].rearrange("p (a n) -> p a n", a=2), xs[:, bt, :], wqkv[:, 0:2, g * G * DL:(g + 1) * G * DL],
                                     start=True, stop=True).then_inc(L["proj_qk"], 1)
                if on(3):
                    pe.wait_ge(L["rot"], n(3) + 1)
                    if reused(first, k, 3, 1):
                        pe.wait_ge(L["qkT"], n(3))
                    for c in range(4):
                        last = nc.tensor.transpose(qkT_ps[:, c * T:(c + 1) * T], rot[:, (k - 3) % 4, 2 * c:2 * c + 2, :].rearrange("p h n -> p (h n)"), ident[:, :])
                    last.then_inc(L["T1"], 1)
                if on(7):
                    pe.wait_ge(L["o"], n(7) + 1)
                    if reused(first, k, 7, 1):
                        pe.wait_ge(L["oT"], n(7))
                    if on(9) and (k - 9) % UB == UB - 1:
                        pe.wait_ge(L["res"], NB + batch_of(i, k, 9) + 1)
                    for c in range(2):
                        last = nc.tensor.transpose(oT_ps[:, c * T:(c + 1) * T], o_sb[:, (k - 7) % 2, 2 * c:2 * c + 2, :].rearrange("p h n -> p (h n)"), ident[:, :])
                    last.then_inc(L["OT"], 1)
                if on(0):
                    if on(7):
                        pe.wait_ge(L["o"], n(7) + 1)
                    elif reused(first, k, 0, 1):
                        pe.wait_ge(L["v"], n(0))
                    nc.tensor.matmul(v_ps, xs[:, bt, :], wqkv[:, 2, g * G * DL:(g + 1) * G * DL], start=True, stop=True).then_inc(L["proj"], 1)
                if on(4):
                    j = (k - 4) % 2
                    pe.wait_ge(L["qkT"], n(4) + 1)
                    if reused(first, k, 4, 1):
                        pe.wait_ge(L["exp"], n(4))
                    for odd in range(2):
                        nc.tensor.matmul(s_ps[:, odd, :], ident_bf[:, :], band_bf[:, :, :].rearrange("p h n -> p (h n)"), start=True, stop=False, skip_group_check=True)
                    for h in range(G):
                        r = slice(h % 2 * DL, h % 2 * DL + DL)
                        last = nc.tensor.matmul(s_ps[:, h % 2, h // 2 * T:(h // 2 + 1) * T], qkT[r, j, h // 2, :], qkT[r, j, 2 + h // 2, :], start=False, stop=(h // 2 == 1), skip_group_check=True)
                    last.then_inc(L["S"], 1)
                if on(5):
                    pe.wait_ge(L["exp"], n(5) + 1)
                    if reused(first, k, 5, 1):
                        pe.wait_ge(L["pT"], n(5))
                    for h in range(G):
                        last = nc.tensor.transpose(pT_ps[:, h * T:(h + 1) * T], p[:, (k - 5) % 2, h, :], ident[:, :])
                    last.then_inc(L["T2"], 1)
                if on(6):
                    pe.wait_ge(L["pT"], n(6) + 1)
                    if on(0):
                        pe.wait_ge(L["v"], n(0) + 1)
                    else:
                        pe.wait_ge(L["o"], n(6))
                    for h in range(G):
                        last = nc.tensor.matmul(pv_ps[:, h * (DL + 1):(h + 1) * (DL + 1)], pTl[:, (k - 6) % 2, h, :], v_sb[:, (k - 6) % 8, h, :], start=True, stop=True)
                    last.then_inc(L["PV"], 1)
                if on(8) and (k - 8) % UB == UB - 1:
                    pe.wait_ge(L["oT"], n(8) + 1)
                    if on(7):
                        pe.wait_ge(L["oT"], n(7) + 1)
                    for c in range(OUT_CHUNKS):
                        slot = (k - 8 - (UB - 1) + c // 2) % 8
                        last = nc.tensor.matmul(y_ps, wo[:, c, :], oT[:, slot, c % 2 * T:(c % 2 + 1) * T], start=(c == 0), stop=(c == OUT_CHUNKS - 1))
                    last.then_inc(L["WO"], 1)
            pe.wait_ge(L["w_attn"], 16 * ATTN_LOADS * (l + 1))
            pipeline(pe, UNITS, 8, 8, emit, peeled=2)

        def batch_of(i, k, d):
            return 2 * i + (k - d) // UB

        def attention_scalar(act, l):
            U = l * UNITS

            def emit(k, i, on):
                first = 8 * i

                def n(d):
                    return U + first + (k - d)
                if on(3):
                    act.wait_ge(L["T1"], n(3) + 1)
                    if reused(first, k, 3, 2):
                        act.wait_ge(L["S"], n(3) - 1)
                    nc.scalar.activation(qkT[:, (k - 3) % 2, :, :].rearrange("p c n -> p (c n)"), qkT_ps[:, :], ACT.Copy).then_inc(L["qkT"], 1)
                if on(7):
                    act.wait_ge(L["OT"], n(7) + 1)
                    nc.scalar.activation(oT[:, (k - 7) % 8, :], oT_ps, ACT.Copy).then_inc(L["oT"], 1)
                if on(0):
                    act.wait_ge(L["proj_qk"], n(0) + 1)
                    if reused(first, k, 0, 2):
                        act.wait_ge(L["ssum"], n(0) - 1)
                    nc.scalar.activation(sq[:, k % 2, :, :].rearrange("p h n -> p (h n)"), banks[k % 2][:, :], ACT.Square).then_inc(L["square"], 1)
                if on(0):
                    act.wait_ge(L["proj"], n(0) + 1)
                    if reused(first, k, 0, 8):
                        act.wait_ge(L["PV"], n(0) - 7)
                    nc.scalar.activation(v_sb[:, k % 8, :, 0:DL], v_ps.rearrange("p (h n) -> p h n", h=G), ACT.Copy).then_inc(L["v"], 1)
                if on(4):
                    act.wait_ge(L["nm"], n(4) + 1)
                    if reused(first, k, 4, 2):
                        act.wait_ge(L["T2"], n(4) - 1)
                    for h in range(G):
                        last = nc.scalar.activation(p[:, (k - 4) % 2, h, :], s_ps[:, h % 2, h // 2 * T:(h // 2 + 1) * T], ACT.Exp,
                                                    bias=nm[:, (k - 4) % 2, h // 2, h % 2:h % 2 + 1], scale=rn[:, (k - 4) % 8, h:h + 1])
                    last.then_inc(L["exp"], 1)
            pipeline(act, UNITS, 8, 8, emit)

        def shift_copy(dst, src, width):
            nc.vector.tensor_copy(dst[0:64], src[0:64])
            return nc.vector.tensor_copy(dst[64:128, :, 1:T], src[64:128, :, 0:T - 1])

        def attention_vector(dve, l):
            U, NB = l * UNITS, l * B

            def shifted_batch(b, j):
                shift_copy(xs[:, j, :].unsqueeze(1), zT[:, bass.ds(b, 1), :], T).then_inc(L["xs"], 1)

            def emit(k, i, on):
                first = 8 * i

                def n(d):
                    return U + first + (k - d)
                if on(1):
                    j, j4 = (k - 1) % 2, (k - 1) % 4
                    dve.wait_ge(L["square"], n(1) + 1)
                    if reused(first, k, 1, 4):
                        dve.wait_ge(L["rot"], n(1) - 3)
                    qk = banks[j][:, :].rearrange("p (a h n) -> p a h n", a=2, h=G)
                    nc.vector.tensor_tensor(own[:, j4, :, :].rearrange("p (a h) n -> p a h n", a=2), qk,
                                            rot_tab[:, 0:2, :].unsqueeze(2).to_broadcast([128, 2, G, DL]), ALU.mult)
                    nc.vector.tensor_tensor(crossed[:, j4, :, :].rearrange("p (a h) n -> p a h n", a=2), qk,
                                            rot_tab[:, 2:4, :].unsqueeze(2).to_broadcast([128, 2, G, DL]), ALU.mult).then_inc(L["own_crossed"], 1)
                    if reused(first, k, 1, 2):
                        dve.wait_ge(L["clamp"], n(1) - 1)
                    nc.vector.tensor_reduce(ss[:, j, :], sq[:, j, :, :], X_AXIS, ALU.add).then_inc(L["ssum"], 1)
                if on(4):
                    j = (k - 4) % 2
                    dve.wait_ge(L["S"], n(4) + 1)
                    nc.vector.tensor_reduce(mx[:, j, :, :], s_ps.rearrange("p o (h n) -> p o h n", h=2), X_AXIS, ALU.max, negate=True).then_inc(L["mx"], 1)
                    dve.wait_ge(L["mx"], n(4) + 1)
                    if reused(first, k, 4, 2):
                        dve.wait_ge(L["exp"], n(4) - 1)
                    nc.vector.tensor_tensor(nm[:, j, :, :], mx[:, j, :, :].rearrange("p o h -> p h o"),
                                            rn[:, (k - 4) % 8, 0:G].rearrange("p (h o) -> p h o", o=2), ALU.mult).then_inc(L["nm"], 1)
                if on(5):
                    dve.wait_ge(L["T2"], n(5) + 1)
                    if reused(first, k, 5, 2):
                        dve.wait_ge(L["PV"], n(5) - 1)
                    nc.vector.tensor_copy(pTl[:, (k - 5) % 2, :, :].rearrange("p h n -> p (h n)"), pT_ps[:, :]).then_inc(L["pT"], 1)
                if on(6):
                    j = (k - 6) % 2
                    pv = pv_ps.rearrange("p (h n) -> p h n", h=G)
                    dve.wait_ge(L["PV"], n(6) + 1)
                    nc.vector.reciprocal(ri[:, j, :], pv[:, :, DL]).then_inc(L["ri"], 1)
                    dve.wait_ge(L["ri"], n(6) + 1)
                    if reused(first, k, 6, 2):
                        dve.wait_ge(L["OT"], n(6) - 1)
                    nc.vector.tensor_tensor(o_sb[:, j, :, :], pv[:, :, 0:DL], ri[:, j, :].unsqueeze(2).to_broadcast([128, G, DL]), ALU.mult).then_inc(L["o"], 1)
                if on(8) and (k - 8) % UB == UB - 1:
                    b = batch_of(i, k, 8)
                    dve.wait_ge(L["WO"], NB + b + 1)
                    zb = zT[:, bass.ds(b, 1), :].rearrange("p a n -> p (a n)")
                    nc.vector.tensor_tensor(zb, y_ps, zb, ALU.add).then_inc(L["res"], 1)
                if on(-2) and (k + 2) % UB == 0:
                    if reused(first, k, -2, 2 * UB):
                        dve.wait_ge(L["proj"], n(-2) - UB)
                    shifted_batch(batch_of(i, k, -2), (k + 2) // UB % 2)
            dve.wait_ge(L["w_attn"], 16 * ATTN_LOADS * (l + 1))
            for a in range(2):
                last = nc.vector.tensor_tensor(rot_tab[:, 2 * a:2 * a + 2, :], rot_base[:, 2 * a:2 * a + 2, :], qk_scl[:, :, :], ALU.mult)
            last.then_inc(L["tab"], 1)
            dve.wait_ge(L["tab"], l + 1)
            shifted_batch(0, 0)
            pipeline(dve, UNITS, 8, 8, emit, peeled_last=1)

        def attention_pool(pool, l):
            U = l * UNITS

            def emit(k, i, on):
                first = 8 * i
                def n(d):
                    return U + first + (k - d)
                j, j4 = k % 2, k % 4
                wait_apart(pool, L["ssum"], n(0) + 1)
                nc.gpsimd.tensor_scalar(ssc[:, j, :], ss[:, j, :], 1e-24, 0.0, ALU.max, ALU.add).then_inc(L["clamp"], 1)
                pool.wait_ge(L["clamp"], n(0) + 1)
                if reused(first, k, 0, 8):
                    pool.wait_ge(L["exp"], n(0) - 7)
                nc.gpsimd.tensor_tensor(rn[:, k % 8, :], ssc[:, j, :], neg_half[:, 0:2 * G], ALU.pow).then_inc(L["rn"], 1)
                pool.wait_ge(L["own_crossed"], n(0) + 1)
                if reused(first, k, 0, 4):
                    pool.wait_ge(L["T1"], n(0) - 3)
                hl = DL // 2
                nc.gpsimd.tensor_tensor(rot[:, j4, :, 0:hl], own[:, j4, :, 0:hl], crossed[:, j4, :, hl:DL], ALU.add)
                nc.gpsimd.tensor_tensor(rot[:, j4, :, hl:DL], own[:, j4, :, hl:DL], crossed[:, j4, :, 0:hl], ALU.add).then_inc(L["rot0"], 1)
                pool.wait_ge(L["rn"], n(0) + 1)
                pool.wait_ge(L["rot0"], n(0) + 1)
                nc.gpsimd.tensor_tensor(rot[:, j4, G:2 * G, :], rot[:, j4, G:2 * G, :],
                                        rn[:, k % 8, G:2 * G].unsqueeze(2).to_broadcast([128, G, DL]), ALU.mult).then_inc(L["rot"], 1)
            pipeline(pool, UNITS, 8, 0, emit)

        mean_ps, var_ps, yf_ps = banks[0], banks[1], banks[7]

        def ffn_tensor(pe, l):
            Q = l * QUADS

            def emit(k, i, on):
                first = 2 * i
                def n(d):
                    return Q + first + (k - d)

                def gate_value(c):
                    turn = 3 * n(2) + c
                    g_ps, a_ps = gate_banks(c, k)
                    c0, m = FF_CHUNKS[c]
                    if not (isinstance(first, int) and 3 * (first + k - 2) + c < 2):
                        pe.wait_ge(Fm["u"], turn - 1)
                    nc.tensor.matmul(g_ps[0:m, :], w1[:, FF + c0:FF + c0 + m], xn[:, k % 2, :], start=True, stop=True)
                    nc.tensor.matmul(a_ps[0:m, :], w1[:, c0:c0 + m], xn[:, k % 2, :], start=True, stop=True).then_inc(Fm["ga"], 1)

                if on(0):
                    pe.wait_ge(Fm["xs4"], n(0) + 1)
                    if reused(first, k, 0, 1):
                        pe.wait_ge(Fm["xc"], n(0))
                    nc.tensor.matmul(mean_ps[:, :], mean_w[:, :], xs4[:, k % 2, :, :].rearrange("p a n -> p (a n)"), start=True, stop=True).then_inc(Fm["mean_mm"], 1)
                if on(1):
                    pe.wait_ge(Fm["sq"], n(1) + 1)
                    if reused(first, k, 1, 1):
                        pe.wait_ge(Fm["xn0"], n(1))
                    for a in range(QUAD):
                        last = nc.tensor.matmul(var_ps[:, a:a + 1], xsq[:, (k - 1) % 2, a * T:(a + 1) * T], mean_w[:, 0:1], start=True, stop=True)
                    last.then_inc(Fm["var_mm"], 1)
                if on(2):
                    pe.wait_ge(Fm["xn"], n(2) + 1)
                    gate_value(0)
                    gate_value(1)
                if on(1):
                    pe.wait_ge(Fm["rstd_rep"], n(1) + 1)
                    for a in range(QUAD):
                        last = nc.tensor.matmul(var_ps[:, a * T:(a + 1) * T], rstd_rep[:, a, :], ident[:, :], start=True, stop=True)
                    last.then_inc(Fm["rstd_mm"], 1)
                if on(3):
                    if reused(first, k, 3, 1):
                        pe.wait_ge(Fm["res"], n(3))
                    pe.wait_ge(Fm["u"], 3 * n(3) + 3)
                    for c, (c0, m) in enumerate(FF_CHUNKS):
                        last = nc.tensor.matmul(yf_ps[:, :], w2[0:m, c, :], uf[0:m, (k - 3) % 2, c, :], start=(c == 0), stop=(c == 2))
                    last.then_inc(Fm["y_mm"], 1)
                if on(2):
                    gate_value(2)
            pe.wait_ge(L["w_ffn"], 16 * FFN_LOADS * (l + 1))
            pipeline(pe, QUADS, 2, 3, emit, peeled=2)

        def gate_banks(c, k):
            t = (3 * (k % 2) + c) % 2
            return banks[2 + 2 * t], banks[3 + 2 * t]

        def ffn_scalar(act, l):
            Q = l * QUADS

            def emit(k, i, on):
                first = 2 * i
                def n(d):
                    return Q + first + (k - d)
                if on(0):
                    act.wait_ge(Fm["xc"], n(0) + 1)
                    if reused(first, k, 0, 2):
                        act.wait_ge(Fm["var_mm"], n(0) - 1)
                    nc.scalar.activation(xsq[:, k % 2, :], xc[:, k % 2, :], ACT.Square).then_inc(Fm["sq"], 1)
                if on(2):
                    for c, (c0, m) in enumerate(FF_CHUNKS):
                        turn = 3 * n(2) + c
                        act.wait_ge(Fm["ga"], turn + 1)
                        g_ps, _ = gate_banks(c, k)
                        t = (3 * (k % 2) + c) % 2
                        if not (isinstance(first, int) and 3 * (first + k - 2) + c < 2):
                            act.wait_ge(Fm["u"], turn - 1)
                        nc.scalar.activation(gel[0:m, t, :], g_ps[0:m, :], ACT.Gelu, bias=b1c[0:m, 1, c:c + 1], scale=1.0).then_inc(Fm["gelu"], 1)
            act.wait_ge(L["w_ffn"], 16 * FFN_LOADS * (l + 1))
            pipeline(act, QUADS, 2, 3, emit, peeled=2)

        def ffn_vector(dve, l):
            Q = l * QUADS

            def emit(k, i, on):
                first = 2 * i
                def n(d):
                    return Q + first + (k - d)
                if on(0):
                    dve.wait_ge(Fm["mean_mm"], n(0) + 1)
                    dve.wait_ge(Fm["xs4"], n(0) + 1)
                    nc.vector.tensor_tensor(xc[:, k % 2, :], xs4[:, k % 2, :, :].rearrange("p a n -> p (a n)"), mean_ps[:, :], ALU.subtract).then_inc(Fm["xc"], 1)
                if on(1):
                    dve.wait_ge(Fm["var_mm"], n(1) + 1)
                    nc.vector.tensor_scalar(var_sb[:, :], var_ps[:, 0:QUAD], EPS, None, ALU.add).then_inc(Fm["var"], 1)
                if on(2):
                    value_chunk(k, first, n, 0)
                if on(1):
                    dve.wait_ge(Fm["rstd"], n(1) + 1)
                    nc.vector.tensor_copy(rstd_rep[:, :, :], var_sb[:, :].unsqueeze(2).to_broadcast([128, QUAD, T])).then_inc(Fm["rstd_rep"], 1)
                if on(2):
                    value_chunk(k, first, n, 1)
                if on(1):
                    dve.wait_ge(Fm["rstd_mm"], n(1) + 1)
                    nc.vector.tensor_tensor(xn0[:, :], xc[:, (k - 1) % 2, :], var_ps[:, :], ALU.mult).then_inc(Fm["xn0"], 1)
                    dve.wait_ge(Fm["xn0"], n(1) + 1)
                    nc.vector.tensor_scalar(xn[:, (k - 1) % 2, :], xn0[:, :], vecs[:, 0:1], vecs[:, 1:2], ALU.mult, ALU.add).then_inc(Fm["xn"], 1)
                if on(-1):
                    shifted_quad(first + k + 1, (k + 1) % 2)
                if on(3):
                    dve.wait_ge(Fm["y_mm"], n(3) + 1)
                    zb = zT[:, bass.ds((first + (k - 3)) * QUAD, QUAD), :].rearrange("p a n -> p (a n)")
                    nc.vector.scalar_tensor_tensor(zb, yf_ps[:, :], vecs[:, 2:3], zb, ALU.add, ALU.add).then_inc(Fm["res"], 1)
                if on(2):
                    value_chunk(k, first, n, 2)

            def shifted_quad(q, j):
                shift_copy(xs4[:, j, :, :], zT[:, bass.ds(q * QUAD, QUAD), :], NQ).then_inc(Fm["xs4"], 1)

            def value_chunk(k, first, n, c):
                c0, m = FF_CHUNKS[c]
                t = (3 * (k % 2) + c) % 2
                _, a_ps = gate_banks(c, k)
                dve.wait_ge(Fm["gelu"], 3 * n(2) + c + 1)
                nc.vector.scalar_tensor_tensor(uf[0:m, k % 2, c, :], a_ps[0:m, :], b1c[0:m, 0, c:c + 1], gel[0:m, t, :],
                                               ALU.add, ALU.mult).then_inc(Fm["u"], 1)

            dve.wait_ge(L["w_ffn"], 16 * FFN_LOADS * (l + 1))
            dve.wait_ge(L["res"], (l + 1) * B)
            shifted_quad(0, 0)
            pipeline(dve, QUADS, 2, 3, emit, peeled=2, peeled_last=1)
            dve.wait_ge(Fm["res"], (l + 1) * QUADS)

        def ffn_pool(pool, l):
            Q = l * QUADS

            def emit(k, i, on):
                first = 2 * i
                pool.wait_ge(Fm["var"], Q + first + k + 1)
                nc.gpsimd.tensor_tensor(var_sb[:, :], var_sb[:, :], neg_half[:, 0:QUAD], ALU.pow).then_inc(Fm["rstd"], 1)
            pipeline(pool, QUADS, 2, 0, emit, peeled=2)

        def final_scalar(act):
            def emit(k, i, on):
                first = 2 * i
                if reused(first, k, 0, 2):
                    act.wait_ge(O["T_mm"], first + k - 1)
                nc.scalar.activation(zq[:, k % 2, :], zT[:, bass.ds((first + k) * QUAD, QUAD), :].rearrange("p a n -> p (a n)"), ACT.Copy).then_inc(O["copied"], 1)
            act.wait_ge(Fm["res"], LAYERS * QUADS)
            pipeline(act, QUADS, 2, 0, emit, peeled=2)

        def final_tensor(pe):
            def emit(k, i, on):
                first = 2 * i
                pe.wait_ge(O["copied"], first + k + 1)
                if reused(first, k, 0, 2):
                    pe.wait_ge(O["added"], first + k - 1)
                for a in range(QUAD):
                    last = nc.tensor.transpose(banks[k % 2][:, a * 128:(a + 1) * 128], zq[:, k % 2, a * 128:(a + 1) * 128], ident[:, :])
                last.then_inc(O["T_mm"], 1)
            pipeline(pe, QUADS, 2, 0, emit, peeled=2)

        def final_vector(dve):
            def emit(k, i, on):
                first = 2 * i
                dve.wait_ge(O["T_mm"], first + k + 1)
                if reused(first, k, 0, 2):
                    dve.wait_ge(O_stored[k % 2], 16 * i)
                nc.vector.tensor_tensor(res[:, k % 2, :, :].rearrange("p a n -> p (a n)"), banks[k % 2][:, :],
                                        x_all[:, bass.ds((first + k) * QUAD, QUAD), :].rearrange("p a n -> p (a n)"), ALU.add).then_inc(O["added"], 1)
            pipeline(dve, QUADS, 2, 0, emit, peeled=2)

        def final_sync(sp):
            def emit(k, i, on):
                first = 2 * i
                wait_apart(sp, O["added"], first + k + 1)
                sp.dma_start(out[bass.ds((first + k) * QUAD, QUAD)].rearrange("b t d -> t b d"), res[:, k % 2, :, :]).then_inc(O_stored[k % 2], 16)
            pipeline(sp, QUADS, 2, 0, emit, peeled=2)
            for stored in O_stored:
                sp.wait_ge(stored, 16 * QUADS // 2)

        part1_done = sem("part1_done")
        ones_set = sem("ones_set")
        rot_in = sem("rot_in")

        ctx.enter_context(nc.allow_non_contiguous_dma(reason="small vectors laid out over partitions"))
        block = ctx.enter_context(nc.Block())

        @block.sync
        def _(sp):
            for dst, src in W0_LOADS:
                sp.dma_start(dst, src).then_inc(loaded_w0, 16)
            for c in range(4):
                sp.dma_start(x_all[:, c * 8:(c + 1) * 8, :], x[c * 8:(c + 1) * 8].rearrange("b t d -> t b d")).then_inc(loaded_x, 16)
            part1_sync(sp)
            sp.wait_ge(part1_done, 4)
            sp.dma_start(rot_base[:, :, :], rotary).then_inc(rot_in, 16)
            layers_sync(sp)
            final_sync(sp)

        @block.tensor
        def _(pe):
            setup_tensor(pe)
            pe.wait_ge(setup_ev, SETUP_RESULTS)
            part1_tensor(pe)
            pe.wait_ge(S1["zT"], B)
            nc.tensor.nop().then_inc(part1_done, 1)
            pe.wait_ge(const_cast, 2)
            with pe.Fori(0, LAYERS) as l:
                attention_tensor(pe, l)
                ffn_tensor(pe, l)
            final_tensor(pe)

        @block.vector
        def _(dve):
            nc.vector.memset(mean_w[:, :], 1.0 / D).then_inc(const_set, 1)
            setup_vector(dve)
            dve.wait_ge(setup_ev, SETUP_RESULTS)
            nc.vector.memset(v2[:, :, :, :], 1.0).then_inc(ones_set, 1)
            dve.wait_ge(ones_set, 1)
            dve.wait_ge(loaded_x, 64)
            part1_vector(dve)
            dve.wait_ge(S1["zT"], B)
            nc.vector.nop().then_inc(part1_done, 1)
            dve.wait_ge(part1_done, 4)
            nc.vector.memset(v_sb[:, :, :, :], 1.0).then_inc(ones_set, 1)
            nc.vector.memset(xs[64:128, :, 0:1], 0.0).then_inc(zeroed, 1)
            nc.vector.memset(xs4[64:128, :, :, 0:1], 0.0).then_inc(zeroed, 1)
            dve.wait_ge(ones_set, 2)
            dve.wait_ge(zeroed, 2)
            dve.wait_ge(rot_in, 16)
            with dve.Fori(0, LAYERS) as l:
                attention_vector(dve, l)
                ffn_vector(dve, l)
            final_vector(dve)

        @block.scalar
        def _(act):
            act.wait_ge(setup_ev, SETUP_RESULTS)
            part1_scalar(act)
            act.wait_ge(S1["zT"], B)
            nc.scalar.nop().then_inc(part1_done, 1)
            act.wait_ge(part1_done, 4)
            with act.Fori(0, LAYERS) as l:
                attention_scalar(act, l)
                ffn_scalar(act, l)
            final_scalar(act)

        @block.gpsimd
        def _(pool):
            nc.gpsimd.memset(neg_half[:, :], -0.5).then_inc(half_set, 1)
            pool.wait_ge(half_set, 1)
            pool.wait_ge(setup_ev, SETUP_RESULTS)
            pool.wait_ge(loaded_x, 64)
            part1_pool(pool)
            pool.wait_ge(S1["zT"], B)
            nc.gpsimd.nop().then_inc(part1_done, 1)
            pool.wait_ge(part1_done, 4)
            with pool.Fori(0, LAYERS) as l:
                attention_pool(pool, l)
                ffn_pool(pool, l)


_INS = ["x", "ctx_2048", "mask_BxS2_fk1", "L0_attn_w_qs", "L0_attn_w_ks", "L0_attn_w_vs", "L0_attn_w_rel_pos_k",
        "L0_attn_rel_embed_bias", "L0_attn_rel_pos_bias", "L0_attn_w_out", "L0_attn_b_out",
        "L0_xattn_W_src", "L0_xattn_b_src", "L0_xattn_W_tgt", "L0_xattn_b_tgt", "L0_xattn_W_out", "L0_xattn_b_out",
        "L0_ffn_Wqkv", "L0_ffn_q_scale", "L0_ffn_k_scale", "L0_ffn_Wo", "L0_ffn_ln_g", "L0_ffn_ln_b",
        "L0_ffn_W1", "L0_ffn_b1", "L0_ffn_W2", "L0_ffn_b2"]


def kernel(**inputs):
    import concourse.bacc as bacc
    from concourse.bass_utils import run_bass_kernel_spmd

    nc = bacc.Bacc("TRN2", target_bir_lowering=False, num_devices=1)
    arrays, args = {}, []
    given = [(n, np.ascontiguousarray(inputs[n])) for n in _INS] + [(n, make()) for n, make in CONSTANTS.items()]
    for name, a in given:
        arrays[f"in_{name}"] = a
        args.append(nc.dram_tensor(f"in_{name}", a.shape, mybir.dt.from_np(a.dtype), kind="ExternalInput").ap())
    args.append(nc.dram_tensor("out_0", (B, T, D), F32, kind="ExternalOutput").ap())
    build(nc, *args)
    r = run_bass_kernel_spmd(nc, [arrays], core_ids=[0])
    return r.results[0]["out_0"]
```

```python
import math

import numpy as np

import concourse.bass as bass
import concourse.mybir as mybir
from concourse.alu_op_type import AluOpType as ALU
from contextlib import ExitStack

F32 = mybir.dt.float32
BF16 = mybir.dt.bfloat16
F32R = mybir.dt.float32r
ACT = mybir.ActivationFunctionType
X_AXIS = mybir.AxisListType.X

B, T, D = 32, 128, 128
H0, DK = 8, 128
NF = 192
NR = 2 * T - 1
CTX = 256
HX, DX = 8, 16
LAYERS, HL, DL = 6, 16, 64
WINDOW = 32
INNER = HL * DL
FF = int(D * 4 * 2 / 3)
G = 4
UNITS = B * HL // G
QUAD = 4
QUADS = B // QUAD
NQ = QUAD * T
FF_CHUNKS = [(0, 128), (128, 128), (256, FF - 256)]
OUT_CHUNKS = INNER // 128
EPS = 1e-5
MASKED = -1e30
SCORE_SCALE0 = DK ** -0.5
SCORE_SCALEX = DX ** -0.5
QK_SCALE = 8.0


def positional_features():
    f = np.float32
    dist = np.arange(-T + 1, T, dtype=f)
    n = NF // 6
    absd = np.abs(dist)[:, None]
    half_life = f(2.0) ** np.linspace(3.0, math.log(T) / math.log(2.0), n, dtype=f)
    feat_exp = np.exp(f(-math.log(2.0)) / half_life[None, :] * absd)
    widths = f(2.0) ** np.arange(1, n + 1, dtype=f) - f(1.0)
    feat_cm = (widths[None, :] > absd).astype(f)
    stddev = T / (2.0 * n)
    mean = np.linspace(T / n, float(T), n, dtype=f)[None, :]
    conc = (mean / f(stddev)) ** 2
    rate = mean / f(stddev ** 2)
    logs = np.log(np.where(absd > 0, absd, f(1.0))).astype(f)
    log_unnorm = np.where(absd > 0, (conc - f(1.0)) * logs, f(-np.inf)) - rate * absd
    lgam = np.array([[math.lgamma(float(c)) for c in conc[0]]], dtype=f)
    log_norm = lgam - conc * np.log(rate)
    probs = np.exp((log_unnorm - log_norm).astype(f)) + f(1e-8)
    feat_gamma = probs / probs.max(axis=-1, keepdims=True)
    emb = np.concatenate([feat_exp, feat_cm, feat_gamma], axis=-1)
    emb = np.concatenate([emb, np.sign(dist)[:, None] * emb], axis=-1)
    return np.ascontiguousarray(emb.T.astype(f))


def rotary_tables():
    f = np.float32
    half = np.arange(0, DL, 2, dtype=f)
    inv_freq = f(1.0) / f(10000.0) ** (half / f(DL))
    t = np.arange(T, dtype=f)
    freqs = t[:, None] * inv_freq[None, :]
    freqs = np.concatenate([freqs, freqs], -1)
    base = (half + f(0.4 * DL)) / f(1.4 * DL)
    power = (t - f(T // 2)) / f(WINDOW // 2)
    scale = base[None, :] ** power[:, None]
    scale = np.concatenate([scale, scale], -1)
    cos, sin = np.cos(freqs), np.sin(freqs)
    sign = np.concatenate([np.ones(DL // 2, f), -np.ones(DL // 2, f)])[None, :]
    q = f(QK_SCALE) * scale
    k = f(1.0) / scale
    return np.ascontiguousarray(np.stack([cos * q, cos * k, sin * q * sign, sin * k * sign], 1).astype(f))


def band_mask():
    i, j = np.arange(T)[:, None], np.arange(T)[None, :]
    return np.where((j <= i) & (j >= i - WINDOW), 0.0, MASKED).astype(np.float32)


def head_rows():
    return (np.arange(D)[:, None] // DX == np.arange(HX)[None, :]).astype(np.float32)


CONSTANTS = {
    "pos_feats": positional_features, "rotary": rotary_tables, "band": band_mask, "head_rows": head_rows,
    "eye": lambda: np.eye(128, dtype=np.float32),
}


def pipeline(eng, units, period, max_skew, emit, peeled=1, peeled_last=0, done=0, beside=None):
    bodies = units // period
    for i in range(peeled):
        for k in range(max(0, done - i * period), period):
            emit(k, i, lambda d, i=i, k=k: 0 <= i * period + k - d < units)
    with eng.Fori(peeled, bodies - peeled_last) as i:
        for k in range(period):
            emit(k, i, lambda d: True)
    for i in range(bodies - peeled_last, bodies):
        for k in range(period):
            emit(k, i, lambda d, i=i, k=k: i * period + k - d < units)
    for k in range(max_skew):
        emit(k, bodies, lambda d, k=k: k - d < 0)
        if beside:
            beside(k)


def reused(first, k, d, depth):
    return not (isinstance(first, int) and first + k - d < depth)


def build(nc, x, ctx_in, mask, w_qs, w_ks, w_vs, w_rel, emb_bias, pos_bias, w_out0, b_out0,
          W_src, b_src, W_tgt, b_tgt, W_outx, b_outx,
          Wqkv, q_scale, k_scale, Wo, ln_g, ln_b, W1, b1, W2, b2,
          pos_feats, rotary, band, head_rows_in, eye, out):
    ctx = ExitStack()
    with ctx:
        def sb(name, shape, dt=F32):
            return ctx.enter_context(nc.sbuf_tensor(name, shape, dt))

        def pb(name):
            return ctx.enter_context(nc.psum_tensor(name, [128, 512], F32))

        def sem(name):
            return ctx.enter_context(nc.semaphore(name))

        ident = sb("ident", [128, 128])
        ident_bf = sb("ident_bf", [128, 128], BF16)
        band_f = sb("band_f", [128, T])
        band_bf = sb("band_bf", [128, 2, T], BF16)
        mean_w = sb("mean_w", [128, 128])
        neg_half = sb("neg_half", [128, 2 * G])
        x_all = sb("x_all", [128, B, D])
        zT = sb("zT", [128, B, T])

        wqkv_hi = sb("wqkv_hi", [128, 3, INNER], F32R)
        wqkv_lo = sb("wqkv_lo", [128, 3, INNER], F32R)
        wqkv = (wqkv_hi, wqkv_lo)
        wo = sb("wo", [128, OUT_CHUNKS, D])
        rot_base = sb("rot_base", [128, 4, DL])
        qk_scl = sb("qk_scl", [128, 2, DL])
        own_crossed = sb("own_crossed", [128, 2, 4, 2 * G, DL])
        own = own_crossed[:, 0]
        crossed = own_crossed[:, 1]
        wqkv_raw = own_crossed[:, :, :, :, :].rearrange("p a b h n -> p (a b h n)")[:, 0:3 * INNER]

        banks = [pb(f"bank{i}") for i in range(6)]
        bank_pair = ctx.enter_context(nc.psum_tensor("bank_pair", [128, 2, 512], F32))
        banks += [bank_pair[:, 0, :], bank_pair[:, 1, :]]
        pos_scratch = nc.dram_tensor("pos_scratch", [2, T * H0 * NR + NR], F32, kind="Internal").ap()

        loaded_w0 = sem("loaded_w0")
        loaded_x = sem("loaded_x")
        const_set = sem("const_set")
        half_set = sem("half_set")
        const_cast = sem("const_cast")
        setup_pe = sem("setup_pe")
        setup_ev = sem("setup_ev")
        setup_cp = sem("setup_cp")

        passed = {id(e): sem(f"passed_{n}") for n, e in (("dve", nc.vector), ("pool", nc.gpsimd), ("sp", nc.sync))}

        def wait_apart(eng, semaphore, value):
            eng.wait_ge(semaphore, value)
            eng.sem_inc(passed[id(eng)], 1)

        part1 = ExitStack()

        def sb1(name, shape, dt=F32):
            return part1.enter_context(nc.sbuf_tensor(name, shape, dt))

        A_w = sb1("A_w", [128, H0, 128])
        C_w = sb1("C_w", [128, H0, NR])
        M_w = sb1("M_w", [128, H0, 128])
        u_b = sb1("u_b", [128, H0])
        pos_c = sb1("pos_c", [128, H0, NR])
        srcT = sb1("srcT", [128, 2, 2 * D])
        tgtT = sb1("tgtT", [128, D])
        outxT = sb1("outxT", [128, 2, D])
        btgt = sb1("btgt", [128, 1])
        bk = sb1("bk", [128, 1])
        bv_row = sb1("bv_row", [128, D])
        bo0_row = sb1("bo0_row", [128, D])
        box_row = sb1("box_row", [128, D])
        heads = sb1("heads", [128, HX])
        mrow = sb1("mrow", [128, B, T])
        mcol = sb1("mcol", [128, B])

        setup = ExitStack()

        def sbs(name, shape, dt=F32):
            return setup.enter_context(nc.sbuf_tensor(name, shape, dt))

        wq_raw = sbs("wq_raw", [128, H0 * DK])
        wk_raw = sbs("wk_raw", [128, H0 * DK])
        wv_raw = sbs("wv_raw", [128, H0 * DK])
        wo_raw = sbs("wo_raw", [128, H0, D])
        rel_a = sbs("rel_a", [128, H0 * DK])
        rel_b = sbs("rel_b", [NF - 128, H0 * DK])
        feat_a = sbs("feat_a", [128, NR])
        feat_b = sbs("feat_b", [NF - 128, NR])
        eb = sbs("eb", [128, H0])
        pbias = sbs("pbias", [128, H0])
        src_raw = sbs("src_raw", [128, 2, CTX])
        tgt_raw = sbs("tgt_raw", [128, D])
        outx_raw = sbs("outx_raw", [128, 2 * D])
        mask_raw = sbs("mask_raw", [B, T])
        wT = sbs("wT", [128, 3, 128])
        relT = sbs("relT", [128, NR])
        pb_rep = sbs("pb_rep", [128, 128])

        W0_LOADS = [
            (wq_raw[:, :], w_qs), (wk_raw[:, :], w_ks), (wv_raw[:, :], w_vs),
            (wo_raw[:, :, :], w_out0.rearrange("(h e) d -> e h d", h=H0)),
            (rel_a[:, :], w_rel[0:128, :]), (rel_b[:, :], w_rel[128:NF, :]),
            (feat_a[:, :], pos_feats[0:128, :]), (feat_b[:, :], pos_feats[128:NF, :]),
            (eb[:, :], emb_bias.rearrange("a h b d -> d (a h b)")),
            (pbias[:, :], pos_bias.rearrange("a h b d -> d (a h b)")),
            (src_raw[:, :, :], W_src.rearrange("(c p) n -> p c n", p=128)),
            (tgt_raw[:, :], W_tgt), (outx_raw[:, :], W_outx), (mask_raw[:, :], mask),
            (btgt[:, :], b_tgt.rearrange("(p a) -> p a", a=1)),
            (bk[:, :], b_src[0:D].rearrange("(p a) -> p a", a=1)),
            (bv_row[:, :], b_src[D:2 * D].partition_broadcast(128)),
            (bo0_row[:, :], b_out0.partition_broadcast(128)),
            (box_row[:, :], b_outx.partition_broadcast(128)),
            (heads[:, :], head_rows_in),
            (mrow[:, :, :], mask.partition_broadcast(128)),
            (ident[:, :], eye), (band_f[:, :], band),
        ]

        def setup_tensor(pe):
            n = [0]

            def group(*mms):
                if n[0] >= 2:
                    pe.wait_ge(setup_ev, n[0] - 1)
                for out_ap, lhsT, rhs, start, stop, tr in mms:
                    last = nc.tensor.matmul(out_ap, lhsT, rhs, start=start, stop=stop, is_transpose=tr)
                last.then_inc(setup_pe, 1)
                n[0] += 1

            pe.wait_ge(loaded_w0, 16 * len(W0_LOADS))
            pe.wait_ge(const_set, 1)
            for h in range(H0):
                bank = banks[n[0] % 2]
                group(*[(bank[:, 128 * j:128 * j + 128], w[:, h * DK:(h + 1) * DK], ident[:, :], True, True, True)
                        for j, w in enumerate((wq_raw, wk_raw, wv_raw))])
                bank = banks[n[0] % 2]
                group((bank[:, 0:NR], rel_a[:, h * DK:(h + 1) * DK], feat_a[:, :], True, False, None),
                      (bank[:, 0:NR], rel_b[:, h * DK:(h + 1) * DK], feat_b[:, :], False, True, None))
                pe.wait_ge(setup_ev, n[0])
                pe.wait_ge(setup_cp, h + 1)
                bank = banks[n[0] % 2]
                group((bank[:, 0:128], wT[:, 0, :], wT[:, 1, :], True, True, None),
                      (bank[:, 128:256], wT[:, 2, :], wo_raw[:, h, :], True, True, None),
                      (bank[:, 256:257], wT[:, 1, :], eb[:, h:h + 1], True, True, None))
                bank = banks[n[0] % 2]
                group((bank[:, 0:NR], wT[:, 0, :], relT[:, :], True, True, None),
                      (bank[:, 256:256 + NR], pb_rep[:, :], relT[:, :], True, True, None))
            bank = banks[n[0] % 2]
            group(*[(bank[:, (2 * c + o) * 128:(2 * c + o) * 128 + 128], src_raw[:, o, c * 128:(c + 1) * 128],
                     ident[:, :], True, True, True) for c in range(2) for o in range(2)])
            bank = banks[n[0] % 2]
            group((bank[:, 0:128], tgt_raw[:, :], ident[:, :], True, True, True),
                  (bank[:, 128:256], outx_raw[:, 0:128], ident[:, :], True, True, True),
                  (bank[:, 256:384], outx_raw[:, 128:256], ident[:, :], True, True, True),
                  (bank[:, 384:384 + B], mask_raw[:, :], ident[0:B, 0:B], True, True, True))

        def setup_vector(dve):
            n = [0]

            def take(*copies):
                dve.wait_ge(setup_pe, n[0] + 1)
                for f in copies:
                    last = f()
                last.then_inc(setup_ev, 1)
                n[0] += 1

            dve.wait_ge(loaded_w0, 16 * len(W0_LOADS))
            nc.vector.tensor_copy(ident_bf[:, :], ident[:, :]).then_inc(const_cast, 1)
            nc.vector.tensor_copy(band_bf[:, :, :], band_f[:, :].unsqueeze(1).to_broadcast([128, 2, T])).then_inc(const_cast, 1)
            for h in range(H0):
                bank = banks[n[0] % 2]
                take(lambda: nc.vector.tensor_copy(wT[:, :, :], bank[:, 0:384].rearrange("p (j n) -> p j n", j=3)))
                bank = banks[n[0] % 2]
                take(lambda: nc.vector.tensor_copy(relT[:, :], bank[:, 0:NR]))
                if h:
                    dve.wait_ge(setup_pe, 4 * h)
                nc.vector.tensor_copy(pb_rep[:, :], pbias[:, h:h + 1].to_broadcast([128, 128])).then_inc(setup_cp, 1)
                bank = banks[n[0] % 2]
                take(lambda: nc.vector.tensor_scalar(A_w[:, h, :], bank[:, 0:128], SCORE_SCALE0, None, ALU.mult),
                     lambda: nc.vector.tensor_copy(M_w[:, h, :], bank[:, 128:256]),
                     lambda: nc.vector.tensor_copy(u_b[:, h:h + 1], bank[:, 256:257]))
                bank = banks[n[0] % 2]
                take(lambda: nc.vector.tensor_scalar(C_w[:, h, :], bank[:, 0:NR], SCORE_SCALE0, None, ALU.mult),
                     lambda: nc.vector.tensor_copy(pos_c[:, h, :], bank[:, 256:256 + NR]))
            bank = banks[n[0] % 2]
            take(lambda: nc.vector.tensor_copy(srcT[:, :, :], bank[:, :].rearrange("p (c n) -> p c n", c=2)))
            bank = banks[n[0] % 2]
            take(lambda: nc.vector.tensor_copy(tgtT[:, :], bank[:, 0:128]),
                 lambda: nc.vector.tensor_copy(outxT[:, :, :], bank[:, 128:384].rearrange("p (c n) -> p c n", c=2)),
                 lambda: nc.vector.tensor_copy(mcol[:, :], bank[:, 384:384 + B]))

        SETUP_RESULTS = 4 * H0 + 2
        setup.close()

        st1 = sb1("st1", [128, 2, 6])
        mv1 = sb1("mv1", [128, 2, 2])
        rs1 = sb1("rs1", [128, 2, 1])
        st2 = sb1("st2", [128, 2, 6])
        mv2 = sb1("mv2", [128, 2, 2])
        rs2 = sb1("rs2", [128, 2, 1])
        st3 = sb1("st3", [128, 2, 6])
        mv3 = sb1("mv3", [128, 2, 2])
        rs3 = sb1("rs3", [128, 2, 1])
        xh = sb1("xh", [128, 2, D])
        xhT = sb1("xhT", [128, 2, T])
        GT = sb1("GT", [128, 2, H0, T])
        pos_sb = sb1("pos_sb", [128, H0, NR])
        sc = sb1("sc", [128, 2, H0, T])
        Y = sb1("Y", [128, 2, H0, D])
        pT = sb1("pT", [128, H0, T])
        nmax = sb1("nmax", [128, 2, H0])
        rsum = sb1("rsum", [128, 2, H0])
        rinv = sb1("rinv", [128, 2, H0])
        xb = sb1("xb", [128, 2, D])
        x1 = sb1("x1", [128, 2, D])
        x1b = sb1("x1b", [128, 2, D])
        xh2 = sb1("xh2", [128, 2, D])
        xh2T = sb1("xh2T", [128, 2, T])
        ctx_sb = sb1("ctx_sb", [128, 2, CTX])
        ctxT = sb1("ctxT", [128, 2, T])
        kT = sb1("kT", [128, T])
        kexp = sb1("kexp", [128, HX, T])
        v2 = sb1("v2", [128, 2, HX, DX + 1])
        q2T = sb1("q2T", [128, T])
        madd = sb1("madd", [128, T])
        p2 = sb1("p2", [128, 2, HX, T])
        p2T = sb1("p2T", [128, HX, T])
        nmax2 = sb1("nmax2", [128, 2, HX])
        r2 = sb1("r2", [128, HX])
        upd = sb1("upd", [128, D])
        updT = sb1("updT", [128, T])
        zh = sb1("zh", [128, D])

        S1 = {n: sem("a_" + n) for n in (
            "stats1 mean1 shift1 rstd1 xh xhT_mm xhT G_mm G pos_mm pos pos_stored shifted_in S_mm summed nmax exp psum rinv pn "
            "pT_mm pT Y_mm Y o_mm xb x1 x1b stats2 mean2 shift2 rstd2 xh2 xh2T_mm xh2T ctx_in ctxT_mm ctxT K_mm KV_mm kv kT v2b v2 kexp q2_mm max2 q2T "
            "madd S2_mm summed2 nmax2 exp2 p2T_mm p2T o2_mm r2 upd updT_mm updT out2_mm x2 stats3 mean3 shift3 rstd3 zh zT_mm zT").split()}

        YB = [banks[0], banks[1]]
        W0 = [banks[2], banks[3]]
        POS_PS = YB + W0
        W1b = [banks[4], banks[5]]
        SMALL_T = banks[6][:, 0:128]
        CTX_T = banks[6][:, 128:384]
        KQ_PS = banks[6][:, 384:512]
        V_PS = banks[7][:, 0:128]
        O_PS = banks[7][:, 128:256]
        O2_PS = banks[0][:, 0:HX * (DX + 1)]
        HALF = H0 // 2

        def part1_sync(sp):
            def emit(k, i, on):
                first = 2 * i
                u0 = first + k
                if on(0):
                    if reused(first, k, 0, 2):
                        wait_apart(sp, S1["ctxT_mm"], u0 - 1)
                    sp.dma_start(ctx_sb[:, k % 2, :], ctx_in[bass.ds(u0, 1)].rearrange("a t c -> t (a c)")).then_inc(S1["ctx_in"], 16)
                    wait_apart(sp, S1["pos"], 4 * u0 + 4)
                    if reused(first, k, 0, 2):
                        wait_apart(sp, S1["shifted_in"], 16 * (u0 - 1))
                    sp.dma_start(pos_scratch[k % 2, 0:T * H0 * NR].rearrange("(t n) -> t n", t=T),
                                 pos_sb[:, :, :].rearrange("p h n -> p (h n)")).then_inc(S1["pos_stored"], 16)
                    wait_apart(sp, S1["pos_stored"], 16 * (u0 + 1))
                    if reused(first, k, 0, 2):
                        sp.wait_ge(S1["pT_mm"], u0 - 1)
                    sp.dma_start(sc[:, k % 2, :, :], shifted_view(k % 2)).then_inc(S1["shifted_in"], 16)
            pipeline(sp, B, 2, 0, emit, peeled=2)

        def shifted_view(slot):
            v = pos_scratch[slot, T - 1:T]
            return bass.AP(v.tensor, v.offset, [[H0 * NR - 1, T], [NR, H0], [1, T]])

        def part1_tensor(pe):
            def emit(k, i, on):
                first = 2 * i
                u0, u1, u2, u3 = first + k, first + k - 1, first + k - 2, first + k - 3
                i0, i1, i2 = k % 2, (k - 1) % 2, k % 2
                if on(0):
                    pe.wait_ge(S1["xh"], u0 + 1)
                    if reused(first, k, 0, 2):
                        pe.wait_ge(S1["q2T"], u0 - 1)
                    elif reused(first, k, 0, 1):
                        pe.wait_ge(S1["xhT"], u0)
                    nc.tensor.transpose(SMALL_T, xh[:, i0, :], ident[:, :]).then_inc(S1["xhT_mm"], 1)
                if on(1):
                    pe.wait_ge(S1["ctx_in"], 16 * (u1 + 1))
                    if on(0):
                        pe.wait_ge(S1["xhT"], u0 + 1)
                    else:
                        pe.wait_ge(S1["q2T"], u1)
                    for c in range(2):
                        last = nc.tensor.transpose(CTX_T[:, c * 128:c * 128 + 128], ctx_sb[:, i1, c * 128:c * 128 + 128], ident[:, :])
                    last.then_inc(S1["ctxT_mm"], 1)
                if on(0):
                    pe.wait_ge(S1["xhT"], u0 + 1)
                    if reused(first, k, 0, 1):
                        pe.wait_ge(S1["Y"], u0)
                    for pr in range(4):
                        if pr == 2 and reused(first, k, 0, 1):
                            pe.wait_ge(S1["summed"], u0)
                        nc.tensor.matmul(POS_PS[pr][:, 0:2 * NR], xhT[:, i0, :], C_w[:, 2 * pr:2 * pr + 2, :].rearrange("p h n -> p (h n)"),
                                         start=True, stop=True).then_inc(S1["pos_mm"], 1)
                if on(3):
                    pe.wait_ge(S1["zh"], u3 + 1)
                    if on(1):
                        pe.wait_ge(S1["ctxT"], u1 + 1)
                    elif on(2):
                        pe.wait_ge(S1["q2T"], u1)
                    else:
                        pe.wait_ge(S1["updT"], u2)
                    nc.tensor.transpose(SMALL_T, zh[:, :], ident[:, :]).then_inc(S1["zT_mm"], 1)
                if on(0):
                    for h in range(H0):
                        if h % HALF == 0:
                            pe.wait_ge(S1["pos"], 4 * u0 + 3 + h // HALF)
                        last = nc.tensor.matmul(W0[h // HALF][:, h % HALF * 128:h % HALF * 128 + 128], A_w[:, h, :], xhT[:, i0, :], start=True, stop=True)
                    last.then_inc(S1["G_mm"], 1)
                if on(1):
                    pe.wait_ge(S1["ctxT"], u1 + 1)
                    if on(3):
                        pe.wait_ge(S1["zT"], u3 + 1)
                    for c in range(2):
                        last = nc.tensor.matmul(KQ_PS, srcT[:, c, 0:D], ctxT[:, c, :], start=(c == 0), stop=(c == 1))
                    last.then_inc(S1["K_mm"], 1)
                    if on(3):
                        pe.wait_ge(S1["x2"], u1 - 1)
                    elif on(2):
                        pe.wait_ge(S1["x1"], u1)
                    for c in range(2):
                        last = nc.tensor.matmul(V_PS, ctxT[:, c, :], srcT[:, c, D:2 * D], start=(c == 0), stop=(c == 1))
                    last.then_inc(S1["KV_mm"], 1)
                if on(2):
                    pe.wait_ge(S1["exp2"], u2 + 1)
                    pe.wait_ge(S1["summed2"], u2 + 1)
                    for h in range(HX):
                        last = nc.tensor.transpose(W1b[h // HALF][:, h % HALF * 128:h % HALF * 128 + 128], p2[:, i2, h, :], ident[:, :])
                    last.then_inc(S1["p2T_mm"], 1)
                if on(0):
                    pe.wait_ge(S1["G"], u0 + 1)
                    for h in range(H0):
                        last = nc.tensor.matmul(W0[h // HALF][:, h % HALF * 128:h % HALF * 128 + 128], GT[:, i0, h, :], xhT[:, i0, :], start=True, stop=True)
                    last.then_inc(S1["S_mm"], 1)
                if on(1):
                    pe.wait_ge(S1["pn"], u1 + 1)
                    if on(2):
                        pe.wait_ge(S1["p2T"], u2 + 1)
                    for h in range(H0):
                        last = nc.tensor.transpose(W1b[h // HALF][:, h % HALF * 128:h % HALF * 128 + 128], sc[:, i1, h, :], ident[:, :])
                    last.then_inc(S1["pT_mm"], 1)
                if on(2):
                    pe.wait_ge(S1["p2T"], u2 + 1)
                    if on(0):
                        pe.wait_ge(S1["pos"], 4 * u0 + 4)
                    elif on(1):
                        pe.wait_ge(S1["Y"], u1 + 1)
                    else:
                        pe.wait_ge(S1["upd"], u2)
                    for h in range(HX):
                        last = nc.tensor.matmul(O2_PS[:, h * (DX + 1):(h + 1) * (DX + 1)], p2T[:, h, :], v2[:, i2, h, :], start=True, stop=True)
                    last.then_inc(S1["o2_mm"], 1)
                if on(1):
                    pe.wait_ge(S1["pT"], u1 + 1)
                    pe.wait_ge(S1["v2b"], u1 + 1)
                    for h in range(H0):
                        last = nc.tensor.matmul(O_PS, pT[:, h, :], Y[:, i1, h, :], start=(h == 0), stop=(h == H0 - 1))
                    last.then_inc(S1["o_mm"], 1)
                if on(2):
                    pe.wait_ge(S1["upd"], u2 + 1)
                    if on(1):
                        pe.wait_ge(S1["kv"], u1 + 1)
                    else:
                        pe.wait_ge(S1["zT"], u3 + 1)
                    nc.tensor.transpose(SMALL_T, upd[:, :], ident[:, :]).then_inc(S1["updT_mm"], 1)
                if on(0):
                    if on(2):
                        pe.wait_ge(S1["upd"], u2 + 1)
                    pe.wait_ge(S1["pos"], 4 * u0 + 4)
                    for j in range(2):
                        last = nc.tensor.matmul(YB[j][:, :], xhT[:, i0, :], M_w[:, HALF * j:HALF * (j + 1), :].rearrange("p h n -> p (h n)"), start=True, stop=True)
                    last.then_inc(S1["Y_mm"], 1)
                if on(1):
                    pe.wait_ge(S1["xh2"], u1 + 1)
                    pe.wait_ge(S1["kv"], u1 + 1)
                    if on(2):
                        pe.wait_ge(S1["updT"], u2 + 1)
                    nc.tensor.transpose(SMALL_T, xh2[:, i1, :], ident[:, :]).then_inc(S1["xh2T_mm"], 1)
                if on(2):
                    pe.wait_ge(S1["updT"], u2 + 1)
                    if on(1):
                        pe.wait_ge(S1["x1"], u1 + 1)
                    else:
                        pe.wait_ge(S1["x2"], u2)
                    nc.tensor.matmul(O_PS, xh2T[:, i2, :], outxT[:, 0, :], start=True, stop=False)
                    nc.tensor.matmul(O_PS, updT[:, :], outxT[:, 1, :], start=False, stop=True).then_inc(S1["out2_mm"], 1)
                if on(1):
                    pe.wait_ge(S1["xh2T"], u1 + 1)
                    nc.tensor.matmul(KQ_PS, tgtT[:, :], xh2T[:, i1, :], start=True, stop=True).then_inc(S1["q2_mm"], 1)
                    pe.wait_ge(S1["q2T"], u1 + 1)
                    pe.wait_ge(S1["kexp"], u1 + 1)
                    pe.wait_ge(S1["pT"], u1 + 1)
                    for j in range(2):
                        last = nc.tensor.matmul(W1b[j][:, :], q2T[:, :], kexp[:, HALF * j:HALF * (j + 1), :].rearrange("p h n -> p (h n)"), start=True, stop=True)
                    last.then_inc(S1["S2_mm"], 1)
            pipeline(pe, B, 2, 3, emit, peeled=2)

        def part1_scalar(act):
            def emit(k, i, on):
                first = 2 * i
                u0, u1, u2, u3 = first + k, first + k - 1, first + k - 2, first + k - 3
                i0, i1, i2 = k % 2, (k - 1) % 2, k % 2
                if on(0):
                    act.wait_ge(S1["xhT_mm"], u0 + 1)
                    if reused(first, k, 0, 2):
                        act.wait_ge(S1["Y_mm"], u0 - 1)
                    nc.scalar.activation(xhT[:, i0, :], SMALL_T, ACT.Copy).then_inc(S1["xhT"], 1)
                if on(1):
                    act.wait_ge(S1["ctxT_mm"], u1 + 1)
                    if reused(first, k, 1, 1):
                        act.wait_ge(S1["KV_mm"], u1)
                    nc.scalar.activation(ctxT[:, :, :].rearrange("p c n -> p (c n)"), CTX_T, ACT.Copy).then_inc(S1["ctxT"], 1)
                    act.wait_ge(S1["nmax"], u1 + 1)
                    if reused(first, k, 1, 2):
                        act.wait_ge(S1["rinv"], u1 - 1)
                    for h in range(H0):
                        last = nc.scalar.activation(sc[:, i1, h, :], sc[:, i1, h, :], ACT.Exp, bias=nmax[:, i1, h:h + 1], scale=1.0,
                                                    accum_out=rsum[:, i1, h:h + 1])
                    last.then_inc(S1["exp"], 1)
                if on(3):
                    act.wait_ge(S1["zT_mm"], u3 + 1)
                    nc.scalar.activation(zT[:, bass.ds(u3, 1), :].rearrange("p a n -> p (a n)"), SMALL_T, ACT.Copy).then_inc(S1["zT"], 1)
                if on(2):
                    act.wait_ge(S1["nmax2"], u2 + 1)
                    for h in range(HX):
                        last = nc.scalar.activation(p2[:, i2, h, :], p2[:, i2, h, :], ACT.Exp, bias=nmax2[:, i2, h:h + 1], scale=SCORE_SCALEX)
                    last.then_inc(S1["exp2"], 1)
                    act.wait_ge(S1["p2T_mm"], u2 + 1)
                    if reused(first, k, 2, 1):
                        act.wait_ge(S1["o2_mm"], u2)
                    for j in range(2):
                        last = nc.scalar.activation(p2T[:, HALF * j:HALF * (j + 1), :].rearrange("p h n -> p (h n)"), W1b[j][:, :], ACT.Copy)
                    last.then_inc(S1["p2T"], 1)
                if on(1):
                    act.wait_ge(S1["pT_mm"], u1 + 1)
                    if reused(first, k, 1, 1):
                        act.wait_ge(S1["o_mm"], u1)
                    for j in range(2):
                        last = nc.scalar.activation(pT[:, HALF * j:HALF * (j + 1), :].rearrange("p h n -> p (h n)"), W1b[j][:, :], ACT.Copy)
                    last.then_inc(S1["pT"], 1)
                if on(2):
                    act.wait_ge(S1["updT_mm"], u2 + 1)
                    if reused(first, k, 2, 1):
                        act.wait_ge(S1["out2_mm"], u2)
                    nc.scalar.activation(updT[:, :], SMALL_T, ACT.Copy).then_inc(S1["updT"], 1)
                if on(1):
                    act.wait_ge(S1["xh2T_mm"], u1 + 1)
                    if reused(first, k, 1, 2):
                        act.wait_ge(S1["out2_mm"], u1 - 1)
                    nc.scalar.activation(xh2T[:, i1, :], SMALL_T, ACT.Copy).then_inc(S1["xh2T"], 1)
                if on(0):
                    act.wait_ge(S1["Y_mm"], u0 + 1)
                    if reused(first, k, 0, 2):
                        act.wait_ge(S1["o_mm"], u0 - 1)
                    for j in range(2):
                        last = nc.scalar.activation(Y[:, i0, HALF * j:HALF * (j + 1), :].rearrange("p h n -> p (h n)"), YB[j][:, :], ACT.Copy)
                    last.then_inc(S1["Y"], 1)
            pipeline(act, B, 2, 3, emit, peeled=2)

        def part1_vector(dve):
            def batch(u):
                return bass.ds(u, 1)

            def norm_stats(src, st, mv, which, u):
                nc.vector.bn_stats(st, src).then_inc(S1["stats" + which], 1)
                wait_apart(dve, S1["stats" + which], u + 1)
                nc.vector.bn_aggr(mv, st).then_inc(S1["mean" + which], 1)

            def first_norm(u, j, again):
                xin = x_all[:, batch(u), :].rearrange("p a n -> p (a n)")
                norm_stats(xin, st1[:, j, :], mv1[:, j, :], "1", u)
                dve.wait_ge(S1["rstd1"], u + 1)
                if again:
                    dve.wait_ge(S1["xhT_mm"], u - 1)
                nc.vector.tensor_scalar(xh[:, j, :], xin, mv1[:, j, 0:1], rs1[:, j, :], ALU.subtract, ALU.mult).then_inc(S1["xh"], 1)

            def emit(k, i, on):
                first = 2 * i
                u0, u1, u2 = first + k, first + k - 1, first + k - 2
                i0, i1, i2 = k % 2, (k - 1) % 2, k % 2

                def pos_pair(pr):
                    dve.wait_ge(S1["pos_mm"], 4 * u0 + pr + 1)
                    nc.vector.tensor_tensor(pos_sb[:, 2 * pr:2 * pr + 2, :].rearrange("p h n -> p (h n)"), POS_PS[pr][:, 0:2 * NR],
                                            pos_c[:, 2 * pr:2 * pr + 2, :].rearrange("p h n -> p (h n)"), ALU.add).then_inc(S1["pos"], 1)

                def sum_scores(j):
                    part = sc[:, i0, HALF * j:HALF * (j + 1), :].rearrange("p h n -> p (h n)")
                    return nc.vector.tensor_tensor(part, W0[j][:, :], part, ALU.add)

                if on(2):
                    dve.wait_ge(S1["S2_mm"], u2 + 1)
                    dve.wait_ge(S1["madd"], u2 + 1)
                    if reused(first, k, 2, 2):
                        dve.wait_ge(S1["p2T_mm"], u2 - 1)
                    for j in range(2):
                        last = nc.vector.tensor_tensor(p2[:, i2, HALF * j:HALF * (j + 1), :], W1b[j][:, :].rearrange("p (h n) -> p h n", h=HALF),
                                                       madd[:, :].unsqueeze(1).to_broadcast([128, HALF, T]), ALU.add)
                    last.then_inc(S1["summed2"], 1)
                    dve.wait_ge(S1["summed2"], u2 + 1)
                    nc.vector.tensor_reduce(r2max[:, :], p2[:, i2, :, :], X_AXIS, ALU.max, negate=True).then_inc(S1["max2"], 1)
                    dve.wait_ge(S1["max2"], u2 + 1)
                    if reused(first, k, 2, 2):
                        dve.wait_ge(S1["exp2"], u2 - 1)
                    nc.vector.tensor_scalar(nmax2[:, i2, :], r2max[:, :], SCORE_SCALEX, None, ALU.mult).then_inc(S1["nmax2"], 1)
                if on(0):
                    if reused(first, k, 0, 1):
                        dve.wait_ge(S1["pos_stored"], 16 * u0)
                    for pr in range(3):
                        pos_pair(pr)
                if on(1):
                    dve.wait_ge(S1["exp"], u1 + 1)
                    if reused(first, k, 1, 2):
                        dve.wait_ge(S1["pn"], u1 - 1)
                    nc.vector.reciprocal(rinv[:, i1, :], rsum[:, i1, :]).then_inc(S1["rinv"], 1)
                if on(0):
                    pos_pair(3)
                    dve.wait_ge(S1["G_mm"], u0 + 1)
                    if reused(first, k, 0, 2):
                        dve.wait_ge(S1["S_mm"], u0 - 1)
                    for j in range(2):
                        last = nc.vector.tensor_tensor(GT[:, i0, HALF * j:HALF * (j + 1), :], W0[j][:, :].rearrange("p (h n) -> p h n", h=HALF),
                                                       u_b[:, HALF * j:HALF * (j + 1)].unsqueeze(2).to_broadcast([128, HALF, T]), ALU.add)
                    last.then_inc(S1["G"], 1)
                if on(1):
                    mr = mrow[:, batch(u1), :].rearrange("p a n -> p (a n)")
                    dve.wait_ge(S1["K_mm"], u1 + 1)
                    if reused(first, k, 1, 1):
                        dve.wait_ge(S1["kexp"], u1)
                    nc.vector.scalar_tensor_tensor(kT[:, :], KQ_PS, bk[:, :], mr, ALU.add, ALU.mult).then_inc(S1["kv"], 1)
                    if reused(first, k, 1, 2):
                        dve.wait_ge(S1["o2_mm"], u1 - 1)
                    vdst = v2[:, i1, :, 0:DX]
                    dve.wait_ge(S1["KV_mm"], u1 + 1)
                    nc.vector.tensor_tensor(vdst, V_PS.rearrange("p (h n) -> p h n", h=HX), bv_row[:, :].rearrange("p (h n) -> p h n", h=HX), ALU.add).then_inc(S1["v2b"], 1)
                    nc.vector.tensor_scalar(madd[:, :], mr, 0.0, MASKED, ALU.is_equal, ALU.mult).then_inc(S1["madd"], 1)
                    dve.wait_ge(S1["v2b"], u1 + 1)
                    nc.vector.tensor_scalar(vdst, vdst, mcol[:, batch(u1)], None, ALU.mult).then_inc(S1["v2"], 1)
                if on(-1):
                    first_norm(u0 + 1, (k + 1) % 2, reused(first, k, -1, 2))
                if on(2):
                    o2 = O2_PS.rearrange("p (h n) -> p h n", h=HX)
                    dve.wait_ge(S1["o2_mm"], u2 + 1)
                    nc.vector.reciprocal(r2[:, :], o2[:, :, DX]).then_inc(S1["r2"], 1)
                    dve.wait_ge(S1["r2"], u2 + 1)
                    if reused(first, k, 2, 1):
                        dve.wait_ge(S1["updT_mm"], u2)
                    nc.vector.tensor_tensor(upd[:, :].rearrange("p (h n) -> p h n", h=HX), o2[:, :, 0:DX],
                                            r2[:, :].unsqueeze(2).to_broadcast([128, HX, DX]), ALU.mult).then_inc(S1["upd"], 1)
                if on(1):
                    dve.wait_ge(S1["o_mm"], u1 + 1)
                    dve.wait_ge(S1["xb"], u1 + 1)
                    if reused(first, k, 1, 2):
                        dve.wait_ge(S1["x1b"], u1 - 1)
                    nc.vector.tensor_tensor(x1[:, i1, :], O_PS, xb[:, i1, :], ALU.add).then_inc(S1["x1"], 1)
                    wait_apart(dve, S1["x1"], u1 + 1)
                    norm_stats(x1[:, i1, :], st2[:, i1, :], mv2[:, i1, :], "2", u1)
                if on(0):
                    dve.wait_ge(S1["S_mm"], u0 + 1)
                    dve.wait_ge(S1["shifted_in"], 16 * (u0 + 1))
                    sum_scores(0)
                if on(1):
                    dve.wait_ge(S1["rstd2"], u1 + 1)
                    if reused(first, k, 1, 2):
                        dve.wait_ge(S1["xh2T_mm"], u1 - 1)
                    nc.vector.tensor_scalar(xh2[:, i1, :], x1[:, i1, :], mv2[:, i1, 0:1], rs2[:, i1, :], ALU.subtract, ALU.mult).then_inc(S1["xh2"], 1)
                if on(0):
                    sum_scores(1).then_inc(S1["summed"], 1)
                if on(1):
                    dve.wait_ge(S1["q2_mm"], u1 + 1)
                    if reused(first, k, 1, 1):
                        dve.wait_ge(S1["S2_mm"], u1)
                    nc.vector.scalar_tensor_tensor(q2T[:, :], KQ_PS, btgt[:, :], mr, ALU.add, ALU.mult).then_inc(S1["q2T"], 1)
                if on(2):
                    dve.wait_ge(S1["out2_mm"], u2 + 1)
                    dve.wait_ge(S1["x1b"], u2 + 1)
                    xout = x_all[:, batch(u2), :].rearrange("p a n -> p (a n)")
                    nc.vector.tensor_tensor(xout, O_PS, x1b[:, i2, :], ALU.add).then_inc(S1["x2"], 1)
                    wait_apart(dve, S1["x2"], u2 + 1)
                    norm_stats(xout, st3[:, i2, :], mv3[:, i2, :], "3", u2)
                if on(0):
                    dve.wait_ge(S1["summed"], u0 + 1)
                    nc.vector.tensor_reduce(nmax[:, i0, :], sc[:, i0, :, :], X_AXIS, ALU.max, negate=True).then_inc(S1["nmax"], 1)
                if on(2):
                    dve.wait_ge(S1["rstd3"], u2 + 1)
                    if reused(first, k, 2, 1):
                        dve.wait_ge(S1["zT_mm"], u2)
                    nc.vector.tensor_scalar(zh[:, :], xout, mv3[:, i2, 0:1], rs3[:, i2, :], ALU.subtract, ALU.mult).then_inc(S1["zh"], 1)
            first_norm(0, 0, False)
            pipeline(dve, B, 2, 2, emit, peeled=2, peeled_last=1)

        r2max = sb1("r2max", [128, HX])

        def part1_pool(pool):
            def rstd(mv, rs, which, u):
                wait_apart(pool, S1["mean" + which], u + 1)
                nc.gpsimd.tensor_scalar(rs, mv[:, 1:2], EPS, 0.0, ALU.add, ALU.add).then_inc(S1["shift" + which], 1)
                pool.wait_ge(S1["shift" + which], u + 1)
                nc.gpsimd.tensor_tensor(rs, rs, neg_half[:, 0:1], ALU.pow).then_inc(S1["rstd" + which], 1)

            def first_norm(u, j):
                rstd(mv1[:, j, :], rs1[:, j, :], "1", u)

            def emit(k, i, on):
                first = 2 * i
                u0, u1, u2 = first + k, first + k - 1, first + k - 2
                i1, i2 = (k - 1) % 2, k % 2
                if on(1):
                    pool.wait_ge(S1["rinv"], u1 + 1)
                    nc.gpsimd.tensor_tensor(sc[:, i1, :, :], sc[:, i1, :, :], rinv[:, i1, :].unsqueeze(2).to_broadcast([128, H0, T]), ALU.mult).then_inc(S1["pn"], 1)
                    nc.gpsimd.tensor_tensor(xb[:, i1, :], x_all[:, bass.ds(u1, 1), :].rearrange("p a n -> p (a n)"), bo0_row[:, :], ALU.add).then_inc(S1["xb"], 1)
                    pool.wait_ge(S1["kv"], u1 + 1)
                    if reused(first, k, 1, 1):
                        pool.wait_ge(S1["S2_mm"], u1)
                    nc.gpsimd.tensor_tensor(kexp[:, :, :], kT[:, :].unsqueeze(1).to_broadcast([128, HX, T]),
                                            heads[:, :].unsqueeze(2).to_broadcast([128, HX, T]), ALU.mult).then_inc(S1["kexp"], 1)
                if on(-1):
                    first_norm(u0 + 1, (k + 1) % 2)
                if on(1):
                    rstd(mv2[:, i1, :], rs2[:, i1, :], "2", u1)
                    nc.gpsimd.tensor_tensor(x1b[:, i1, :], x1[:, i1, :], box_row[:, :], ALU.add).then_inc(S1["x1b"], 1)
                if on(2):
                    rstd(mv3[:, i2, :], rs3[:, i2, :], "3", u2)
            first_norm(0, 0)
            pipeline(pool, B, 2, 2, emit, peeled=2, peeled_last=1)

        part1.close()

        w1_raw = sb("w1_raw", [128, 2 * FF])
        w1_hi = sb("w1_hi", [128, 2 * FF], F32R)
        w1_lo = sb("w1_lo", [128, 2 * FF], F32R)
        w1 = (w1_hi, w1_lo)
        w2 = sb("w2", [128, 3, D])
        vecs = sb("vecs", [128, 3])
        b1c = sb("b1c", [128, 2, 3])
        rot_tab = sb("rot_tab", [128, 4, DL])
        xs_hi = sb("xs_hi", [128, 2, T], F32R)
        xs_lo = sb("xs_lo", [128, 2, T], F32R)
        xs = (xs_hi, xs_lo)
        sq = sb("sq", [128, 2, 2 * G, DL])
        ss = sb("ss", [128, 2, 2 * G])
        ssc = sb("ssc", [128, 2, 2 * G])
        rn = sb("rn", [128, 8, 2 * G])
        rot = sb("rot", [128, 4, 2 * G, DL])
        qkT = sb("qkT", [128, 2, 4, T])
        v_sb = sb("v_sb", [128, 8, G, DL + 1])
        nm = sb("nm", [128, 2, G // 2, 2])
        mx = sb("mx", [128, 2, 2, G // 2])
        p = sb("p", [128, 2, G, T])
        pTl = sb("pTl", [128, 2, G, T])
        ri = sb("ri", [128, 2, G])
        o_sb = sb("o_sb", [128, 2, G, DL])
        oT = sb("oT", [128, 8, 2 * T])
        xs4 = sb("xs4", [128, 2, QUAD, T])
        xc = sb("xc", [128, 2, NQ])
        xsq = sb("xsq", [128, 2, NQ])
        var_sb = sb("var_sb", [128, QUAD])
        rstd_rep = sb("rstd_rep", [128, QUAD, T])
        xn0 = sb("xn0", [128, NQ])
        xn_f = sb("xn_f", [128, NQ])
        xn_hi = sb("xn_hi", [128, 2, NQ], F32R)
        xn_lo = sb("xn_lo", [128, 2, NQ], F32R)
        xn = (xn_hi, xn_lo)
        gel = sb("gel", [128, 2, NQ])
        uf = sb("uf", [128, 2, 3, NQ])
        zq = sb("zq", [128, 2, NQ])
        res = sb("res", [128, 2, QUAD, D])

        L = {n: sem("l_" + n) for n in (
            "w_attn w_ffn wqkv_hi wqkv_split w1_hi w1_split tab xs_hi xs proj_qk proj square ssum clamp rn own_crossed rot0 rot v T1 qkT S mx nm exp T2 pT PV ri o OT oT WO res").split()}
        Fm = {n: sem("f_" + n) for n in (
            "xs4 mean_mm xc sq var_mm var rstd rstd_rep rstd_mm xn0 xn_f xn_hi xn ga gelu u y_mm res").split()}
        O = {n: sem("o_" + n) for n in "copied T_mm added stored_even stored_odd".split()}
        O_stored = [O["stored_even"], O["stored_odd"]]
        zeroed = sem("zeroed")

        ATTN_LOADS, FFN_LOADS = 4, 10
        v_ps, pv_ps = banks[2][:, 0:G * DL], banks[2][:, 0:G * (DL + 1)]
        oT_ps, y_ps = banks[3][:, 0:2 * T], banks[3][:, 256:384]
        qkT_ps, pT_ps = banks[4], banks[5]
        s_ps = bank_pair[:, :, 0:2 * T]
        UB = HL // G

        def layer_loads(sp):
            def load_attention(l):
                if not isinstance(l, int):
                    wait_apart(sp, L["proj"], l * UNITS)
                    wait_apart(sp, L["rot0"], l * UNITS)
                    wait_apart(sp, L["tab"], l)
                    wait_apart(sp, L["WO"], l * B)
                lay = bass.ds(l, 1)
                sp.dma_start(wqkv_raw, Wqkv[lay].rearrange("a p n -> p (a n)")).then_inc(L["w_attn"], 16)
                sp.dma_start(wo[:, :, :], Wo[lay].rearrange("a (c p) n -> p (a c) n", p=128)).then_inc(L["w_attn"], 16)
                sp.dma_start(qk_scl[:, 0, :], q_scale[lay].rearrange("a n -> (a n)").partition_broadcast(128)).then_inc(L["w_attn"], 16)
                sp.dma_start(qk_scl[:, 1, :], k_scale[lay].rearrange("a n -> (a n)").partition_broadcast(128)).then_inc(L["w_attn"], 16)

            def load_ffn(l):
                lay = bass.ds(l, 1)
                if not isinstance(l, int):
                    wait_apart(sp, Fm["res"], l * QUADS)
                sp.dma_start(w1_raw[:, :], W1[lay].rearrange("a p n -> p (a n)")).then_inc(L["w_ffn"], 16)
                sp.dma_start(w2[:, 0:2, :], W2[lay, 0:256].rearrange("a (c p) n -> p (a c) n", p=128)).then_inc(L["w_ffn"], 16)
                sp.dma_start(w2[0:FF - 256, 2, :], W2[lay, 256:FF].rearrange("a p n -> p (a n)")).then_inc(L["w_ffn"], 16)
                for j, v in enumerate((ln_g, ln_b, b2)):
                    sp.dma_start(vecs[:, j:j + 1], v[lay].rearrange("a p -> p a")).then_inc(L["w_ffn"], 16)
                for half in range(2):
                    sp.dma_start(b1c[:, half, 0:2], b1[lay, half * FF:half * FF + 256].rearrange("a (c p) -> p (a c)", p=128)).then_inc(L["w_ffn"], 16)
                    sp.dma_start(b1c[0:FF - 256, half, 2:3], b1[lay, half * FF + 256:(half + 1) * FF].rearrange("a p -> p a")).then_inc(L["w_ffn"], 16)

            return load_attention, load_ffn

        def split_product(out_ap, lhsT, rhs):
            nc.tensor.matmul(out_ap, lhsT[1], rhs[0], start=True, stop=False)
            nc.tensor.matmul(out_ap, lhsT[0], rhs[1], start=False, stop=False)
            return nc.tensor.matmul(out_ap, lhsT[0], rhs[0], start=False, stop=True)

        def attention_tensor(pe, l, beside):
            U, NB = l * UNITS, l * B

            def emit(k, i, on):
                first = 8 * i

                def n(d):
                    return U + first + (k - d)
                if on(0):
                    bt = k // UB % 2
                    if k % UB == 0:
                        pe.wait_ge(L["xs"], NB + batch_of(i, k, 0) + 1)
                    if reused(first, k, 0, 2):
                        pe.wait_ge(L["own_crossed"], n(0) - 1)
                    g = k % UB
                    split_product(banks[k % 2][:, :].rearrange("p (a n) -> p a n", a=2), [x[:, bt, :] for x in xs],
                                  [w[:, 0:2, g * G * DL:(g + 1) * G * DL] for w in wqkv]).then_inc(L["proj_qk"], 1)
                if on(3):
                    pe.wait_ge(L["rot"], n(3) + 1)
                    if reused(first, k, 3, 1):
                        pe.wait_ge(L["qkT"], n(3))
                    for c in range(4):
                        last = nc.tensor.transpose(qkT_ps[:, c * T:(c + 1) * T], rot[:, (k - 3) % 4, 2 * c:2 * c + 2, :].rearrange("p h n -> p (h n)"), ident[:, :])
                    last.then_inc(L["T1"], 1)
                if on(7):
                    pe.wait_ge(L["o"], n(7) + 1)
                    if reused(first, k, 7, 1):
                        pe.wait_ge(L["oT"], n(7))
                    if on(9) and (k - 9) % UB == UB - 1:
                        pe.wait_ge(L["res"], NB + batch_of(i, k, 9) + 1)
                    for c in range(2):
                        last = nc.tensor.transpose(oT_ps[:, c * T:(c + 1) * T], o_sb[:, (k - 7) % 2, 2 * c:2 * c + 2, :].rearrange("p h n -> p (h n)"), ident[:, :])
                    last.then_inc(L["OT"], 1)
                if on(0):
                    if on(7):
                        pe.wait_ge(L["o"], n(7) + 1)
                    elif reused(first, k, 0, 1):
                        pe.wait_ge(L["v"], n(0))
                    split_product(v_ps, [x[:, bt, :] for x in xs], [w[:, 2, g * G * DL:(g + 1) * G * DL] for w in wqkv]).then_inc(L["proj"], 1)
                if on(4):
                    j = (k - 4) % 2
                    pe.wait_ge(L["qkT"], n(4) + 1)
                    if reused(first, k, 4, 1):
                        pe.wait_ge(L["exp"], n(4))
                    for odd in range(2):
                        nc.tensor.matmul(s_ps[:, odd, :], ident_bf[:, :], band_bf[:, :, :].rearrange("p h n -> p (h n)"), start=True, stop=False, skip_group_check=True)
                    for h in range(G):
                        r = slice(h % 2 * DL, h % 2 * DL + DL)
                        last = nc.tensor.matmul(s_ps[:, h % 2, h // 2 * T:(h // 2 + 1) * T], qkT[r, j, h // 2, :], qkT[r, j, 2 + h // 2, :], start=False, stop=(h // 2 == 1), skip_group_check=True)
                    last.then_inc(L["S"], 1)
                if on(5):
                    pe.wait_ge(L["exp"], n(5) + 1)
                    if reused(first, k, 5, 1):
                        pe.wait_ge(L["pT"], n(5))
                    for h in range(G):
                        last = nc.tensor.transpose(pT_ps[:, h * T:(h + 1) * T], p[:, (k - 5) % 2, h, :], ident[:, :])
                    last.then_inc(L["T2"], 1)
                if on(6):
                    pe.wait_ge(L["pT"], n(6) + 1)
                    if on(0):
                        pe.wait_ge(L["v"], n(0) + 1)
                    else:
                        pe.wait_ge(L["o"], n(6))
                    for h in range(G):
                        last = nc.tensor.matmul(pv_ps[:, h * (DL + 1):(h + 1) * (DL + 1)], pTl[:, (k - 6) % 2, h, :], v_sb[:, (k - 6) % 8, h, :], start=True, stop=True)
                    last.then_inc(L["PV"], 1)
                if on(8) and (k - 8) % UB == UB - 1:
                    pe.wait_ge(L["oT"], n(8) + 1)
                    if on(7):
                        pe.wait_ge(L["oT"], n(7) + 1)
                    for c in range(OUT_CHUNKS):
                        slot = (k - 8 - (UB - 1) + c // 2) % 8
                        last = nc.tensor.matmul(y_ps, wo[:, c, :], oT[:, slot, c % 2 * T:(c % 2 + 1) * T], start=(c == 0), stop=(c == OUT_CHUNKS - 1))
                    last.then_inc(L["WO"], 1)
            pe.wait_ge(L["w_attn"], 16 * ATTN_LOADS * (l + 1))
            pe.wait_ge(L["wqkv_split"], QUADS * (l + 1))
            pipeline(pe, UNITS, 8, 8, emit, peeled=2, beside=beside)

        def batch_of(i, k, d):
            return 2 * i + (k - d) // UB

        def attention_scalar(act, l, beside):
            U = l * UNITS

            def emit(k, i, on):
                first = 8 * i

                def n(d):
                    return U + first + (k - d)
                if on(3):
                    act.wait_ge(L["T1"], n(3) + 1)
                    if reused(first, k, 3, 2):
                        act.wait_ge(L["S"], n(3) - 1)
                    nc.scalar.activation(qkT[:, (k - 3) % 2, :, :].rearrange("p c n -> p (c n)"), qkT_ps[:, :], ACT.Copy).then_inc(L["qkT"], 1)
                if on(7):
                    act.wait_ge(L["OT"], n(7) + 1)
                    nc.scalar.activation(oT[:, (k - 7) % 8, :], oT_ps, ACT.Copy).then_inc(L["oT"], 1)
                if on(0):
                    act.wait_ge(L["proj_qk"], n(0) + 1)
                    if reused(first, k, 0, 2):
                        act.wait_ge(L["ssum"], n(0) - 1)
                    nc.scalar.activation(sq[:, k % 2, :, :].rearrange("p h n -> p (h n)"), banks[k % 2][:, :], ACT.Square).then_inc(L["square"], 1)
                if on(0):
                    act.wait_ge(L["proj"], n(0) + 1)
                    if reused(first, k, 0, 8):
                        act.wait_ge(L["PV"], n(0) - 7)
                    nc.scalar.activation(v_sb[:, k % 8, :, 0:DL], v_ps.rearrange("p (h n) -> p h n", h=G), ACT.Copy).then_inc(L["v"], 1)
                if on(4):
                    act.wait_ge(L["nm"], n(4) + 1)
                    if reused(first, k, 4, 2):
                        act.wait_ge(L["T2"], n(4) - 1)
                    for h in range(G):
                        last = nc.scalar.activation(p[:, (k - 4) % 2, h, :], s_ps[:, h % 2, h // 2 * T:(h // 2 + 1) * T], ACT.Exp,
                                                    bias=nm[:, (k - 4) % 2, h // 2, h % 2:h % 2 + 1], scale=rn[:, (k - 4) % 8, h:h + 1])
                    last.then_inc(L["exp"], 1)
            pipeline(act, UNITS, 8, 8, emit, beside=beside)

        def shift_copy(dst, src, width):
            nc.vector.tensor_copy(dst[0:64], src[0:64])
            return nc.vector.tensor_copy(dst[64:128, :, 1:T], src[64:128, :, 0:T - 1])

        def attention_vector(dve, l, beside):
            U, NB = l * UNITS, l * B

            def shifted_batch(b, j):
                z = zT[:, bass.ds(b, 1), :].rearrange("p a n -> p (a n)")
                hi, lo = (x[:, j, :] for x in xs)
                nc.vector.tensor_copy(hi[0:64, :], z[0:64, :])
                nc.vector.tensor_copy(hi[64:128, 1:T], z[64:128, 0:T - 1]).then_inc(L["xs_hi"], 1)
                dve.wait_ge(L["xs_hi"], NB + b + 1)
                nc.vector.tensor_tensor(lo[0:64, :], z[0:64, :], hi[0:64, :].bitcast(F32), ALU.subtract)
                nc.vector.tensor_tensor(lo[64:128, 1:T], z[64:128, 0:T - 1], hi[64:128, 1:T].bitcast(F32), ALU.subtract).then_inc(L["xs"], 1)

            def emit(k, i, on):
                first = 8 * i

                def n(d):
                    return U + first + (k - d)
                if on(1):
                    j, j4 = (k - 1) % 2, (k - 1) % 4
                    dve.wait_ge(L["square"], n(1) + 1)
                    if reused(first, k, 1, 4):
                        dve.wait_ge(L["rot"], n(1) - 3)
                    qk = banks[j][:, :].rearrange("p (a h n) -> p a h n", a=2, h=G)
                    nc.vector.tensor_tensor(own[:, j4, :, :].rearrange("p (a h) n -> p a h n", a=2), qk,
                                            rot_tab[:, 0:2, :].unsqueeze(2).to_broadcast([128, 2, G, DL]), ALU.mult)
                    nc.vector.tensor_tensor(crossed[:, j4, :, :].rearrange("p (a h) n -> p a h n", a=2), qk,
                                            rot_tab[:, 2:4, :].unsqueeze(2).to_broadcast([128, 2, G, DL]), ALU.mult).then_inc(L["own_crossed"], 1)
                    if reused(first, k, 1, 2):
                        dve.wait_ge(L["clamp"], n(1) - 1)
                    nc.vector.tensor_reduce(ss[:, j, :], sq[:, j, :, :], X_AXIS, ALU.add).then_inc(L["ssum"], 1)
                if on(4):
                    j = (k - 4) % 2
                    dve.wait_ge(L["S"], n(4) + 1)
                    nc.vector.tensor_reduce(mx[:, j, :, :], s_ps.rearrange("p o (h n) -> p o h n", h=2), X_AXIS, ALU.max, negate=True).then_inc(L["mx"], 1)
                    dve.wait_ge(L["mx"], n(4) + 1)
                    if reused(first, k, 4, 2):
                        dve.wait_ge(L["exp"], n(4) - 1)
                    nc.vector.tensor_tensor(nm[:, j, :, :], mx[:, j, :, :].rearrange("p o h -> p h o"),
                                            rn[:, (k - 4) % 8, 0:G].rearrange("p (h o) -> p h o", o=2), ALU.mult).then_inc(L["nm"], 1)
                if on(5):
                    dve.wait_ge(L["T2"], n(5) + 1)
                    if reused(first, k, 5, 2):
                        dve.wait_ge(L["PV"], n(5) - 1)
                    nc.vector.tensor_copy(pTl[:, (k - 5) % 2, :, :].rearrange("p h n -> p (h n)"), pT_ps[:, :]).then_inc(L["pT"], 1)
                if on(6):
                    j = (k - 6) % 2
                    pv = pv_ps.rearrange("p (h n) -> p h n", h=G)
                    dve.wait_ge(L["PV"], n(6) + 1)
                    nc.vector.reciprocal(ri[:, j, :], pv[:, :, DL]).then_inc(L["ri"], 1)
                    dve.wait_ge(L["ri"], n(6) + 1)
                    if reused(first, k, 6, 2):
                        dve.wait_ge(L["OT"], n(6) - 1)
                    nc.vector.tensor_tensor(o_sb[:, j, :, :], pv[:, :, 0:DL], ri[:, j, :].unsqueeze(2).to_broadcast([128, G, DL]), ALU.mult).then_inc(L["o"], 1)
                if on(8) and (k - 8) % UB == UB - 1:
                    b = batch_of(i, k, 8)
                    dve.wait_ge(L["WO"], NB + b + 1)
                    zb = zT[:, bass.ds(b, 1), :].rearrange("p a n -> p (a n)")
                    nc.vector.tensor_tensor(zb, y_ps, zb, ALU.add).then_inc(L["res"], 1)
                if on(-2) and (k + 2) % UB == 0:
                    if reused(first, k, -2, 2 * UB):
                        dve.wait_ge(L["proj"], n(-2) - UB)
                    shifted_batch(batch_of(i, k, -2), (k + 2) // UB % 2)
            dve.wait_ge(L["w_attn"], 16 * ATTN_LOADS * (l + 1))
            for a in range(2):
                last = nc.vector.tensor_tensor(rot_tab[:, 2 * a:2 * a + 2, :], rot_base[:, 2 * a:2 * a + 2, :], qk_scl[:, :, :], ALU.mult)
            last.then_inc(L["tab"], 1)
            dve.wait_ge(L["tab"], l + 1)
            shifted_batch(0, 0)
            pipeline(dve, UNITS, 8, 8, emit, peeled_last=1, beside=beside)

        def attention_pool(pool, l):
            U = l * UNITS

            def emit(k, i, on):
                first = 8 * i
                def n(d):
                    return U + first + (k - d)
                j, j4 = k % 2, k % 4
                wait_apart(pool, L["ssum"], n(0) + 1)
                nc.gpsimd.tensor_scalar(ssc[:, j, :], ss[:, j, :], 1e-24, 0.0, ALU.max, ALU.add).then_inc(L["clamp"], 1)
                pool.wait_ge(L["clamp"], n(0) + 1)
                if reused(first, k, 0, 8):
                    pool.wait_ge(L["exp"], n(0) - 7)
                nc.gpsimd.tensor_tensor(rn[:, k % 8, :], ssc[:, j, :], neg_half[:, 0:2 * G], ALU.pow).then_inc(L["rn"], 1)
                pool.wait_ge(L["own_crossed"], n(0) + 1)
                if reused(first, k, 0, 4):
                    pool.wait_ge(L["T1"], n(0) - 3)
                hl = DL // 2
                nc.gpsimd.tensor_tensor(rot[:, j4, :, 0:hl], own[:, j4, :, 0:hl], crossed[:, j4, :, hl:DL], ALU.add)
                nc.gpsimd.tensor_tensor(rot[:, j4, :, hl:DL], own[:, j4, :, hl:DL], crossed[:, j4, :, 0:hl], ALU.add).then_inc(L["rot0"], 1)
                pool.wait_ge(L["rn"], n(0) + 1)
                pool.wait_ge(L["rot0"], n(0) + 1)
                nc.gpsimd.tensor_tensor(rot[:, j4, G:2 * G, :], rot[:, j4, G:2 * G, :],
                                        rn[:, k % 8, G:2 * G].unsqueeze(2).to_broadcast([128, G, DL]), ALU.mult).then_inc(L["rot"], 1)
            pipeline(pool, UNITS, 8, 0, emit)

        mean_ps, var_ps, yf_ps = banks[0], banks[1], banks[7]

        def ffn_tensor(pe, l):
            Q = l * QUADS

            def emit(k, i, on):
                first = 2 * i
                def n(d):
                    return Q + first + (k - d)

                def gate_value(c):
                    turn = 3 * n(3) + c
                    g_ps, a_ps = gate_banks(c, k - 3)
                    c0, m = FF_CHUNKS[c]
                    if not (isinstance(first, int) and 3 * (first + k - 3) + c < 2):
                        pe.wait_ge(Fm["u"], turn - 1)
                    xq = [x[:, (k - 3) % 2, :] for x in xn]
                    split_product(g_ps[0:m, :], [w[:, FF + c0:FF + c0 + m] for w in w1], xq)
                    split_product(a_ps[0:m, :], [w[:, c0:c0 + m] for w in w1], xq).then_inc(Fm["ga"], 1)

                if on(2):
                    spread_roots(first, k - 2)
                if on(0):
                    mean(first, k)
                if on(3):
                    pe.wait_ge(Fm["xn"], n(3) + 1)
                    gate_value(0)
                if on(1):
                    variance(first, k - 1)
                if on(4):
                    if reused(first, k, 4, 1):
                        pe.wait_ge(Fm["res"], n(4))
                    pe.wait_ge(Fm["u"], 3 * n(4) + 3)
                    for c, (c0, m) in enumerate(FF_CHUNKS):
                        last = nc.tensor.matmul(yf_ps[:, :], w2[0:m, c, :], uf[0:m, k % 2, c, :], start=(c == 0), stop=(c == 2))
                    last.then_inc(Fm["y_mm"], 1)
                if on(3):
                    gate_value(1)
                    gate_value(2)

            def mean(first, k):
                pe.wait_ge(Fm["xs4"], Q + first + k + 1)
                if reused(first, k, 0, 1):
                    pe.wait_ge(Fm["xc"], Q + first + k)
                nc.tensor.matmul(mean_ps[:, :], mean_w[:, :], xs4[:, k % 2, :, :].rearrange("p a n -> p (a n)"), start=True, stop=True).then_inc(Fm["mean_mm"], 1)

            def variance(first, k):
                pe.wait_ge(Fm["sq"], Q + first + k + 1)
                if reused(first, k, 0, 1):
                    pe.wait_ge(Fm["xn0"], Q + first + k)
                for a in range(QUAD):
                    last = nc.tensor.matmul(var_ps[:, a:a + 1], xsq[:, k % 2, a * T:(a + 1) * T], mean_w[:, 0:1], start=True, stop=True)
                last.then_inc(Fm["var_mm"], 1)

            def spread_roots(first, k):
                pe.wait_ge(Fm["rstd_rep"], Q + first + k + 1)
                for a in range(QUAD):
                    last = nc.tensor.transpose(var_ps[:, a * T:(a + 1) * T], rstd_rep[:, a, :], ident[:, :])
                last.then_inc(Fm["rstd_mm"], 1)

            def beside(k):
                if k == 1:
                    pe.wait_ge(L["own_crossed"], (l + 1) * UNITS)
                    mean(0, 0)
                if k == 2:
                    mean(0, 1)
                if k == 3:
                    variance(0, 0)
                if k == 4:
                    mean(2, 0)
                if k == 5:
                    spread_roots(0, 0)
                if k == 6:
                    variance(0, 1)

            def rest():
                pe.wait_ge(L["w_ffn"], 16 * FFN_LOADS * (l + 1))
                pe.wait_ge(L["w1_split"], l + 1)
                pipeline(pe, QUADS, 2, 4, emit, peeled=2, done=3)
            return beside, rest

        def gate_banks(c, k):
            t = (3 * (k % 2) + c) % 2
            return banks[2 + 2 * t], banks[3 + 2 * t]

        def ffn_scalar(act, l):
            Q = l * QUADS

            def emit(k, i, on):
                first = 2 * i
                def n(d):
                    return Q + first + (k - d)
                if on(0):
                    squares(first, k)
                if on(3):
                    for c, (c0, m) in enumerate(FF_CHUNKS):
                        turn = 3 * n(3) + c
                        act.wait_ge(Fm["ga"], turn + 1)
                        g_ps, _ = gate_banks(c, k - 3)
                        t = (3 * ((k - 3) % 2) + c) % 2
                        if not (isinstance(first, int) and 3 * (first + k - 3) + c < 2):
                            act.wait_ge(Fm["u"], turn - 1)
                        nc.scalar.activation(gel[0:m, t, :], g_ps[0:m, :], ACT.Gelu, bias=b1c[0:m, 1, c:c + 1], scale=1.0).then_inc(Fm["gelu"], 1)

            def squares(first, k):
                act.wait_ge(Fm["xc"], Q + first + k + 1)
                if reused(first, k, 0, 2):
                    act.wait_ge(Fm["var_mm"], Q + first + k - 1)
                nc.scalar.activation(xsq[:, k % 2, :], xc[:, k % 2, :], ACT.Square).then_inc(Fm["sq"], 1)

            def beside(k):
                if k in (2, 3):
                    squares(0, k - 2)
                if k == 7:
                    squares(2, 0)

            def rest():
                act.wait_ge(L["w_ffn"], 16 * FFN_LOADS * (l + 1))
                pipeline(act, QUADS, 2, 4, emit, peeled=2, done=3)
            return beside, rest

        def ffn_vector(dve, l):
            Q = l * QUADS

            def emit(k, i, on):
                first = 2 * i
                def n(d):
                    return Q + first + (k - d)
                if on(2):
                    norm(first, k - 2)
                if on(0):
                    centre(first, k)
                if on(1):
                    shift_variance(first, k - 1)
                if on(-1):
                    shifted_quad(first + k + 1, (k + 1) % 2)
                if on(3):
                    value_chunk(k - 3, n, 0)
                if on(1):
                    repeat_roots(first, k - 1)
                if on(4):
                    dve.wait_ge(Fm["y_mm"], n(4) + 1)
                    zb = zT[:, bass.ds((first + (k - 4)) * QUAD, QUAD), :].rearrange("p a n -> p (a n)")
                    nc.vector.scalar_tensor_tensor(zb, yf_ps[:, :], vecs[:, 2:3], zb, ALU.add, ALU.add).then_inc(Fm["res"], 1)
                if on(3):
                    value_chunk(k - 3, n, 1)
                    value_chunk(k - 3, n, 2)

            def centre(first, k):
                dve.wait_ge(Fm["mean_mm"], Q + first + k + 1)
                dve.wait_ge(Fm["xs4"], Q + first + k + 1)
                nc.vector.tensor_tensor(xc[:, k % 2, :], xs4[:, k % 2, :, :].rearrange("p a n -> p (a n)"), mean_ps[:, :], ALU.subtract).then_inc(Fm["xc"], 1)

            def shift_variance(first, k):
                dve.wait_ge(Fm["var_mm"], Q + first + k + 1)
                nc.vector.tensor_scalar(var_sb[:, :], var_ps[:, 0:QUAD], EPS, None, ALU.add).then_inc(Fm["var"], 1)

            def repeat_roots(first, k):
                dve.wait_ge(Fm["rstd"], Q + first + k + 1)
                nc.vector.tensor_copy(rstd_rep[:, :, :], var_sb[:, :].unsqueeze(2).to_broadcast([128, QUAD, T])).then_inc(Fm["rstd_rep"], 1)

            def norm(first, k):
                done = Q + first + k + 1
                dve.wait_ge(Fm["rstd_mm"], done)
                nc.vector.tensor_tensor(xn0[:, :], xc[:, k % 2, :], var_ps[:, :], ALU.mult).then_inc(Fm["xn0"], 1)
                dve.wait_ge(Fm["xn0"], done)
                nc.vector.tensor_scalar(xn_f[:, :], xn0[:, :], vecs[:, 0:1], vecs[:, 1:2], ALU.mult, ALU.add).then_inc(Fm["xn_f"], 1)
                dve.wait_ge(Fm["xn_f"], done)
                nc.vector.tensor_copy(xn_hi[:, k % 2, :], xn_f[:, :]).then_inc(Fm["xn_hi"], 1)
                dve.wait_ge(Fm["xn_hi"], done)
                nc.vector.tensor_tensor(xn_lo[:, k % 2, :], xn_f[:, :], xn_hi[:, k % 2, :].bitcast(F32), ALU.subtract).then_inc(Fm["xn"], 1)

            def shifted_quad(q, j):
                shift_copy(xs4[:, j, :, :], zT[:, bass.ds(q * QUAD, QUAD), :], NQ).then_inc(Fm["xs4"], 1)

            def value_chunk(k, n, c):
                c0, m = FF_CHUNKS[c]
                t = (3 * (k % 2) + c) % 2
                _, a_ps = gate_banks(c, k)
                dve.wait_ge(Fm["gelu"], 3 * n(3) + c + 1)
                nc.vector.scalar_tensor_tensor(uf[0:m, k % 2, c, :], a_ps[0:m, :], b1c[0:m, 0, c:c + 1], gel[0:m, t, :],
                                               ALU.add, ALU.mult).then_inc(Fm["u"], 1)

            def beside(k):
                if k == 0:
                    dve.wait_ge(L["res"], l * B + 4 * QUAD)
                    shifted_quad(0, 0)
                    shifted_quad(1, 1)
                if k == 1:
                    centre(0, 0)
                if k == 2:
                    centre(0, 1)
                    shifted_quad(2, 0)
                if k == 3:
                    shift_variance(0, 0)
                if k == 4:
                    repeat_roots(0, 0)
                if k == 5:
                    dve.wait_ge(L["w_ffn"], 16 * FFN_LOADS * (l + 1))
                    norm(0, 0)
                if k == 6:
                    centre(2, 0)
                    shift_variance(0, 1)
                if k == 7:
                    repeat_roots(0, 1)
                    shifted_quad(3, 1)

            def rest():
                dve.wait_ge(L["res"], (l + 1) * B)
                pipeline(dve, QUADS, 2, 4, emit, peeled=2, peeled_last=1, done=3)
                dve.wait_ge(Fm["res"], (l + 1) * QUADS)
            return beside, rest

        WQ = 3 * INNER // QUADS

        def split_wqkv(pool, l, e):
            cols = bass.ds(e * WQ, WQ)
            raw = wqkv_raw[:, cols]
            hi, lo = (w[:, :, :].rearrange("p a n -> p (a n)")[:, cols] for w in wqkv)
            nc.gpsimd.tensor_copy(hi, raw).then_inc(L["wqkv_hi"], 1)
            pool.wait_ge(L["wqkv_hi"], l * QUADS + e + 1)
            nc.gpsimd.tensor_tensor(lo, raw, hi.bitcast(F32), ALU.subtract).then_inc(L["wqkv_split"], 1)

        def ffn_pool(pool, l, has_next):
            Q = l * QUADS
            wait_apart(pool, L["w_ffn"], 16 * FFN_LOADS * (l + 1))
            nc.gpsimd.tensor_copy(w1_hi[:, :], w1_raw[:, :]).then_inc(L["w1_hi"], 1)
            pool.wait_ge(L["w1_hi"], l + 1)
            nc.gpsimd.tensor_tensor(w1_lo[:, :], w1_raw[:, :], w1_hi[:, :].bitcast(F32), ALU.subtract).then_inc(L["w1_split"], 1)

            def emit(k, i, on):
                first = 2 * i
                if on(0):
                    pool.wait_ge(Fm["var"], Q + first + k + 1)
                    nc.gpsimd.tensor_tensor(var_sb[:, :], var_sb[:, :], neg_half[:, 0:QUAD], ALU.pow).then_inc(Fm["rstd"], 1)
                if has_next and on(3):
                    if not reused(first, k, 3, 1):
                        wait_apart(pool, L["w_attn"], 16 * ATTN_LOADS * (l + 2))
                    split_wqkv(pool, l + 1, first + k - 3)
            pipeline(pool, QUADS, 2, 3, emit, peeled=2)

        def final_scalar(act):
            def emit(k, i, on):
                first = 2 * i
                if reused(first, k, 0, 2):
                    act.wait_ge(O["T_mm"], first + k - 1)
                nc.scalar.activation(zq[:, k % 2, :], zT[:, bass.ds((first + k) * QUAD, QUAD), :].rearrange("p a n -> p (a n)"), ACT.Copy).then_inc(O["copied"], 1)
            act.wait_ge(Fm["res"], LAYERS * QUADS)
            pipeline(act, QUADS, 2, 0, emit, peeled=2)

        def final_tensor(pe):
            def emit(k, i, on):
                first = 2 * i
                pe.wait_ge(O["copied"], first + k + 1)
                if reused(first, k, 0, 2):
                    pe.wait_ge(O["added"], first + k - 1)
                for a in range(QUAD):
                    last = nc.tensor.transpose(banks[k % 2][:, a * 128:(a + 1) * 128], zq[:, k % 2, a * 128:(a + 1) * 128], ident[:, :])
                last.then_inc(O["T_mm"], 1)
            pipeline(pe, QUADS, 2, 0, emit, peeled=2)

        def final_vector(dve):
            def emit(k, i, on):
                first = 2 * i
                dve.wait_ge(O["T_mm"], first + k + 1)
                if reused(first, k, 0, 2):
                    dve.wait_ge(O_stored[k % 2], 16 * i)
                nc.vector.tensor_tensor(res[:, k % 2, :, :].rearrange("p a n -> p (a n)"), banks[k % 2][:, :],
                                        x_all[:, bass.ds((first + k) * QUAD, QUAD), :].rearrange("p a n -> p (a n)"), ALU.add).then_inc(O["added"], 1)
            pipeline(dve, QUADS, 2, 0, emit, peeled=2)

        def final_sync(sp):
            def emit(k, i, on):
                first = 2 * i
                wait_apart(sp, O["added"], first + k + 1)
                sp.dma_start(out[bass.ds((first + k) * QUAD, QUAD)].rearrange("b t d -> t b d"), res[:, k % 2, :, :]).then_inc(O_stored[k % 2], 16)
            pipeline(sp, QUADS, 2, 0, emit, peeled=2)
            for stored in O_stored:
                sp.wait_ge(stored, 16 * QUADS // 2)

        part1_done = sem("part1_done")
        ones_set = sem("ones_set")
        rot_in = sem("rot_in")

        ctx.enter_context(nc.allow_non_contiguous_dma(reason="small vectors laid out over partitions"))
        block = ctx.enter_context(nc.Block())

        @block.sync
        def _(sp):
            for dst, src in W0_LOADS:
                sp.dma_start(dst, src).then_inc(loaded_w0, 16)
            for c in range(4):
                sp.dma_start(x_all[:, c * 8:(c + 1) * 8, :], x[c * 8:(c + 1) * 8].rearrange("b t d -> t b d")).then_inc(loaded_x, 16)
            load_attention, load_ffn = layer_loads(sp)
            sp.dma_start(rot_base[:, :, :], rotary).then_inc(rot_in, 16)
            load_attention(0)
            part1_sync(sp)
            sp.wait_ge(part1_done, 4)
            load_ffn(0)
            with sp.Fori(1, LAYERS) as l:
                load_attention(l)
                load_ffn(l)
            final_sync(sp)

        @block.tensor
        def _(pe):
            setup_tensor(pe)
            pe.wait_ge(setup_ev, SETUP_RESULTS)
            part1_tensor(pe)
            pe.wait_ge(S1["zT"], B)
            nc.tensor.nop().then_inc(part1_done, 1)
            pe.wait_ge(const_cast, 2)
            with pe.Fori(0, LAYERS) as l:
                ffn_start, ffn_rest = ffn_tensor(pe, l)
                attention_tensor(pe, l, ffn_start)
                ffn_rest()
            final_tensor(pe)

        @block.vector
        def _(dve):
            nc.vector.memset(mean_w[:, :], 1.0 / D).then_inc(const_set, 1)
            setup_vector(dve)
            dve.wait_ge(setup_ev, SETUP_RESULTS)
            nc.vector.memset(v2[:, :, :, DX:DX + 1], 1.0).then_inc(ones_set, 1)
            dve.wait_ge(ones_set, 1)
            dve.wait_ge(loaded_x, 64)
            part1_vector(dve)
            dve.wait_ge(S1["zT"], B)
            nc.vector.nop().then_inc(part1_done, 1)
            dve.wait_ge(part1_done, 4)
            nc.vector.memset(v_sb[:, :, :, DL:DL + 1], 1.0).then_inc(ones_set, 1)
            nc.vector.memset(xs4[64:128, :, :, 0:1], 0.0).then_inc(zeroed, 1)
            dve.wait_ge(ones_set, 2)
            dve.wait_ge(zeroed, 1)
            for x in xs:
                nc.vector.tensor_copy(x[64:128, :, 0:1], xs4[64:128, :, 0, 0:1]).then_inc(zeroed, 1)
            dve.wait_ge(zeroed, 3)
            dve.wait_ge(rot_in, 16)
            with dve.Fori(0, LAYERS) as l:
                ffn_start, ffn_rest = ffn_vector(dve, l)
                attention_vector(dve, l, ffn_start)
                ffn_rest()
            final_vector(dve)

        @block.scalar
        def _(act):
            act.wait_ge(setup_ev, SETUP_RESULTS)
            part1_scalar(act)
            act.wait_ge(S1["zT"], B)
            nc.scalar.nop().then_inc(part1_done, 1)
            act.wait_ge(part1_done, 4)
            with act.Fori(0, LAYERS) as l:
                ffn_start, ffn_rest = ffn_scalar(act, l)
                attention_scalar(act, l, ffn_start)
                ffn_rest()
            final_scalar(act)

        @block.gpsimd
        def _(pool):
            nc.gpsimd.memset(neg_half[:, :], -0.5).then_inc(half_set, 1)
            pool.wait_ge(half_set, 1)
            wait_apart(pool, L["w_attn"], 16 * ATTN_LOADS)
            for e in range(QUADS):
                split_wqkv(pool, 0, e)
            pool.wait_ge(setup_ev, SETUP_RESULTS)
            pool.wait_ge(loaded_x, 64)
            part1_pool(pool)
            pool.wait_ge(S1["zT"], B)
            nc.gpsimd.nop().then_inc(part1_done, 1)
            pool.wait_ge(part1_done, 4)
            with pool.Fori(0, LAYERS - 1) as l:
                attention_pool(pool, l)
                ffn_pool(pool, l, True)
            attention_pool(pool, LAYERS - 1)
            ffn_pool(pool, LAYERS - 1, False)


_INS = ["x", "ctx_2048", "mask_BxS2_fk1", "L0_attn_w_qs", "L0_attn_w_ks", "L0_attn_w_vs", "L0_attn_w_rel_pos_k",
        "L0_attn_rel_embed_bias", "L0_attn_rel_pos_bias", "L0_attn_w_out", "L0_attn_b_out",
        "L0_xattn_W_src", "L0_xattn_b_src", "L0_xattn_W_tgt", "L0_xattn_b_tgt", "L0_xattn_W_out", "L0_xattn_b_out",
        "L0_ffn_Wqkv", "L0_ffn_q_scale", "L0_ffn_k_scale", "L0_ffn_Wo", "L0_ffn_ln_g", "L0_ffn_ln_b",
        "L0_ffn_W1", "L0_ffn_b1", "L0_ffn_W2", "L0_ffn_b2"]


def kernel(**inputs):
    import concourse.bacc as bacc
    from concourse.bass_utils import run_bass_kernel_spmd

    nc = bacc.Bacc("TRN2", target_bir_lowering=False, num_devices=1)
    arrays, args = {}, []
    given = [(n, np.ascontiguousarray(inputs[n])) for n in _INS] + [(n, make()) for n, make in CONSTANTS.items()]
    for name, a in given:
        arrays[f"in_{name}"] = a
        args.append(nc.dram_tensor(f"in_{name}", a.shape, mybir.dt.from_np(a.dtype), kind="ExternalInput").ap())
    args.append(nc.dram_tensor("out_0", (B, T, D), F32, kind="ExternalOutput").ap())
    build(nc, *args)
    r = run_bass_kernel_spmd(nc, [arrays], core_ids=[0])
    return r.results[0]["out_0"]
```
